# Optimizing a Trainium2 kernel written in Bass

```python
import numpy as np
import jax
import jax.numpy as jnp

def _softmax(x, axis=-1):
    return jax.nn.softmax(x, axis=axis)

def _gelu(x):
    return jax.nn.gelu(x, approximate=True)

def _silu(x):
    return jax.nn.silu(x)

def _sigmoid(x):
    return jax.nn.sigmoid(x)

def _layernorm(x, axis=-1, eps=1e-05):
    m = jnp.mean(x, axis=axis, keepdims=True)
    v = jnp.var(x, axis=axis, keepdims=True)
    return (x - m) / jnp.sqrt(v + eps)

def _scatter_add(tgt, idx, src, axis=0):
    return tgt.at[idx].add(src)

def _segment_sum(src, seg, n):
    return jax.ops.segment_sum(src, seg, n)
kernel_name = 'mk_gnn_resnorm_d4_gnn_r8_d44ad0'

def setup_inputs(seed: int=0):
    np.random.seed(seed)
    _w = jnp.asarray

    def _rec_inputs():
        import jax
        import jax.numpy as jnp
        _gk = jax.random.key(seed)
        x = -0.0009044 + 1 * jax.random.normal(jax.random.fold_in(_gk, 1), (12500, 16), jnp.float32)
        src = jax.random.randint(jax.random.fold_in(_gk, 2), (400000,), 0, 12500, jnp.int32)
        dst = jax.random.randint(jax.random.fold_in(_gk, 3), (400000,), 0, 12500, jnp.int32)
        _o = jnp.argsort(dst, stable=True)
        src = src[_o]
        dst = dst[_o]
        edge_attr_16 = -0.00010739 + 0.99994 * jax.random.normal(jax.random.fold_in(_gk, 11), (400000, 16), jnp.float32)
        edge_attr_8 = -5.3897e-05 + 0.999841 * jax.random.normal(jax.random.fold_in(_gk, 12), (400000, 8), jnp.float32)
        node_vec1 = -0.00472126 + 0.997171 * jax.random.normal(jax.random.fold_in(_gk, 15), (12500, 1), jnp.float32)
        return (x, src, dst, edge_attr_16, edge_attr_8, node_vec1)
    x, src, dst, edge_attr_16, edge_attr_8, node_vec1 = _rec_inputs()

    def _L0_gnn_setup():
        import jax, jax.numpy as jnp
        import numpy as np
        N = 12500
        E = 100000
        F_IN = 16
        H1, C1 = (3, 32)
        H2, C2 = (1, 32)
        NC = 16
        SLOPE = 0.2

        def _gat_layer(x, src, dst, W, a_s, a_d, b, heads, outc):
            h = (x @ W).reshape(N, heads, outc)
            alpha_s = (h * a_s).sum(-1)
            alpha_d = (h * a_d).sum(-1)
            e = jax.nn.leaky_relu(alpha_s[src] + alpha_d[dst], SLOPE)
            m = jax.ops.segment_max(e, dst, num_segments=N)
            p = jnp.exp(e - m[dst])
            z = jax.ops.segment_sum(p, dst, num_segments=N)
            alpha = p / (z[dst] + 1e-16)
            out = jax.ops.segment_sum(h[src] * alpha[:, :, None], dst, num_segments=N)
            return out.reshape(N, heads * outc) + b
        key = jax.random.key(seed)
        ks = jax.random.split(key, 12)
        s = 0.1
        return {'x': jax.random.normal(ks[0], (N, F_IN), jnp.float32), 'edge_index': jax.random.randint(ks[1], (2, E), 0, N, dtype=jnp.int32), 'W1': jax.random.normal(ks[2], (F_IN, H1 * C1), jnp.float32) * s, 'a_src1': jax.random.normal(ks[3], (H1, C1), jnp.float32) * s, 'a_dst1': jax.random.normal(ks[4], (H1, C1), jnp.float32) * s, 'b1': jnp.zeros((H1 * C1,), jnp.float32), 'W2': jax.random.normal(ks[5], (H1 * C1, H2 * C2), jnp.float32) * s, 'a_src2': jax.random.normal(ks[6], (H2, C2), jnp.float32) * s, 'a_dst2': jax.random.normal(ks[7], (H2, C2), jnp.float32) * s, 'b2': jnp.zeros((H2 * C2,), jnp.float32), 'Wf': jax.random.normal(ks[8], (C2, NC), jnp.float32) * s, 'bf': jnp.zeros((NC,), jnp.float32)}
    _L0_gnn_all = _L0_gnn_setup()
    _L0_gnn_in = {k: v for k, v in _L0_gnn_all.items() if k in ('W1', 'a_src1', 'a_dst1', 'b1', 'W2', 'a_src2', 'a_dst2', 'b2', 'Wf', 'bf')}
    del _L0_gnn_all

    def _L1_gnn_setup():
        import jax, jax.numpy as jnp
        import numpy as np
        N_NODES = 12500
        N_EDGES = 400000
        D_NODE = 16
        D_EDGE = 8
        D_HIDDEN = 16
        key = jax.random.key(seed)
        ks = jax.random.split(key, 8)
        node_features = jax.random.normal(ks[0], (N_NODES, D_NODE), dtype=jnp.float32)
        edge_attr_e3nn = jax.random.normal(ks[1], (N_EDGES, D_EDGE), dtype=jnp.float32)
        node_attr_scalar_raw = jax.random.normal(ks[2], (N_NODES, 1), dtype=jnp.float32)
        W_msg_tp = jax.random.normal(ks[3], (D_NODE, D_EDGE, D_HIDDEN), dtype=jnp.float32)
        W_msg_lin = jax.random.normal(ks[4], (D_HIDDEN, D_HIDDEN), dtype=jnp.float32)
        W_upd_tp = jax.random.normal(ks[5], (D_NODE, D_HIDDEN, D_HIDDEN), dtype=jnp.float32)
        W_upd_lin = jax.random.normal(ks[6], (D_HIDDEN, D_NODE), dtype=jnp.float32)
        edge_index = jax.random.randint(ks[7], (2, N_EDGES), 0, N_NODES, dtype=jnp.int64)
        return {'node_features': node_features, 'edge_attr_e3nn': edge_attr_e3nn, 'node_attr_scalar_raw': node_attr_scalar_raw, 'W_msg_tp': W_msg_tp, 'W_msg_lin': W_msg_lin, 'W_upd_tp': W_upd_tp, 'W_upd_lin': W_upd_lin, 'edge_index': edge_index}
    _L1_gnn_all = _L1_gnn_setup()
    _L1_gnn_in = {k: v for k, v in _L1_gnn_all.items() if k in ('W_msg_tp', 'W_msg_lin', 'W_upd_tp', 'W_upd_lin')}
    del _L1_gnn_all

    def _L2_gnn_setup():
        import jax, jax.numpy as jnp
        import numpy as np
        STALK_DIM = 16
        N_NODES = 6250
        N_EDGES = 50000
        HIDDEN = 64
        key = jax.random.key(seed)
        k1, k2, k3, k4 = jax.random.split(key, 4)
        d = STALK_DIM
        x = jax.random.normal(k1, (N_NODES, d), dtype=jnp.float32)
        edge_index = jax.random.randint(k2, (2, N_EDGES), 0, N_NODES, dtype=jnp.int64)
        W1 = jax.random.normal(k3, (HIDDEN, 2 * d), dtype=jnp.float32) * (1.0 / np.sqrt(2 * d))
        b1 = jnp.zeros((HIDDEN,), dtype=jnp.float32)
        W2 = jax.random.normal(k4, (d, HIDDEN), dtype=jnp.float32) * (1.0 / np.sqrt(HIDDEN))
        b2 = jnp.zeros((d,), dtype=jnp.float32)
        return {'x': x, 'edge_index': edge_index, 'W1': W1, 'b1': b1, 'W2': W2, 'b2': b2}
    _L2_gnn_all = _L2_gnn_setup()
    _L2_gnn_in = {k: v for k, v in _L2_gnn_all.items() if k in ('W1', 'b1', 'W2', 'b2')}
    del _L2_gnn_all

    def _L3_gnn_setup():
        import jax, jax.numpy as jnp
        import numpy as np
        N_NODES = 6250
        N_EDGES = 100000
        NODE_DIM = 16
        EDGE_DIM = 16
        key = jax.random.key(seed)
        k1, k2, k3, k4 = jax.random.split(key, 4)
        node_features = jax.random.normal(k1, (N_NODES, NODE_DIM), dtype=jnp.float32)
        edge_features = jax.random.normal(k2, (N_EDGES, EDGE_DIM), dtype=jnp.float32)
        pair_indices = jax.random.randint(k3, (N_EDGES, 2), 0, N_NODES, dtype=jnp.int64)
        limit = float(np.sqrt(6.0 / (EDGE_DIM + NODE_DIM * NODE_DIM)))
        kernel = jax.random.uniform(k4, (EDGE_DIM, NODE_DIM * NODE_DIM), minval=-limit, maxval=limit, dtype=jnp.float32)
        bias = jnp.zeros((NODE_DIM * NODE_DIM,), dtype=jnp.float32)
        return {'node_features': node_features, 'edge_features': edge_features, 'pair_indices': pair_indices, 'kernel': kernel, 'bias': bias}
    _L3_gnn_all = _L3_gnn_setup()
    _L3_gnn_in = {k: v for k, v in _L3_gnn_all.items() if k in ('kernel', 'bias')}
    del _L3_gnn_all
    return {'x': x, 'src': src, 'dst': dst, 'edge_attr_16': edge_attr_16, 'edge_attr_8': edge_attr_8, 'node_vec1': node_vec1, 'L0_gnn_W1': _L0_gnn_in['W1'], 'L0_gnn_a_src1': _L0_gnn_in['a_src1'], 'L0_gnn_a_dst1': _L0_gnn_in['a_dst1'], 'L0_gnn_b1': _L0_gnn_in['b1'], 'L0_gnn_W2': _L0_gnn_in['W2'], 'L0_gnn_a_src2': _L0_gnn_in['a_src2'], 'L0_gnn_a_dst2': _L0_gnn_in['a_dst2'], 'L0_gnn_b2': _L0_gnn_in['b2'], 'L0_gnn_Wf': _L0_gnn_in['Wf'], 'L0_gnn_bf': _L0_gnn_in['bf'], 'L1_gnn_W_msg_tp': _L1_gnn_in['W_msg_tp'], 'L1_gnn_W_msg_lin': _L1_gnn_in['W_msg_lin'], 'L1_gnn_W_upd_tp': _L1_gnn_in['W_upd_tp'], 'L1_gnn_W_upd_lin': _L1_gnn_in['W_upd_lin'], 'L2_gnn_W1': _L2_gnn_in['W1'], 'L2_gnn_b1': _L2_gnn_in['b1'], 'L2_gnn_W2': _L2_gnn_in['W2'], 'L2_gnn_b2': _L2_gnn_in['b2'], 'L3_gnn_kernel': _L3_gnn_in['kernel'], 'L3_gnn_bias': _L3_gnn_in['bias']}

def reference(x, src, dst, edge_attr_16, edge_attr_8, node_vec1, L0_gnn_W1, L0_gnn_a_src1, L0_gnn_a_dst1, L0_gnn_b1, L0_gnn_W2, L0_gnn_a_src2, L0_gnn_a_dst2, L0_gnn_b2, L0_gnn_Wf, L0_gnn_bf, L1_gnn_W_msg_tp, L1_gnn_W_msg_lin, L1_gnn_W_upd_tp, L1_gnn_W_upd_lin, L2_gnn_W1, L2_gnn_b1, L2_gnn_W2, L2_gnn_b2, L3_gnn_kernel, L3_gnn_bias):
    import jax
    import jax.numpy as jnp

    def _L0_gnn_ref(x, edge_index, W1, a_src1, a_dst1, b1, W2, a_src2, a_dst2, b2, Wf, bf):
        import jax, jax.numpy as jnp
        import numpy as np
        N = 12500
        E = 100000
        F_IN = 16
        H1, C1 = (3, 32)
        H2, C2 = (1, 32)
        NC = 16
        SLOPE = 0.2

        def _gat_layer(x, src, dst, W, a_s, a_d, b, heads, outc):
            h = (x @ W).reshape(N, heads, outc)
            alpha_s = (h * a_s).sum(-1)
            alpha_d = (h * a_d).sum(-1)
            e = jax.nn.leaky_relu(alpha_s[src] + alpha_d[dst], SLOPE)
            m = jax.ops.segment_max(e, dst, num_segments=N)
            p = jnp.exp(e - m[dst])
            z = jax.ops.segment_sum(p, dst, num_segments=N)
            alpha = p / (z[dst] + 1e-16)
            out = jax.ops.segment_sum(h[src] * alpha[:, :, None], dst, num_segments=N)
            return out.reshape(N, heads * outc) + b
        loops = jnp.arange(N, dtype=edge_index.dtype)
        src = jnp.concatenate([edge_index[0], loops])
        dst = jnp.concatenate([edge_index[1], loops])
        h = jax.nn.selu(_gat_layer(x, src, dst, W1, a_src1, a_dst1, b1, H1, C1))
        h = jax.nn.selu(_gat_layer(h, src, dst, W2, a_src2, a_dst2, b2, H2, C2))
        return h @ Wf + bf

    def _L1_gnn_ref(node_features, edge_attr_e3nn, node_attr_scalar_raw, W_msg_tp, W_msg_lin, W_upd_tp, W_upd_lin, edge_index):
        import jax, jax.numpy as jnp
        import numpy as np
        N_NODES = 12500
        N_EDGES = 400000
        D_NODE = 16
        D_EDGE = 8
        D_HIDDEN = 16
        n_nodes = node_features.shape[0]
        row = edge_index[0]
        col = edge_index[1]
        norm_msg_tp = 1.0 / np.float32(np.sqrt(D_NODE * D_EDGE))
        norm_upd_tp = 1.0 / np.float32(np.sqrt(D_NODE * D_HIDDEN))
        norm_lin = 1.0 / np.float32(np.sqrt(D_HIDDEN))
        x_j = node_features[col]
        m = jnp.einsum('ei,ej,ijh->eh', x_j, edge_attr_e3nn, W_msg_tp) * norm_msg_tp
        m = jax.nn.silu(m)
        m = m @ W_msg_lin * norm_lin
        agg = jax.ops.segment_sum(m, row, num_segments=n_nodes)
        u = jnp.einsum('ni,nh,ihk->nk', node_features, agg, W_upd_tp) * norm_upd_tp
        u = jax.nn.silu(u)
        u = u @ W_upd_lin * norm_lin
        return node_features + u

    def _L2_gnn_ref(x, edge_index, W1, b1, W2, b2):
        import jax, jax.numpy as jnp
        import numpy as np
        STALK_DIM = 16
        N_NODES = 6250
        N_EDGES = 50000
        HIDDEN = 64
        d = x.shape[1]
        n = x.shape[0]
        src, dst = (edge_index[0], edge_index[1])
        xs, xd = (x[src], x[dst])

        def reflection(a, b):
            h = jax.nn.relu(jnp.concatenate([a, b], axis=1) @ W1.T + b1)
            return h @ W2.T + b2

        def householder(v):
            vn = v / jnp.maximum(jnp.linalg.norm(v, axis=1, keepdims=True), 1e-12)
            return jnp.eye(d, dtype=v.dtype)[None] - 2.0 * vn[:, :, None] * vn[:, None, :]
        F_s = householder(reflection(xs, xd))
        F_d = householder(reflection(xd, xs))
        L_sd = -jnp.einsum('eki,ekj->eij', F_s, F_d)
        ones_e = jnp.ones(src.shape[0], dtype=x.dtype)
        deg = jnp.zeros(n, dtype=x.dtype).at[src].add(ones_e).at[dst].add(ones_e)
        deg_inv_sqrt = 1.0 / jnp.sqrt(jnp.maximum(deg, 1e-05))
        coef = deg_inv_sqrt[src] * deg_inv_sqrt[dst]
        msg_s = coef[:, None] * jnp.einsum('eij,ej->ei', L_sd, xd)
        msg_d = coef[:, None] * jnp.einsum('eji,ej->ei', L_sd, xs)
        out = x - jnp.zeros_like(x).at[src].add(msg_s) - jnp.zeros_like(x).at[dst].add(msg_d)
        return jax.nn.relu(out)

    def _L3_gnn_ref(node_features, edge_features, pair_indices, kernel, bias):
        import jax, jax.numpy as jnp
        import numpy as np
        N_NODES = 6250
        N_EDGES = 100000
        NODE_DIM = 16
        EDGE_DIM = 16
        d = node_features.shape[-1]
        edge_mats = (edge_features @ kernel + bias).reshape(-1, d, d)
        neighbors = node_features[pair_indices[:, 1]]
        transformed = jnp.einsum('eij,ej->ei', edge_mats, neighbors)
        aggregated = jax.ops.segment_sum(transformed, pair_indices[:, 0], num_segments=node_features.shape[0])
        return aggregated
    edge_index = jnp.stack([src, dst])
    edge_index_t = jnp.stack([src, dst], axis=1)
    x = _layernorm(x + _L0_gnn_ref(x, edge_index, L0_gnn_W1, L0_gnn_a_src1, L0_gnn_a_dst1, L0_gnn_b1, L0_gnn_W2, L0_gnn_a_src2, L0_gnn_a_dst2, L0_gnn_b2, L0_gnn_Wf, L0_gnn_bf), axis=-1)
    x = _layernorm(x + _L1_gnn_ref(x, edge_attr_8, node_vec1, L1_gnn_W_msg_tp, L1_gnn_W_msg_lin, L1_gnn_W_upd_tp, L1_gnn_W_upd_lin, edge_index), axis=-1)
    x = _layernorm(x + _L2_gnn_ref(x, edge_index, L2_gnn_W1, L2_gnn_b1, L2_gnn_W2, L2_gnn_b2), axis=-1)
    x = _layernorm(x + _L3_gnn_ref(x, edge_attr_16, edge_index_t, L3_gnn_kernel, L3_gnn_bias), axis=-1)
    return x

_drawn_inputs = setup_inputs


def setup_inputs(seed=0):
    import zlib

    import numpy as np

    out = dict(_drawn_inputs(seed))
    spreads = {'L0_gnn_b1': (0.0, 0.1),
     'L0_gnn_b2': (0.0, 0.1),
     'L0_gnn_bf': (0.0, 0.1),
     'L2_gnn_b1': (0.0, 0.8),
     'L2_gnn_b2': (0.0, 0.547),
     'L3_gnn_bias': (0.0, 0.1)}
    factors = {'L0_gnn_W1': 3.089, 'L0_gnn_a_dst1': 8.0, 'L0_gnn_a_src2': 8.0, 'L0_gnn_a_dst2': 30.105}
    for name, (base, spread) in spreads.items():
        noise = np.random.default_rng([zlib.crc32(name.encode()), seed]).standard_normal(out[name].shape)
        drawn = base * np.exp(spread * noise) if base else spread * noise
        out[name] = jnp.asarray(drawn.astype(out[name].dtype))
    for name, factor in factors.items():
        out[name] = (out[name] * factor).astype(out[name].dtype)
    return out
```

```python
from contextlib import ExitStack

import concourse.bass as bass
from concourse import mybir

P = 128
CW = 25
CT = 125
ALU = mybir.AluOpType
ACT = mybir.ActivationFunctionType
F32 = mybir.dt.float32
BF16 = mybir.dt.bfloat16
I32 = mybir.dt.int32
AX_X = mybir.AxisListType.X
BIG = 1.0e30
FAR = 4194304.0
SLOPE = 0.2
SELU_SCALE = 1.0507009873554805
SELU_ALPHA = 1.6732632423543772


class Chain:

    def __init__(self, eng, sem):
        self.eng, self.sem, self.base, self.n, self.per = eng, sem, 0, 0, None

    def begin(self, i):
        if self.per is None and self.n:
            self.per = self.n
        assert self.per is None or self.n == self.per
        self.base = 0 if self.per is None else i * self.per
        self.n = 0

    def add(self, ins):
        ins.then_inc(self.sem, 1)
        self.n += 1

    def sync(self):
        self.eng.wait_ge(self.sem, self.base + self.n)

    def link(self, ins):
        self.add(ins)
        self.sync()


def run_turns(eng, total, body):
    body(0, 0, 0, True)
    body(1, 1, 0, True)
    with eng.Fori(1, total // 2) as h:
        body(2 * h, 0, h, False)
        body(2 * h + 1, 1, h, False)
    if total % 2:
        body(total - 1, 0, total // 2, False)


def run_turns_late(eng, total, pre, post):
    pre(0, 0, 0, True)
    pre(1, 1, 0, True)
    post(0, 0, 0, True)
    pre(2, 0, 1, False)
    post(1, 1, 0, True)
    with eng.Fori(1, (total - 1) // 2) as h:
        pre(2 * h + 1, 1, h, False)
        post(2 * h, 0, h, False)
        pre(2 * h + 2, 0, h + 1, False)
        post(2 * h + 1, 1, h, False)
    if total % 2 == 0:
        pre(total - 1, 1, total // 2 - 1, False)
        post(total - 2, 0, total // 2 - 1, False)
    post(total - 1, (total - 1) % 2, (total - 1) // 2, False)


def gnn_kernel(nc, x, src, dst, edge_attr_16, edge_attr_8, node_vec1,
               L0_gnn_W1, L0_gnn_a_src1, L0_gnn_a_dst1, L0_gnn_b1, L0_gnn_W2, L0_gnn_a_src2,
               L0_gnn_a_dst2, L0_gnn_b2, L0_gnn_Wf, L0_gnn_bf,
               L1_gnn_W_msg_tp, L1_gnn_W_msg_lin, L1_gnn_W_upd_tp, L1_gnn_W_upd_lin,
               L2_gnn_W1, L2_gnn_b1, L2_gnn_W2, L2_gnn_b2, L3_gnn_kernel, L3_gnn_bias, out):
    N, D = x.shape
    E = src.shape[0]
    C = E // P
    NCH = C // CW
    NCT = C // CT
    NP = (N + P - 1) // P
    NK = P
    FULL = N // P
    REST = N - FULL * P
    NR = NP * NK
    GK = 4
    assert E == P * C and C % CW == 0 and C % CT == 0 and D == 16 and NP <= P
    H1, C1 = L0_gnn_a_src1.shape
    H2, C2 = L0_gnn_a_src2.shape
    HC1 = H1 * C1
    HID = L2_gnn_W1.shape[0]
    DE = edge_attr_8.shape[1]
    EXW = 32

    root = ExitStack()
    in_use = []

    def sem(name):
        in_use.append(nc.alloc_semaphore(name=name))
        return in_use[-1]

    def renew_semaphores():
        nc.all_engine_barrier()
        nc.clear_and_free_semaphores(list(in_use))
        in_use.clear()
        nc.all_engine_barrier()

    def sb(name, shape, dt=F32, ctx=root):
        return ctx.enter_context(nc.sbuf_tensor(name, shape, dt))

    def dram(name, shape, dt=F32):
        return nc.dram_tensor(name, shape, dt, kind="Internal").ap()

    def edges(t):
        return t.rearrange("(p c) w -> p c w", p=P)

    def node_rows(t):
        return t.rearrange("(p k) w -> p k w", k=NK)

    ex4 = dram("ex4", [E, 4])
    ex32 = dram("ex32", [E, EXW])
    marks = {o: dram(f"marks_{o}", [E, 2]) for o in ("d", "s")}
    W1R = H1 * D + 2 * H1
    W2R = C2 + 2
    gat1_sums = dram("gat1_sums", [E, W1R])
    gat2_sums = dram("gat2_sums", [E, W2R])
    table1 = dram("table1", [NR, 20])
    table2 = dram("table2", [NR, 36])
    table3 = dram("table3", [NR, 20])
    pos_rows = dram("pos_rows", [P, C], I32)
    msgs = dram("msgs", [E, D])
    src_sums = dram("src_sums", [E, D])
    dst_sums = dram("dst_sums", [E, D])

    src_v = src.rearrange("(p c) -> p c", p=P)
    dst_v = dst.rearrange("(p c) -> p c", p=P)

    with root:
        ident = sb("ident", [P, P])
        ident_b = sb("ident_b", [P, P], BF16)
        before = sb("before", [P, P])
        iota_b = sb("iota_b", [P, P], BF16)
        x_cur = sb("x_cur", [NP, NK, D])
        x_new = sb("x_new", [NP, NK, D])
        first_edge = sb("first_edge", [P, 1])
        last_edge = sb("last_edge", [P, 1])
        keep = {o: sb(f"keep_{o}", [P, C]) for o in ("d", "s")}
        fresh = sb("fresh", [P, C])

        def order_arrays(o):
            return dict(
                has=sb(f"has_{o}", [NP, NK]), start=sb(f"start_{o}", [NP, NK]),
                put=sb(f"put_{o}", [NP, NK], I32), take=sb(f"take_{o}", [NP, NK], I32),
                begins=sb(f"begins_{o}", [P, 1], I32), whole=sb(f"whole_{o}", [P, 1]),
                fix_get=sb(f"fix_get_{o}", [P, 1], I32), fix_put=sb(f"fix_put_{o}", [P, 1], I32))

        order = {o: order_arrays(o) for o in ("d", "s")}
        cnt = sb("cnt", [NP, NK])
        deg = sb("deg", [NP, NK])

        def setup():
            with ExitStack() as ctx:
                zeros = sb("zeros", [P, CW * EXW * 5], F32, ctx)
                it = sb("it", [P, P], I32, ctx)
                ones = sb("ones", [P, P], F32, ctx)
                fe = sb("fe", [P, 2], I32, ctx)
                zeroed, made, loaded, cleared, tables = (
                    sem("zeroed"), sem("made"), sem("loaded"), sem("cleared"), sem("tables"))
                block = ctx.enter_context(nc.Block())

                @block.gpsimd
                def _(pool):
                    chain = Chain(pool, made)
                    chain.add(pool.memset(ones[:, :], 1.0))
                    chain.add(pool.memset(ident[:, :], 0.0))
                    chain.add(pool.iota(it[:, :], [[1, P]], base=0, channel_multiplier=0))
                    chain.link(pool.iota(fe[:, 0:1], [[1, 1]], base=0, channel_multiplier=C))
                    chain.link(pool.iota(fe[:, 1:2], [[1, 1]], base=C, channel_multiplier=C))
                    chain.add(pool.affine_select(out=ident[:, :], in_=ident[:, :], compare_op=ALU.not_equal,
                                                 fill=1.0, base=0, pattern=[[-1, P]], channel_multiplier=1))
                    chain.add(pool.affine_select(out=before[:, :], in_=ones[:, :], compare_op=ALU.is_gt,
                                                 fill=0.0, base=0, pattern=[[1, P]], channel_multiplier=-1))

                @block.vector
                def _(dve):
                    dve.memset(zeros[:, :], 0.0).then_inc(zeroed, 1)
                    dve.memset(x_cur[:, :, :], 0.0).then_inc(cleared, 1)
                    dve.wait_ge(made, 7)
                    dve.tensor_copy(ident_b[:, :], ident[:, :])
                    dve.tensor_copy(iota_b[:, :], it[:, :])
                    dve.tensor_copy(first_edge[:, :], fe[:, 0:1])
                    dve.tensor_copy(last_edge[:, :], fe[:, 1:2])

                @block.sync
                def _(sp):
                    sp.wait_ge(cleared, 1)
                    sp.dma_start(x_cur[0:FULL, :, :], x[0:FULL * P, :].rearrange("(p k) d -> p k d", k=NK)
                                 ).then_inc(loaded, 16)
                    if REST:
                        sp.dma_start(x_cur[FULL:NP, 0:REST, :],
                                     x[FULL * P:N, :].rearrange("(p k) d -> p k d", k=REST)).then_inc(loaded, 16)
                    sp.wait_ge(zeroed, 1)
                    flat = ex32.rearrange("(p c) w -> p (c w)", p=P)
                    width = CW * EXW * 5
                    with sp.Fori(0, C * EXW // width) as i:
                        sp.dma_start(flat[:, bass.ds(i * width, width)], zeros[:, :]).then_inc(tables, 16)
                    for t, w in ((ex4, 4), (marks["d"], 2), (marks["s"], 2)):
                        flat_t = t.rearrange("(p c) w -> p (c w)", p=P)
                        step = CT * w
                        with sp.Fori(0, NCT) as i:
                            sp.dma_start(flat_t[:, bass.ds(i * step, step)], zeros[:, 0:step]).then_inc(tables, 16)
                    sp.wait_ge(tables, 16 * (C * EXW // width + 3 * NCT))
                    sp.wait_ge(loaded, 32 if REST else 16)

        class OneHots:

            def __init__(self, name, ctx):
                self.key = [sb(f"{name}_key{b}", [P, CW], I32, ctx) for b in range(2)]
                self.part = sb(f"{name}_part", [P, 2, CW], I32, ctx)
                self.part_b = sb(f"{name}_part_b", [P, 2, CW], BF16, ctx)
                self.hot_a = [sb(f"{name}_hot_a{b}", [P, CW, NP], BF16, ctx) for b in range(2)]
                self.hot_k = [sb(f"{name}_hot_k{b}", [P, CW, NK], BF16, ctx) for b in range(2)]

            def make(self, chain, dve, b, ready):
                chain.add(dve.tensor_scalar(self.part[:, 0, :], self.key[b][:, :], 7, None,
                                            ALU.logical_shift_right))
                chain.link(dve.tensor_scalar(self.part[:, 1, :], self.key[b][:, :], NK - 1, None,
                                             ALU.bitwise_and))
                chain.link(dve.tensor_copy(self.part_b[:, :, :], self.part[:, :, :]))
                pa, pk = (self.part_b[:, n, :].unsqueeze(2) for n in range(2))
                chain.add(dve.tensor_tensor(self.hot_a[b][:, :, :], iota_b[:, 0:NP].unsqueeze(1).to_broadcast([P, CW, NP]),
                                            pa.to_broadcast([P, CW, NP]), ALU.is_equal))
                dve.tensor_tensor(self.hot_k[b][:, :, :], iota_b[:, :].unsqueeze(1).to_broadcast([P, CW, NK]),
                                  pk.to_broadcast([P, CW, NK]), ALU.is_equal).then_inc(ready, 1)

        class Histogram:

            def __init__(self, name, keys, ctx):
                self.keys = keys
                self.counts = ctx.enter_context(nc.psum_tensor(f"{name}_counts", [P, 512], F32))
                self.hots = OneHots(name, ctx)
                self.zero = sb(f"{name}_zero", [P, P], BF16, ctx)
                self.loaded = [sem(f"{name}_loaded{b}") for b in range(2)]
                self.steps, self.ready, self.counted, self.zero_set = (
                    sem(f"{name}_steps"), sem(f"{name}_ready"), sem(f"{name}_counted"), sem(f"{name}_zero_set"))

            def load(self, sp, i, b, first):
                if not first:
                    sp.wait_ge(self.ready, i - 1)
                sp.dma_start(self.hots.key[b][:, :], self.keys[:, bass.ds(i * CW, CW)]).then_inc(self.loaded[b], 16)

            def dve_start(self, dve):
                dve.memset(self.zero[:, :], 0.0).then_inc(self.zero_set, 1)
                self.chain = Chain(dve, self.steps)

            def dve(self, dve, i, b, turn, first):
                self.chain.begin(i)
                dve.wait_ge(self.loaded[b], 16 * turn + 16)
                if not first:
                    dve.wait_ge(self.counted, i - 1)
                self.hots.make(self.chain, dve, b, self.ready)

            def pe_start(self, pe):
                pe.wait_ge(self.zero_set, 1)
                pe.matmul(self.counts[0:NP, 0:NK], self.zero[:, 0:NP], self.zero[:, 0:NK], start=True, stop=False,
                          skip_group_check=True)

            def pe(self, pe, i, b, turn, first):
                pe.wait_ge(self.ready, i + 1)
                for t in range(CW):
                    last = pe.matmul(self.counts[0:NP, 0:NK], self.hots.hot_a[b][:, t, :], self.hots.hot_k[b][:, t, :],
                                     start=False, stop=False, skip_group_check=True)
                last.then_inc(self.counted, 1)

            def finish(self, dve):
                dve.wait_ge(self.counted, NCH)
                dve.tensor_copy(cnt[:, :], self.counts[0:NP, 0:NK])

        def count_destinations():
            with ExitStack() as ctx:
                hist = Histogram("hist_d", dst_v, ctx)
                block = ctx.enter_context(nc.Block())

                @block.sync
                def _(sp):
                    run_turns(sp, NCH, lambda i, b, turn, first: hist.load(sp, i, b, first))

                @block.vector
                def _(dve):
                    hist.dve_start(dve)
                    run_turns(dve, NCH, lambda i, b, turn, first: hist.dve(dve, i, b, turn, first))
                    hist.finish(dve)

                @block.tensor
                def _(pe):
                    hist.pe_start(pe)
                    run_turns(pe, NCH, lambda i, b, turn, first: hist.pe(pe, i, b, turn, first))

        def find_segments(o):
            g = order[o]
            with ExitStack() as ctx:
                incl, end = sb(f"incl_{o}", [NP, NK], F32, ctx), sb(f"end_{o}", [NP, NK], F32, ctx)
                tmp, zero = sb(f"tmp_{o}", [NP, NK], F32, ctx), sb(f"zero_{o}", [NP, NK], F32, ctx)
                mark = sb(f"mark_{o}", [NP, NK, 2], F32, ctx)
                mk = sb(f"mk_{o}", [P, C, 2], F32, ctx)
                top, row, row2 = (sb(f"top_{o}", [P, 2], F32, ctx), sb(f"row_{o}", [2, P], F32, ctx),
                                  sb(f"row2_{o}", [2, P + 1], F32, ctx))
                seg = sb(f"seg_{o}", [P, 2], F32, ctx)
                v = sb(f"v_{o}", [P, 8], F32, ctx)
                zrow = sb(f"zrow_{o}", [2, P], F32, ctx)
                ps = ctx.enter_context(nc.psum_tensor(f"ps_{o}", [P, 512], F32))
                steps, totals, offs, marked, put_done, got, t1, t2 = (
                    sem(f"seg_{n}_{o}") for n in ("steps", "totals", "offs", "marked", "put", "got", "t1", "t2"))
                rowed, backed, shifted, topped = (sem(f"seg_{n}_{o}") for n in ("rowed", "backed", "shifted", "topped"))
                block = ctx.enter_context(nc.Block())

                @block.vector
                def _(dve):
                    ch = Chain(dve, steps)
                    if o == "d":
                        ch.link(dve.tensor_copy(deg[:, :], cnt[:, :]))
                    else:
                        ch.link(dve.tensor_tensor(deg[:, :], deg[:, :], cnt[:, :], ALU.add))
                    ch.link(dve.memset(zero[:, :], 0.0))
                    dve.tensor_tensor_scan(incl[:, :], cnt[:, :], zero[:, :], 0.0, ALU.add, ALU.add).then_inc(totals, 1)
                    dve.wait_ge(offs, 1)
                    ch.add(dve.tensor_scalar(g["has"][:, :], cnt[:, :], 0.0, None, ALU.is_gt))
                    ch.link(dve.tensor_copy(v[0:NP, 0:1], ps[0:NP, 0:1]))
                    ch.link(dve.tensor_scalar(end[:, :], incl[:, :], v[0:NP, 0:1], None, ALU.add))
                    ch.link(dve.tensor_tensor(g["start"][:, :], end[:, :], cnt[:, :], ALU.subtract))
                    ch.add(dve.tensor_scalar(mark[:, :, 0], g["start"][:, :], 1.0, None, ALU.add))
                    ch.add(dve.tensor_copy(mark[:, :, 1], end[:, :]))
                    ch.link(dve.tensor_scalar(tmp[:, :], g["has"][:, :], -FAR, FAR, ALU.mult, ALU.add))
                    ch.link(dve.tensor_tensor(tmp[:, :], tmp[:, :], g["start"][:, :], ALU.add))
                    ch.link(dve.tensor_copy(g["put"][:, :], tmp[:, :]))
                    ch.link(dve.tensor_scalar(tmp[:, :], end[:, :], -1.0, 0.0, ALU.add, ALU.max))
                    dve.tensor_copy(g["take"][:, :], tmp[:, :]).then_inc(marked, 1)
                    dve.wait_ge(got, 16)
                    if o == "d":
                        ch.add(dve.tensor_scalar(fresh[:, :], mk[:, :, 1], 0.0, -BIG, ALU.is_gt, ALU.mult))
                    ch.add(dve.tensor_scalar(keep[o][:, :], mk[:, :, 1], 0.0, None, ALU.is_equal))
                    ch.add(dve.memset(zrow[:, :], 0.0))
                    ch.add(dve.memset(row2[:, 0:1], 0.0))
                    dve.tensor_reduce(top[:, :], mk[:, :, :].rearrange("p c w -> p w c"), AX_X, ALU.max).then_inc(topped, 1)
                    dve.wait_ge(rowed, 1)
                    ch.link(dve.tensor_copy(row[:, :], ps[0:2, 128:256]))
                    dve.tensor_tensor_scan(row2[:, 1:P + 1], zrow[:, :], row[:, :], 0.0, ALU.add, ALU.max
                                           ).then_inc(shifted, 1)
                    dve.wait_ge(backed, 1)
                    ch.link(dve.tensor_tensor(seg[:, :], ps[:, 256:258], mk[:, 0, :], ALU.max))
                    a1, b = seg[:, 0:1], seg[:, 1:2]
                    ch.add(dve.tensor_tensor(v[:, 0:1], a1, first_edge[:, :], ALU.is_le))
                    ch.add(dve.tensor_tensor(v[:, 1:2], b, last_edge[:, :], ALU.is_le))
                    ch.add(dve.tensor_tensor(v[:, 2:3], b, last_edge[:, :], ALU.is_ge))
                    ch.add(dve.tensor_scalar(v[:, 3:4], b, -1.0, None, ALU.add))
                    ch.link(dve.tensor_scalar(v[:, 4:5], a1, -1.0, None, ALU.add))
                    ch.add(dve.tensor_tensor(g["whole"][:, :], v[:, 0:1], v[:, 2:3], ALU.mult))
                    ch.add(dve.tensor_copy(g["fix_get"][:, :], v[:, 3:4]))
                    ch.add(dve.tensor_copy(g["begins"][:, :], v[:, 4:5]))
                    ch.link(dve.tensor_tensor(v[:, 5:6], v[:, 0:1], v[:, 1:2], ALU.mult))
                    ch.link(dve.tensor_scalar(v[:, 6:7], v[:, 5:6], -FAR, FAR, ALU.mult, ALU.add))
                    ch.link(dve.tensor_tensor(v[:, 7:8], v[:, 6:7], v[:, 3:4], ALU.add))
                    ch.link(dve.tensor_copy(g["fix_put"][:, :], v[:, 7:8]))

                @block.tensor
                def _(pe):
                    pe.wait_ge(totals, 1)
                    pe.matmul(ps[0:NP, 0:1], before[0:NP, 0:NP], incl[:, NK - 1:NK], start=True, stop=True
                              ).then_inc(offs, 1)
                    pe.wait_ge(topped, 1)
                    pe.transpose(ps[0:2, 128:256], top[:, :], ident[:, :]).then_inc(rowed, 1)
                    pe.wait_ge(shifted, 1)
                    pe.transpose(ps[:, 256:258], row2[:, 0:P], ident[0:2, 0:2]).then_inc(backed, 1)

                @block.gpsimd
                def _(pool):
                    pool.wait_ge(marked, 1)
                    for k in range(NK):
                        pool.indirect_dma_start(marks[o], bass.IndirectOffsetOnAxis(g["put"][:, k:k + 1], 0),
                                                mark[:, k, :], None, bounds_check=E - 1, oob_is_err=False
                                                ).then_inc(put_done, 16)

                @block.sync
                def _(sp):
                    sp.wait_ge(put_done, 16 * NK)
                    sp.dma_start(mk[:, :, :], edges(marks[o])).then_inc(got, 16)

        def node_product(name, widths, fill, weights, cols, use, middle=None):
            groups = NK // GK
            L = GK * NP
            total = sum(widths)
            starts = [sum(widths[:n]) for n in range(len(widths))]
            with ExitStack() as ctx:
                stage = [sb(f"{name}_stage{b}", [NP, GK, total], F32, ctx) for b in range(2)]
                flipped = [[sb(f"{name}_flip{b}_{n}", [w, L], F32, ctx) for n, w in enumerate(widths)] for b in range(2)]
                flip_ps = [[ctx.enter_context(nc.psum_tensor(f"{name}_fps{b}_{n}", [P, 512], F32))
                            for n in range(len(widths))] for b in range(2)]
                prod_ps = [ctx.enter_context(nc.psum_tensor(f"{name}_pps{b}", [P, 512], F32)) for b in range(2)]
                s = {n: sem(f"{name}_{n}") for n in
                     ("fill_steps", "staged", "turned", "flipped", "multiplied", "use_steps", "used", "mid_multiplied",
                      "mid_steps", "mid_done", "admitted")}
                if middle:
                    mid_w, M, mid_function = middle
                    mid_ps = [ctx.enter_context(nc.psum_tensor(f"{name}_mps{b}", [P, 512], F32)) for b in range(2)]
                    mid = [[sb(f"{name}_mid{b}{n}", [M, L], F32, ctx) for n in range(2)] for b in range(2)]
                block = ctx.enter_context(nc.Block())

                @block.vector
                def _(dve):
                    filling, using = Chain(dve, s["fill_steps"]), Chain(dve, s["use_steps"])

                    def take(i, b, turn, first):
                        using.begin(i)
                        dve.wait_ge(s["multiplied"], i + 1)
                        use(dve, using, i, prod_ps[b][0:NP, 0:GK * cols].rearrange("p (k w) -> p k w", w=cols)
                            ).then_inc(s["used"], 1)

                    def put(i, b, turn, first):
                        filling.begin(i)
                        if not first:
                            dve.wait_ge(s["turned"], i - 1)
                        fill(dve, filling, i, stage[b]).then_inc(s["staged"], 1)

                    run_turns_late(dve, groups, put, take)

                @block.tensor
                def _(pe):
                    def body(i, b, turn, first):
                        pe.wait_ge(s["staged"], i + 1)
                        if not first:
                            pe.wait_ge(s["flipped"], i - 1)
                        pe.sem_inc(s["admitted"], 1)
                        for n, w in enumerate(widths):
                            for k in range(GK):
                                last = pe.transpose(flip_ps[b][n][0:w, k * NP:(k + 1) * NP],
                                                    stage[b][:, k, starts[n]:starts[n] + w], ident[0:NP, 0:NP])
                        last.then_inc(s["turned"], 1)
                        pe.wait_ge(s["flipped"], i + 1)
                        pe.sem_inc(s["admitted"], 1)
                        left = flipped[b]
                        if middle:
                            pe.matmul(mid_ps[b][0:M, 0:L], mid_w, flipped[b][0][:, :], start=True, stop=True
                                      ).then_inc(s["mid_multiplied"], 1)
                            pe.wait_ge(s["mid_done"], i + 1)
                            left = mid[b]
                        if not first:
                            pe.wait_ge(s["used"], i - 1)
                        for k in range(GK):
                            for n in range(len(left)):
                                last = pe.matmul(prod_ps[b][0:NP, k * cols:(k + 1) * cols],
                                                 left[n][:, k * NP:(k + 1) * NP], weights[n],
                                                 start=(n == 0), stop=(n == len(left) - 1))
                        last.then_inc(s["multiplied"], 1)

                    run_turns(pe, groups, body)

                @block.scalar
                def _(act):
                    mid_chain = Chain(act, s["mid_steps"])

                    def body(i, b, turn, first):
                        act.wait_ge(s["turned"], i + 1)
                        if not first:
                            act.wait_ge(s["multiplied"], i - 1)
                        for n, w in enumerate(widths):
                            last = act.copy(flipped[b][n][:, :], flip_ps[b][n][0:w, 0:L])
                        last.then_inc(s["flipped"], 1)
                        if middle:
                            mid_chain.begin(i)
                            act.wait_ge(s["mid_multiplied"], i + 1)
                            mid_function(act, mid_chain, mid[b], mid_ps[b][0:M, 0:L]).then_inc(s["mid_done"], 1)

                    run_turns(act, groups, body)

        def whole_groups(src_tile, scale=1.0):
            def fill(dve, ch, i, stage):
                return dve.tensor_scalar(stage[:, :, :], src_tile[:, bass.ds(i * GK, GK), :], scale, None, ALU.mult)
            return fill

        def into(dst_tile, scale=1.0):
            def use(dve, ch, i, prod):
                return dve.tensor_scalar(dst_tile[:, bass.ds(i * GK, GK), :], prod, scale, None, ALU.mult)
            return use

        def load_all(name, pairs, ctx):
            done = sem(f"{name}_in")
            with nc.Block() as block:
                @block.sync
                def _(sp):
                    with nc.allow_non_contiguous_dma(reason="small weights"):
                        for d, s_ in pairs:
                            sp.dma_start(d, s_).then_inc(done, 16)
                    sp.wait_ge(done, 16 * len(pairs))

        def on_vector(name, body):
            steps = sem(f"{name}_steps")
            with nc.Block() as block:
                @block.vector
                def _(dve):
                    body(dve, Chain(dve, steps))

        def spread(row, parts, w):
            return row.unsqueeze(0).to_broadcast([parts, w])

        def put_rows(name, table_rows, table_tile, starts_tile, starts_table, width):
            stored, put = sem(f"{name}_stored"), sem(f"{name}_put")
            with nc.Block() as block:
                if table_rows is not None:
                    @block.sync
                    def _(sp):
                        sp.dma_start(node_rows(table_rows), table_tile[:, :, :]).then_inc(stored, 16)
                        sp.wait_ge(stored, 16)

                @block.gpsimd
                def _(pool):
                    for k in range(NK):
                        pool.indirect_dma_start(starts_table, bass.IndirectOffsetOnAxis(order["d"]["put"][:, k:k + 1], 0),
                                                starts_tile[:, k, :], None, bounds_check=E - 1, oob_is_err=False
                                                ).then_inc(put, 16)
                    pool.wait_ge(put, 16 * NK)

        def take_rows(name, o, table, tile, w, fixed_rows=None):
            took = sem(f"{name}_took")
            with nc.Block() as block:
                @block.gpsimd
                def _(pool):
                    for k in range(NK):
                        pool.indirect_dma_start(tile[:, k, :], None, table,
                                                bass.IndirectOffsetOnAxis(order[o]["take"][:, k:k + 1], 0)
                                                ).then_inc(took, 16)
                    pool.wait_ge(took, 16 * NK)

        def join_sums(name, o, table, w, last_rows):
            with ExitStack() as ctx:
                wide, rows = sb(f"{name}_wide", [P, w], F32, ctx), sb(f"{name}_rows", [w, 3, P + 1], F32, ctx)
                at = sb(f"{name}_at", [P, w], F32, ctx)
                ps = ctx.enter_context(nc.psum_tensor(f"{name}_ps", [P, 512], F32))
                steps, ready, turned, summed, back, got, fixed, put = (
                    sem(f"{name}_{n}") for n in ("steps", "ready", "turned", "summed", "back", "got", "fixed", "put"))
                block = ctx.enter_context(nc.Block())

                @block.vector
                def _(dve):
                    ch = Chain(dve, steps)
                    dve.tensor_copy(wide[:, :], order[o]["whole"][:, :].to_broadcast([P, w])).then_inc(ready, 1)
                    dve.wait_ge(turned, 1)
                    ch.add(dve.tensor_copy(rows[:, 0, 0:P], ps[0:w, 0:P]))
                    ch.add(dve.memset(rows[:, 2, 0:1], 0.0))
                    ch.link(dve.tensor_copy(rows[:, 1, 0:P], ps[0:w, P:2 * P]))
                    dve.tensor_tensor_scan(rows[:, 2, 1:P + 1], rows[:, 1, 0:P], rows[:, 0, 0:P], 0.0, ALU.mult, ALU.add
                                           ).then_inc(summed, 1)
                    dve.wait_ge(back, 1)
                    dve.wait_ge(got, 16)
                    dve.tensor_tensor(at[:, :], at[:, :], ps[:, 2 * P:2 * P + w], ALU.add).then_inc(fixed, 1)

                @block.tensor
                def _(pe):
                    pe.wait_ge(ready, 1)
                    pe.transpose(ps[0:w, 0:P], last_rows[:, :], ident[:, :])
                    pe.transpose(ps[0:w, P:2 * P], wide[:, :], ident[:, :]).then_inc(turned, 1)
                    pe.wait_ge(summed, 1)
                    pe.transpose(ps[:, 2 * P:2 * P + w], rows[:, 2, 0:P], ident[0:w, 0:w]).then_inc(back, 1)

                @block.gpsimd
                def _(pool):
                    pool.indirect_dma_start(at[:, :], None, table, bass.IndirectOffsetOnAxis(order[o]["fix_get"][:, 0:1], 0)
                                            ).then_inc(got, 16)
                    pool.wait_ge(fixed, 1)
                    pool.indirect_dma_start(table, bass.IndirectOffsetOnAxis(order[o]["fix_put"][:, 0:1], 0), at[:, :], None,
                                            bounds_check=E - 1, oob_is_err=False).then_inc(put, 16)
                    pool.wait_ge(put, 16)

        def join_softmax(name, heads, feats, table, last_rows):
            w = heads * (feats + 1)
            full = w + heads
            with ExitStack() as ctx:
                tops, wide = sb(f"{name}_tops", [P, w], F32, ctx), sb(f"{name}_wide", [P, w], F32, ctx)
                rows = sb(f"{name}_rows", [w, 7, P + 1], F32, ctx)
                at, at_top = sb(f"{name}_at", [P, full], F32, ctx), sb(f"{name}_at_top", [P, w], F32, ctx)
                cin = sb(f"{name}_cin", [P, 2, w], F32, ctx)
                new_top, e1, e2 = (sb(f"{name}_{n}", [P, w], F32, ctx) for n in ("new_top", "e1", "e2"))
                done = sb(f"{name}_done", [P, full], F32, ctx)
                ps = ctx.enter_context(nc.psum_tensor(f"{name}_ps", [P, 512], F32))
                ps2 = ctx.enter_context(nc.psum_tensor(f"{name}_ps2", [P, 512], F32))
                steps, ready, turned, summed, back, got, fixed, put, ask, said = (
                    sem(f"{name}_{n}") for n in
                    ("steps", "ready", "turned", "summed", "back", "got", "fixed", "put", "ask", "said"))
                block = ctx.enter_context(nc.Block())

                def by_head(t, rows_ap, first, last):
                    for h in range(heads):
                        yield (t[:, h * feats:(h + 1) * feats], rows_ap[:, w + h:w + h + 1].to_broadcast([P, feats]))
                        yield (t[:, heads * feats + h:heads * feats + h + 1], rows_ap[:, w + h:w + h + 1])

                @block.vector
                def _(dve):
                    ch = Chain(dve, steps)
                    for o_, i_ in by_head(tops, last_rows, 0, 0):
                        ch.add(dve.tensor_copy(o_, i_))
                    ch.sync()
                    dve.tensor_scalar(wide[:, :], order["d"]["whole"][:, :].to_broadcast([P, w]), BIG, -BIG, ALU.mult, ALU.add
                                      ).then_inc(ready, 1)
                    dve.wait_ge(turned, 1)
                    A, B, T, M, DD, S, X = (rows[:, n, :] for n in range(7))
                    ch.add(dve.tensor_copy(A[:, 0:P], ps[0:w, 0:P]))
                    ch.add(dve.tensor_copy(B[:, 0:P], ps[0:w, P:2 * P]))
                    ch.add(dve.tensor_copy(T[:, 0:P], ps[0:w, 2 * P:3 * P]))
                    ch.add(dve.memset(M[:, 0:1], -BIG))
                    ch.link(dve.memset(S[:, 0:1], 0.0))
                    ch.link(dve.tensor_tensor_scan(M[:, 1:P + 1], B[:, 0:P], T[:, 0:P], -BIG, ALU.add, ALU.max))
                    ch.add(dve.tensor_tensor(T[:, 0:P], T[:, 0:P], M[:, 1:P + 1], ALU.subtract))
                    ch.link(dve.tensor_tensor(DD[:, 0:P], M[:, 0:P], B[:, 0:P], ALU.add))
                    dve.tensor_tensor(DD[:, 0:P], DD[:, 0:P], M[:, 1:P + 1], ALU.subtract).then_inc(ask, 1)
                    dve.wait_ge(said, 1)
                    ch.link(dve.tensor_tensor(X[:, 0:P], A[:, 0:P], T[:, 0:P], ALU.mult))
                    dve.tensor_tensor_scan(S[:, 1:P + 1], DD[:, 0:P], X[:, 0:P], 0.0, ALU.mult, ALU.add).then_inc(summed, 1)
                    dve.wait_ge(got, 16)
                    for o_, i_ in by_head(at_top, at, 0, 0):
                        ch.add(dve.tensor_copy(o_, i_))
                    dve.wait_ge(back, 1)
                    ch.add(dve.tensor_copy(cin[:, 0, :], ps2[:, 0:w]))
                    ch.link(dve.tensor_copy(cin[:, 1, :], ps2[:, w:2 * w]))
                    ch.link(dve.tensor_tensor(new_top[:, :], at_top[:, :], cin[:, 1, :], ALU.max))
                    ch.add(dve.tensor_tensor(e1[:, :], at_top[:, :], new_top[:, :], ALU.subtract))
                    dve.tensor_tensor(e2[:, :], cin[:, 1, :], new_top[:, :], ALU.subtract).then_inc(ask, 1)
                    dve.wait_ge(said, 2)
                    ch.add(dve.tensor_tensor(e1[:, :], e1[:, :], at[:, 0:w], ALU.mult))
                    ch.add(dve.tensor_tensor(e2[:, :], e2[:, :], cin[:, 0, :], ALU.mult))
                    for h in range(heads):
                        ch.add(dve.tensor_copy(done[:, w + h:w + h + 1], new_top[:, heads * feats + h:heads * feats + h + 1]))
                    ch.sync()
                    dve.tensor_tensor(done[:, 0:w], e1[:, :], e2[:, :], ALU.add).then_inc(fixed, 1)

                @block.scalar
                def _(act):
                    act.wait_ge(ask, 1)
                    act.activation(rows[:, 2, 0:P], rows[:, 2, 0:P], ACT.Exp)
                    act.activation(rows[:, 4, 0:P], rows[:, 4, 0:P], ACT.Exp).then_inc(said, 1)
                    act.wait_ge(ask, 2)
                    act.activation(e1[:, :], e1[:, :], ACT.Exp)
                    act.activation(e2[:, :], e2[:, :], ACT.Exp).then_inc(said, 1)

                @block.tensor
                def _(pe):
                    pe.wait_ge(ready, 1)
                    pe.transpose(ps[0:w, 0:P], last_rows[:, 0:w], ident[:, :])
                    pe.transpose(ps[0:w, P:2 * P], wide[:, :], ident[:, :])
                    pe.transpose(ps[0:w, 2 * P:3 * P], tops[:, :], ident[:, :]).then_inc(turned, 1)
                    pe.wait_ge(summed, 1)
                    pe.transpose(ps2[:, 0:w], rows[:, 5, 0:P], ident[0:w, 0:w])
                    pe.transpose(ps2[:, w:2 * w], rows[:, 3, 0:P], ident[0:w, 0:w]).then_inc(back, 1)

                @block.gpsimd
                def _(pool):
                    pool.indirect_dma_start(at[:, :], None, table,
                                            bass.IndirectOffsetOnAxis(order["d"]["fix_get"][:, 0:1], 0)).then_inc(got, 16)
                    pool.wait_ge(fixed, 1)
                    pool.indirect_dma_start(table, bass.IndirectOffsetOnAxis(order["d"]["fix_put"][:, 0:1], 0),
                                            done[:, :], None, bounds_check=E - 1, oob_is_err=False).then_inc(put, 16)
                    pool.wait_ge(put, 16)

        def attention(name, heads, feats, table, tw, sums, last_rows, extra):
            w = heads * (feats + 1)
            full = w + heads
            sums_v = edges(sums)
            ex_v = edges(ex4)
            with ExitStack() as ctx:
                idx = [sb(f"{name}_idx{b}", [P, CW], I32, ctx) for b in range(2)]
                got = [sb(f"{name}_got{b}", [P, CW, tw], F32, ctx) for b in range(2)]
                ex = [sb(f"{name}_ex{b}", [P, CW, 4], F32, ctx) for b in range(2)]
                ad = [sb(f"{name}_ad{b}", [P, heads, CW], F32, ctx) for b in range(2)]
                sc = sb(f"{name}_sc", [P, heads, CW], F32, ctx)
                top = [sb(f"{name}_top{b}", [P, heads, CW + 1], F32, ctx) for b in range(2)]
                ex_in = sb(f"{name}_ex_in", [P, 2, heads, CW], F32, ctx)
                ex_out = sb(f"{name}_ex_out", [P, 2, heads, CW], F32, ctx)
                px = sb(f"{name}_px", [P, heads, feats, CW], F32, ctx)
                acc = [sb(f"{name}_acc{b}", [P, CW, full], F32, ctx) for b in range(2)]
                first_row = sb(f"{name}_first", [P, 4], F32, ctx)
                idx_in, ex_in_s, gathered, stored = ([sem(f"{name}_{n}{b}") for b in range(2)]
                                                     for n in ("idx_in", "ex_in", "gathered", "stored"))
                steps, spread_, asked, said, done, admitted, let_in, first_got, start_steps = (
                    sem(f"{name}_{n}") for n in
                    ("steps", "spread", "asked", "said", "done", "admitted", "let_in", "first_got", "start_steps"))
                extra.allocate(ctx)
                block = ctx.enter_context(nc.Block())

                @block.sync
                def _(sp):
                    def body(i, b, turn, first):
                        if not first:
                            sp.wait_ge(gathered[b], 16 * CW * turn)
                        sp.dma_start(idx[b][:, :], src_v[:, bass.ds(i * CW, CW)]).then_inc(idx_in[b], 16)
                        if not first:
                            sp.wait_ge(spread_, i - 1)
                            sp.sem_inc(let_in, 1)
                        sp.dma_start(ex[b][:, :, :], ex_v[:, bass.ds(i * CW, CW), :]).then_inc(ex_in_s[b], 16)
                        extra.sync(sp, i, b, turn, first)
                    run_turns(sp, NCH, body)
                    extra.sync_end(sp)

                @block.gpsimd
                def _(pool):
                    pool.indirect_dma_start(first_row[:, :], None, ex4,
                                            bass.IndirectOffsetOnAxis(order["d"]["begins"][:, 0:1], 0)).then_inc(first_got, 16)

                    def body(i, b, turn, first):
                        pool.wait_ge(idx_in[b], 16 * turn + 16)
                        if not first:
                            pool.wait_ge(done, i - 1)
                        pool.sem_inc(admitted, 1)
                        for j in range(CW):
                            pool.indirect_dma_start(got[b][:, j, :], None, table,
                                                    bass.IndirectOffsetOnAxis(idx[b][:, j:j + 1], 0)
                                                    ).then_inc(gathered[b], 16)
                    run_turns(pool, NCH, body)

                @block.vector
                def _(dve):
                    start = Chain(dve, start_steps)
                    dve.wait_ge(first_got, 16)
                    for h in range(heads):
                        start.add(dve.tensor_copy(ad[1][:, h, CW - 1:CW], first_row[:, h:h + 1]))
                    start.add(dve.memset(top[1][:, :, CW:CW + 1], -BIG))
                    start.add(dve.memset(acc[1][:, CW - 1, :], 0.0))
                    start.sync()
                    extra.vector_start(dve)
                    ch = Chain(dve, steps)

                    def body(i, b, turn, first):
                        extra.vector(dve, i, b, turn, first)
                        ch.begin(i)
                        kp, fr = keep["d"][:, bass.ds(i * CW, CW)], fresh[:, bass.ds(i * CW, CW)]
                        dve.wait_ge(ex_in_s[b], 16 * turn + 16)
                        for h in range(heads):
                            last = dve.tensor_tensor_scan(ad[b][:, h, :], kp, ex[b][:, :, h], ad[1 - b][:, h, CW - 1:CW],
                                                          ALU.mult, ALU.add)
                        last.then_inc(spread_, 1)
                        dve.wait_ge(spread_, i + 1)
                        dve.wait_ge(gathered[b], 16 * CW * (turn + 1))
                        g_x = got[b][:, :, 0:feats].rearrange("p t f -> p f t")
                        g_a = got[b][:, :, feats:feats + heads].rearrange("p t f -> p f t")
                        ch.add(dve.tensor_copy(top[b][:, :, 0:1], top[1 - b][:, :, CW:CW + 1]))
                        ch.link(dve.tensor_tensor(sc[:, :, :], ad[b][:, :, :], g_a, ALU.add))
                        ch.link(dve.scalar_tensor_tensor(out=sc[:, :, :], in0=sc[:, :, :], scalar=SLOPE, in1=sc[:, :, :],
                                                         op0=ALU.mult, op1=ALU.max))
                        for h in range(heads):
                            ch.add(dve.tensor_tensor_scan(top[b][:, h, 1:CW + 1], fr, sc[:, h, :],
                                                          top[1 - b][:, h, CW:CW + 1], ALU.add, ALU.max))
                        ch.sync()
                        ch.add(dve.tensor_tensor(ex_in[:, 1, :, :], sc[:, :, :], top[b][:, :, 1:CW + 1], ALU.subtract))
                        ch.link(dve.tensor_tensor(ex_in[:, 0, :, :], top[b][:, :, 0:CW],
                                                  fr.unsqueeze(1).to_broadcast([P, heads, CW]), ALU.add))
                        dve.tensor_tensor(ex_in[:, 0, :, :], ex_in[:, 0, :, :], top[b][:, :, 1:CW + 1], ALU.subtract
                                          ).then_inc(asked, 1)
                        dve.wait_ge(said, i + 1)
                        p = ex_out[:, 1, :, :]
                        ch.link(dve.tensor_tensor(px[:, :, :, :], g_x.unsqueeze(1).to_broadcast([P, heads, feats, CW]),
                                                  p.unsqueeze(2).to_broadcast([P, heads, feats, CW]), ALU.mult))
                        if not first:
                            dve.wait_ge(stored[b], 16 * turn)
                        for h in range(heads):
                            for f in range(feats):
                                c = h * feats + f
                                dve.tensor_tensor_scan(acc[b][:, :, c], ex_out[:, 0, h, :], px[:, h, f, :],
                                                       acc[1 - b][:, CW - 1, c:c + 1], ALU.mult, ALU.add)
                            c = heads * feats + h
                            dve.tensor_tensor_scan(acc[b][:, :, c], ex_out[:, 0, h, :], p[:, h, :],
                                                   acc[1 - b][:, CW - 1, c:c + 1], ALU.mult, ALU.add)
                        dve.tensor_copy(acc[b][:, :, w:full], top[b][:, :, 1:CW + 1].rearrange("p h t -> p t h")
                                        ).then_inc(done, 1)
                        dve.wait_ge(done, i + 1)

                    run_turns(dve, NCH, body)
                    dve.tensor_copy(last_rows[:, :], acc[0][:, CW - 1, :])
                    extra.vector_end(dve)

                @block.scalar
                def _(act):
                    def body(i, b, turn, first):
                        extra.scalar(act, i, b, turn, first)
                        act.wait_ge(asked, i + 1)
                        act.activation(ex_out[:, :, :, :], ex_in[:, :, :, :], ACT.Exp).then_inc(said, 1)
                        act.wait_ge(done, i + 1)
                        act.dma_start(sums_v[:, bass.ds(i * CW, CW), :], acc[b][:, :, :]).then_inc(stored[b], 16)
                    run_turns(act, NCH, body)
                    act.wait_ge(stored[0], 16 * ((NCH + 1) // 2))
                    act.wait_ge(stored[1], 16 * (NCH // 2))
                    extra.scalar_end(act)

                @block.tensor
                def _(pe):
                    extra.tensor_start(pe)
                    run_turns(pe, NCH, lambda i, b, turn, first: extra.tensor(pe, i, b, turn, first))

        class CountSources:

            def allocate(self, ctx):
                self.hist = Histogram("hist_s", src_v, ctx)

            def sync(self, sp, i, b, turn, first):
                self.hist.load(sp, i, b, first)

            def sync_end(self, sp):
                pass

            def vector_start(self, dve):
                self.hist.dve_start(dve)

            def vector(self, dve, i, b, turn, first):
                self.hist.dve(dve, i, b, turn, first)

            def vector_end(self, dve):
                self.hist.finish(dve)

            def scalar(self, act, i, b, turn, first):
                pass

            def scalar_end(self, act):
                pass

            def tensor_start(self, pe):
                self.hist.pe_start(pe)

            def tensor(self, pe, i, b, turn, first):
                self.hist.pe(pe, i, b, turn, first)

        class PlaceBySource:

            def allocate(self, ctx):
                ps = lambda n: ctx.enter_context(nc.psum_tensor(n, [P, 512], F32))
                self.hots = OneHots("place", ctx)
                self.loaded = [sem(f"place_loaded{b}") for b in range(2)]
                self.next_ps = ps("place_next_ps")
                self.turn_ps = [ctx.enter_context(nc.psum_tensor(f"place_turn_ps{q}", [P, 1024], BF16)) for q in range(2)]
                self.same_ps = [ps(f"place_same_ps{q}") for q in range(2)]
                self.look_ps = [ps(f"place_look_ps{q}") for q in range(2)]
                self.hot_at = [sb(f"place_hot_at{q}", [NP, 4, P], F32, ctx) for q in range(2)]
                self.nexts = [sb(f"place_nexts{q}", [NP, NK], F32, ctx) for q in range(2)]
                self.same = [sb(f"place_same{q}", [P, 4, P], BF16, ctx) for q in range(2)]
                self.tmp = sb("place_tmp", [P, 4, NK], F32, ctx)
                self.place = [sb(f"place_place{b}", [P, CW], F32, ctx) for b in range(2)]
                self.place_i = [sb(f"place_place_i{b}", [P, CW], I32, ctx) for b in range(2)]
                self.groups = [list(range(t, min(t + 4, CW))) for t in range(0, CW, 4)]
                self.stored = [sem(f"place_stored{b}") for b in range(2)]
                (self.steps, self.ready, self.turned, self.flat, self.matched, self.masked, self.looked, self.summed,
                 self.counted, self.copied, self.placed, self.mul_steps, self.used) = (
                    sem(f"place_{n}") for n in
                    ("steps", "ready", "turned", "flat", "matched", "masked", "looked", "summed", "counted", "copied",
                     "placed", "mul_steps", "used"))

            def sync(self, sp, i, b, turn, first):
                if not first:
                    sp.wait_ge(self.ready, i - 1)
                sp.dma_start(self.hots.key[b][:, :], src_v[:, bass.ds(i * CW, CW)]).then_inc(self.loaded[b], 16)

            def sync_end(self, sp):
                pass

            def vector_start(self, dve):
                self.chain = Chain(dve, self.steps)

            def vector(self, dve, i, b, turn, first):
                G, ch = len(self.groups), self.chain
                ch.begin(i)
                dve.wait_ge(self.loaded[b], 16 * turn + 16)
                if not first:
                    dve.wait_ge(self.counted, CW * (i - 1) + 1)
                self.hots.make(ch, dve, b, self.ready)
                dve.wait_ge(self.ready, i + 1)
                if not first:
                    dve.wait_ge(self.stored[b], 16 * turn)
                for g, ts in enumerate(self.groups):
                    q, n = (b * G + g) % 2, len(ts)
                    dve.wait_ge(self.matched, i * G + g + 1)
                    dve.tensor_tensor(self.same[q][:, 0:n, :], self.same_ps[q][:, 0:n * P].rearrange("p (t e) -> p t e", e=P),
                                      before[:, :].unsqueeze(1).to_broadcast([P, n, P]), ALU.mult).then_inc(self.masked, 1)
                    if g:
                        self.take(dve, ch, i, b, g - 1)
                self.take(dve, ch, i, b, G - 1)
                dve.tensor_copy(self.place_i[b][:, :], self.place[b][:, :]).then_inc(self.placed, 1)

            def take(self, dve, ch, i, b, g):
                G, ts = len(self.groups), self.groups[g]
                q, n = (b * G + g) % 2, len(ts)
                dve.wait_ge(self.looked, i * G + g + 1)
                ch.link(dve.tensor_tensor(self.tmp[:, 0:n, :], self.look_ps[q][:, 0:n * NK].rearrange("p (t k) -> p t k", k=NK),
                                          self.hots.hot_k[b][:, ts[0]:ts[0] + n, :], ALU.mult))
                dve.tensor_reduce(self.place[b][:, ts[0]:ts[0] + n], self.tmp[:, 0:n, :], AX_X, ALU.add).then_inc(self.summed, 1)
                dve.wait_ge(self.summed, i * G + g + 1)

            def vector_end(self, dve):
                pass

            def flatten(self, act, i, b, g):
                G, n = len(self.groups), len(self.groups[g])
                q = (b * G + g) % 2
                act.wait_ge(self.turned, i * G + g + 1)
                if g > 1:
                    act.wait_ge(self.looked, i * G + g - 1)
                act.copy(self.hot_at[q][:, 0:n, :], self.turn_ps[q][0:NP, 0:n * P].rearrange("a (t e) -> a t e", e=P)
                         ).then_inc(self.flat, 1)

            def scalar(self, act, i, b, turn, first):
                G = len(self.groups)
                self.flatten(act, i, b, 0)
                for g, ts in enumerate(self.groups):
                    if g + 1 < G:
                        self.flatten(act, i, b, g + 1)
                    for t in ts:
                        act.wait_ge(self.counted, i * CW + t + 1)
                        act.copy(self.nexts[(b * CW + t) % 2][:, :], self.next_ps[0:NP, 0:NK]).then_inc(self.copied, 1)
                act.wait_ge(self.placed, i + 1)
                act.dma_start(pos_rows[:, bass.ds(i * CW, CW)], self.place_i[b][:, :]).then_inc(self.stored[b], 16)

            def scalar_end(self, act):
                act.wait_ge(self.stored[0], 16 * ((NCH + 1) // 2))
                act.wait_ge(self.stored[1], 16 * (NCH // 2))

            def tensor_start(self, pe):
                pe.matmul(self.next_ps[0:NP, 0:NK], ident[0:NP, 0:NP], order["s"]["start"][:, :], start=True, stop=False,
                          skip_group_check=True).then_inc(self.counted, 1)

            def tensor(self, pe, i, b, turn, first):
                G = len(self.groups)
                hot_a, hot_k = self.hots.hot_a[b], self.hots.hot_k[b]

                def match(g):
                    q, ts = (b * G + g) % 2, self.groups[g]
                    for n, t in enumerate(ts):
                        last = pe.transpose(self.turn_ps[q][0:NP, n * P:(n + 1) * P], hot_a[:, t, :], ident_b[:, :])
                    last.then_inc(self.turned, 1)
                    pe.wait_ge(self.flat, i * G + g + 1)
                    if not (first and b == 0 and g < 2):
                        pe.wait_ge(self.masked, i * G + g - 1)
                    for n, t in enumerate(ts):
                        last = pe.matmul(self.same_ps[q][:, n * P:(n + 1) * P], self.hot_at[q][:, n, :],
                                         self.hot_at[q][:, n, :], start=True, stop=True)
                    last.then_inc(self.matched, 1)

                pe.wait_ge(self.ready, i + 1)
                match(0)
                for g, ts in enumerate(self.groups):
                    if g + 1 < G:
                        match(g + 1)
                    q = (b * G + g) % 2
                    pe.wait_ge(self.masked, i * G + g + 1)
                    if not (first and b == 0 and g < 2):
                        pe.wait_ge(self.summed, i * G + g - 1)
                    for n, t in enumerate(ts):
                        pe.wait_ge(self.copied, i * CW + t + 1)
                        pe.matmul(self.look_ps[q][:, n * NK:(n + 1) * NK], self.hot_at[q][:, n, :],
                                  self.nexts[(b * CW + t) % 2][:, :], start=True, stop=False, skip_group_check=True)
                        last = pe.matmul(self.look_ps[q][:, n * NK:(n + 1) * NK], self.same[q][:, n, :], hot_k[:, t, :],
                                         start=False, stop=True, skip_group_check=True)
                        if n == len(ts) - 1:
                            last.then_inc(self.looked, 1)
                        pe.matmul(self.next_ps[0:NP, 0:NK], hot_a[:, t, :], hot_k[:, t, :], start=False, stop=False,
                                  skip_group_check=True).then_inc(self.counted, 1)

        def messages(name, attr, fills, outer_of, weights, finish, exp_scale=None):
            de = attr.shape[1]
            lots = len(weights)
            attr_v, ex_v = edges(attr), edges(ex32)
            groups = [list(range(t, min(t + 4, CW))) for t in range(0, CW, 4)]
            G = len(groups)
            with ExitStack() as ctx:
                att = [sb(f"{name}_att{b}", [P, CW, de], F32, ctx) for b in range(2)]
                ex = [sb(f"{name}_ex{b}", [P, CW, EXW], F32, ctx) for b in range(2)]
                pos = [sb(f"{name}_pos{b}", [P, CW], I32, ctx) for b in range(2)]
                own = [sb(f"{name}_own{b}", [P, fills, CW], F32, ctx) for b in range(2)]
                outer = [sb(f"{name}_outer{b}", [P, CW, lots * P], F32, ctx) for b in range(2)]
                flip = [[sb(f"{name}_flip{q}{n}", [P, 4 * P], F32, ctx) for n in range(lots)] for q in range(2)]
                msg = [sb(f"{name}_msg{b}", [P, CW, D], F32, ctx) for b in range(2)]
                work = sb(f"{name}_work", [P, CW, D], F32, ctx)
                first_row = sb(f"{name}_first", [P, EXW], F32, ctx)
                flip_ps = [[ctx.enter_context(nc.psum_tensor(f"{name}_fps{q}{n}", [P, 512], F32)) for n in range(lots)]
                           for q in range(2)]
                msg_ps = [ctx.enter_context(nc.psum_tensor(f"{name}_mps{b}", [P, 512], F32)) for b in range(2)]
                att_in, ex_in, pos_in, scattered = ([sem(f"{name}_{n}{b}") for b in range(2)]
                                                    for n in ("att_in", "ex_in", "pos_in", "scattered"))
                spread_, outered, turned, copied, multiplied, done, asked, said, admitted, let_in, first_got, steps, start_steps = (
                    sem(f"{name}_{n}") for n in
                    ("spread", "outered", "turned", "copied", "multiplied", "done", "asked", "said", "admitted", "let_in",
                     "first_got", "steps", "start_steps"))
                block = ctx.enter_context(nc.Block())

                @block.sync
                def _(sp):
                    def body(i, b, turn, first):
                        if not first:
                            sp.wait_ge(outered, i - 1)
                        sp.dma_start(att[b][:, :, :], attr_v[:, bass.ds(i * CW, CW), :]).then_inc(att_in[b], 16)
                        sp.dma_start(ex[b][:, :, :], ex_v[:, bass.ds(i * CW, CW), :]).then_inc(ex_in[b], 16)
                        if not first:
                            sp.wait_ge(scattered[b], 16 * CW * turn)
                            sp.sem_inc(let_in, 1)
                        sp.dma_start(pos[b][:, :], pos_rows[:, bass.ds(i * CW, CW)]).then_inc(pos_in[b], 16)
                    run_turns(sp, NCH, body)

                @block.gpsimd
                def _(pool):
                    pool.indirect_dma_start(first_row[:, :], None, ex32,
                                            bass.IndirectOffsetOnAxis(order["d"]["begins"][:, 0:1], 0)).then_inc(first_got, 16)

                    def body(i, b, turn, first):
                        pool.wait_ge(pos_in[b], 16 * turn + 16)
                        pool.wait_ge(done, i + 1)
                        pool.sem_inc(admitted, 1)
                        for j in range(CW):
                            pool.indirect_dma_start(msgs, bass.IndirectOffsetOnAxis(pos[b][:, j:j + 1], 0),
                                                    msg[b][:, j, :], None).then_inc(scattered[b], 16)
                    run_turns(pool, NCH, body)
                    pool.wait_ge(scattered[0], 16 * CW * ((NCH + 1) // 2))
                    pool.wait_ge(scattered[1], 16 * CW * (NCH // 2))

                @block.vector
                def _(dve):
                    start, ch = Chain(dve, start_steps), Chain(dve, steps)
                    dve.wait_ge(first_got, 16)
                    start.link(dve.tensor_copy(own[1][:, :, CW - 1], first_row[:, 0:fills]))

                    def post(i, b, turn, first):
                        ch.begin(i)
                        if not (first and b == 0):
                            dve.wait_ge(done, i)
                        dve.wait_ge(multiplied, G * (i + 1))
                        if not first:
                            dve.wait_ge(scattered[b], 16 * CW * turn)
                        finish(dve, ch, i, msg[b], msg_ps[b][:, 0:CW * D].rearrange("p (t f) -> p t f", f=D), work,
                               own[b], said).then_inc(done, 1)

                    def body(i, b, turn, first):
                        if not first:
                            dve.wait_ge(done, i - 1)
                        dve.wait_ge(att_in[b], 16 * turn + 16)
                        dve.wait_ge(ex_in[b], 16 * turn + 16)
                        kp = keep["d"][:, bass.ds(i * CW, CW)]
                        for f in range(fills):
                            last = dve.tensor_tensor_scan(own[b][:, f, :], kp, ex[b][:, :, f], own[1 - b][:, f, CW - 1:CW],
                                                          ALU.mult, ALU.add)
                        last.then_inc(spread_, 1)
                        dve.wait_ge(spread_, i + 1)
                        if not first:
                            dve.wait_ge(turned, G * (i - 1))
                        mine = own[b][:, 0:D, :].rearrange("p f t -> p t f")
                        left, right = outer_of(att[b][:, :, :], mine)
                        la, ra = left.shape[2], right.shape[2]
                        dve.tensor_tensor(outer[b][:, :, :].rearrange("p t (l r) -> p t l r", r=ra),
                                          left.unsqueeze(3).to_broadcast([P, CW, la, ra]),
                                          right.unsqueeze(2).to_broadcast([P, CW, la, ra]), ALU.mult).then_inc(outered, 1)
                    run_turns_late(dve, NCH, body, post)

                @block.tensor
                def _(pe):
                    def turn_group(i, b, g, first):
                        q = (b * G + g) % 2
                        if not (first and b == 0 and g < 2):
                            pe.wait_ge(copied, i * G + g - 1)
                        for n in range(lots):
                            for k, t in enumerate(groups[g]):
                                last = pe.transpose(flip_ps[q][n][:, k * P:(k + 1) * P], outer[b][:, t, n * P:(n + 1) * P],
                                                    ident[:, :])
                        last.then_inc(turned, 1)

                    def body(i, b, turn, first):
                        pe.wait_ge(outered, i + 1)
                        if not first:
                            pe.wait_ge(done, i - 1)
                        turn_group(i, b, 0, first)
                        for g, ts in enumerate(groups):
                            if g + 1 < G:
                                turn_group(i, b, g + 1, first)
                            pe.wait_ge(copied, i * G + g + 1)
                            q = (b * G + g) % 2
                            for k, t in enumerate(ts):
                                for n in range(lots):
                                    last = pe.matmul(msg_ps[b][:, t * D:(t + 1) * D], flip[q][n][:, k * P:(k + 1) * P],
                                                     weights[n], start=(n == 0), stop=(n == lots - 1),
                                                     skip_group_check=True)
                            last.then_inc(multiplied, 1)
                    run_turns(pe, NCH, body)

                @block.scalar
                def _(act):
                    def body(i, b, turn, first):
                        for g, ts in enumerate(groups):
                            q = (b * G + g) % 2
                            act.wait_ge(turned, i * G + g + 1)
                            if not (first and b == 0 and g < 2):
                                act.wait_ge(multiplied, i * G + g - 1)
                            for n in range(lots):
                                last = act.copy(flip[q][n][:, 0:len(ts) * P], flip_ps[q][n][:, 0:len(ts) * P])
                            last.then_inc(copied, 1)

                    def exponential(i, b, turn, first):
                        act.wait_ge(multiplied, G * (i + 1))
                        if not first:
                            act.wait_ge(scattered[b], 16 * CW * turn)
                        act.activation(msg[b][:, :, :].rearrange("p t f -> p (t f)"), msg_ps[b][:, 0:CW * D], ACT.Exp,
                                       scale=exp_scale).then_inc(said, 1)

                    if exp_scale is None:
                        run_turns(act, NCH, body)
                    else:
                        run_turns_late(act, NCH, body, exponential)

        def sum_by_source(name, last_rows):
            msg_v, out_v = edges(msgs), edges(src_sums)
            with ExitStack() as ctx:
                m = [sb(f"{name}_m{b}", [P, CT, D], F32, ctx) for b in range(2)]
                acc = [sb(f"{name}_acc{b}", [P, CT, D], F32, ctx) for b in range(2)]
                loaded, stored = ([sem(f"{name}_{n}{b}") for b in range(2)] for n in ("loaded", "stored"))
                summed, cleared = sem(f"{name}_summed"), sem(f"{name}_cleared")
                block = ctx.enter_context(nc.Block())

                @block.sync
                def _(sp):
                    def body(i, b, turn, first):
                        if not first:
                            sp.wait_ge(summed, i - 1)
                        sp.dma_start(m[b][:, :, :], msg_v[:, bass.ds(i * CT, CT), :]).then_inc(loaded[b], 16)
                    run_turns(sp, NCT, body)

                @block.vector
                def _(dve):
                    dve.memset(acc[1][:, CT - 1, :], 0.0).then_inc(cleared, 1)
                    dve.wait_ge(cleared, 1)

                    def body(i, b, turn, first):
                        dve.wait_ge(loaded[b], 16 * turn + 16)
                        if not first:
                            dve.wait_ge(stored[b], 16 * turn)
                        for f in range(D):
                            last = dve.tensor_tensor_scan(acc[b][:, :, f], keep["s"][:, bass.ds(i * CT, CT)], m[b][:, :, f],
                                                          acc[1 - b][:, CT - 1, f:f + 1], ALU.mult, ALU.add)
                        last.then_inc(summed, 1)
                        dve.wait_ge(summed, i + 1)
                    run_turns(dve, NCT, body)
                    dve.tensor_copy(last_rows[:, :], acc[(NCT - 1) % 2][:, CT - 1, :])

                @block.scalar
                def _(act):
                    def body(i, b, turn, first):
                        act.wait_ge(summed, i + 1)
                        act.dma_start(out_v[:, bass.ds(i * CT, CT), :], acc[b][:, :, :]).then_inc(stored[b], 16)
                    run_turns(act, NCT, body)
                    act.wait_ge(stored[0], 16 * ((NCT + 1) // 2))
                    act.wait_ge(stored[1], 16 * (NCT // 2))

        def sheaf(w1_pair, b1_pair, w2_pair, b2_pair, last_rows):
            name = "sheaf"
            groups = [list(range(t, min(t + 4, CW))) for t in range(0, CW, 4)]
            G = len(groups)
            tw = 20
            ex_v, out_v = edges(ex32), edges(dst_sums)
            with ExitStack() as ctx:
                two = lambda n, shape, dt=F32: [sb(f"{name}_{n}{b}", shape, dt, ctx) for b in range(2)]
                idx, pos = two("idx", [P, CW], I32), two("pos", [P, CW], I32)
                got, ex = two("got", [P, CW, tw]), two("ex", [P, CW, EXW])
                cat = two("cat", [P, CW, 2, D])
                own = two("own", [P, CW])
                cat_t, hid = two("cat_t", [2 * D, 4 * P]), two("hid", [P, 4 * P])
                msg, dmsg, dacc = two("msg", [P, CW, D]), sb(f"{name}_dmsg", [P, CW, D], F32, ctx), two("dacc", [P, CW, D])
                v, y, t1 = (sb(f"{name}_{n}", [P, CW, 2, D], F32, ctx) for n in ("v", "y", "t1"))
                q2, dot = (sb(f"{name}_{n}", [P, CW, 2], F32, ctx) for n in ("q2", "dot"))
                first_row = sb(f"{name}_first", [P, EXW], F32, ctx)
                ps = lambda n, w: ctx.enter_context(nc.psum_tensor(f"{name}_{n}", [P, w], F32))
                cat_ps, hid_ps, v_ps = [ps(f"cps{q}", 512) for q in range(2)], [ps(f"hps{q}", 512) for q in range(2)], [
                    ps(f"vps{b}", 1024) for b in range(2)]
                idx_in, pos_in, ex_in, gathered, scattered, stored = ([sem(f"{name}_{n}{b}") for b in range(2)] for n in
                    ("idx_in", "pos_in", "ex_in", "gathered", "scattered", "stored"))
                (spread_, paired, turned, copied, hidden, rectified, reflected, sent, summed, admitted, let_in, first_got,
                 steps, start_steps, taken) = (
                    sem(f"{name}_{n}") for n in
                    ("spread", "paired", "turned", "copied", "hidden", "rectified", "reflected", "sent", "summed",
                     "admitted", "let_in", "first_got", "steps", "start_steps", "taken"))
                block = ctx.enter_context(nc.Block())

                @block.sync
                def _(sp):
                    def body(i, b, turn, first):
                        if not first:
                            sp.wait_ge(gathered[b], 16 * CW * turn)
                            sp.wait_ge(paired, i - 1)
                        sp.dma_start(idx[b][:, :], src_v[:, bass.ds(i * CW, CW)]).then_inc(idx_in[b], 16)
                        sp.dma_start(ex[b][:, :, :], ex_v[:, bass.ds(i * CW, CW), :]).then_inc(ex_in[b], 16)
                        if not first:
                            sp.wait_ge(scattered[b], 16 * CW * turn)
                            sp.sem_inc(let_in, 1)
                        sp.dma_start(pos[b][:, :], pos_rows[:, bass.ds(i * CW, CW)]).then_inc(pos_in[b], 16)
                    run_turns(sp, NCH, body)

                @block.gpsimd
                def _(pool):
                    pool.indirect_dma_start(first_row[:, :], None, ex32,
                                            bass.IndirectOffsetOnAxis(order["d"]["begins"][:, 0:1], 0)).then_inc(first_got, 16)

                    def gather(i, b, turn, first):
                        pool.wait_ge(idx_in[b], 16 * turn + 16)
                        if not first:
                            pool.wait_ge(sent, i - 1)
                        pool.sem_inc(admitted, 1)
                        for j in range(CW):
                            pool.indirect_dma_start(got[b][:, j, :], None, table3,
                                                    bass.IndirectOffsetOnAxis(idx[b][:, j:j + 1], 0)).then_inc(gathered[b], 16)

                    def scatter(i, b, turn, first):
                        pool.wait_ge(pos_in[b], 16 * turn + 16)
                        pool.wait_ge(sent, i + 1)
                        pool.sem_inc(admitted, 1)
                        for j in range(CW):
                            pool.indirect_dma_start(msgs, bass.IndirectOffsetOnAxis(pos[b][:, j:j + 1], 0),
                                                    msg[b][:, j, :], None).then_inc(scattered[b], 16)
                    run_turns_late(pool, NCH, gather, scatter)
                    pool.wait_ge(scattered[0], 16 * CW * ((NCH + 1) // 2))
                    pool.wait_ge(scattered[1], 16 * CW * (NCH // 2))

                @block.vector
                def _(dve):
                    start, ch = Chain(dve, start_steps), Chain(dve, steps)
                    dve.wait_ge(first_got, 16)
                    start.add(dve.tensor_copy(cat[1][:, CW - 1, 1, :], first_row[:, 0:D]))
                    start.add(dve.memset(dacc[1][:, CW - 1, :], 0.0))
                    start.link(dve.tensor_copy(own[1][:, CW - 1:CW], first_row[:, D:D + 1]))

                    def pre(i, b, turn, first):
                        kp = keep["d"][:, bass.ds(i * CW, CW)]
                        dve.wait_ge(ex_in[b], 16 * turn + 16)
                        if not first:
                            dve.wait_ge(turned, G * (i - 1))
                        for f in range(D):
                            dve.tensor_tensor_scan(cat[b][:, :, 1, f], kp, ex[b][:, :, f], cat[1 - b][:, CW - 1, 1, f:f + 1],
                                                   ALU.mult, ALU.add)
                        dve.tensor_tensor_scan(own[b][:, :], kp, ex[b][:, :, D], own[1 - b][:, CW - 1:CW],
                                               ALU.mult, ALU.add).then_inc(spread_, 1)
                        dve.wait_ge(gathered[b], 16 * CW * (turn + 1))
                        dve.tensor_copy(cat[b][:, :, 0, :], got[b][:, :, 0:D]).then_inc(paired, 1)
                        dve.wait_ge(spread_, i + 1)

                    def apply(i, source, target, swapped):
                        ch.link(dve.tensor_tensor(t1[:, :, :, :], v[:, :, :, :], source[:, :, :, :], ALU.mult))
                        ch.link(dve.tensor_reduce(dot[:, :, :], t1[:, :, :, :], AX_X, ALU.add))
                        ch.link(dve.tensor_tensor(dot[:, :, :], dot[:, :, :], q2[:, :, :], ALU.mult))
                        ch.link(dve.tensor_tensor(t1[:, :, :, :], v[:, :, :, :], dot[:, :, :].unsqueeze(3).to_broadcast([P, CW, 2, D]),
                                                  ALU.mult))
                        if swapped:
                            for h in range(2):
                                ch.add(dve.tensor_tensor(target[:, :, 1 - h, :], source[:, :, h, :], t1[:, :, h, :], ALU.add))
                            ch.sync()

                    def post(i, b, turn, first):
                        ch.begin(i)
                        dve.wait_ge(reflected, G * (i + 1))
                        vp = v_ps[b][:, 0:CW * 2 * D].rearrange("p (t s f) -> p t (s f)", s=2, f=D)
                        dve.tensor_tensor(v[:, :, :, :].rearrange("p t s f -> p t (s f)"), vp,
                                          b2_pair.unsqueeze(1).to_broadcast([P, CW, 2 * D]), ALU.add).then_inc(taken, 1)
                        dve.wait_ge(taken, i + 1)
                        ch.link(dve.tensor_tensor(t1[:, :, :, :], v[:, :, :, :], v[:, :, :, :], ALU.mult))
                        ch.link(dve.tensor_reduce(q2[:, :, :], t1[:, :, :, :], AX_X, ALU.add))
                        ch.link(dve.tensor_scalar(q2[:, :, :], q2[:, :, :], 1.0e-24, None, ALU.max))
                        ch.link(dve.reciprocal(q2[:, :, :], q2[:, :, :]))
                        ch.link(dve.tensor_scalar(q2[:, :, :], q2[:, :, :], -2.0, None, ALU.mult))
                        apply(i, cat[b], y, True)
                        apply(i, y, None, False)
                        ch.link(dve.tensor_tensor(y[:, :, :, :], y[:, :, :, :], t1[:, :, :, :], ALU.add))
                        ch.link(dve.tensor_tensor(dmsg[:, :, :], y[:, :, 1, :],
                                                  got[b][:, :, D:D + 1].to_broadcast([P, CW, D]), ALU.mult))
                        if not first:
                            dve.wait_ge(scattered[b], 16 * CW * turn)
                            dve.wait_ge(stored[b], 16 * turn)
                        dve.tensor_tensor(msg[b][:, :, :], y[:, :, 0, :], own[b][:, :].unsqueeze(2).to_broadcast([P, CW, D]),
                                          ALU.mult).then_inc(sent, 1)
                        for f in range(D):
                            last = dve.tensor_tensor_scan(dacc[b][:, :, f], keep["d"][:, bass.ds(i * CW, CW)], dmsg[:, :, f],
                                                          dacc[1 - b][:, CW - 1, f:f + 1], ALU.mult, ALU.add)
                        last.then_inc(summed, 1)
                        dve.wait_ge(summed, i + 1)

                    run_turns_late(dve, NCH, pre, post)
                    dve.tensor_copy(last_rows[:, :], dacc[(NCH - 1) % 2][:, CW - 1, :])

                @block.tensor
                def _(pe):
                    def turn_group(i, b, g, first):
                        q = (b * G + g) % 2
                        if not (first and b == 0 and g < 2):
                            pe.wait_ge(copied, i * G + g - 1)
                        for k, t in enumerate(groups[g]):
                            last = pe.transpose(cat_ps[q][0:2 * D, k * P:(k + 1) * P],
                                                cat[b][:, t, :, :].rearrange("p s f -> p (s f)"), ident[:, :])
                        last.then_inc(turned, 1)

                    def body(i, b, turn, first):
                        pe.wait_ge(paired, i + 1)
                        pe.wait_ge(spread_, i + 1)
                        if not first:
                            pe.wait_ge(taken, i - 1)
                        turn_group(i, b, 0, first)
                        for g, ts in enumerate(groups):
                            if g + 1 < G:
                                turn_group(i, b, g + 1, first)
                            q, n = (b * G + g) % 2, len(ts) * P
                            pe.wait_ge(copied, i * G + g + 1)
                            pe.matmul(hid_ps[q][:, 0:n], w1_pair, cat_t[q][:, 0:n], start=True, stop=True).then_inc(hidden, 1)
                            pe.wait_ge(rectified, i * G + g + 1)
                            for k, t in enumerate(ts):
                                last = pe.matmul(v_ps[b][:, t * 2 * D:(t + 1) * 2 * D], hid[q][:, k * P:(k + 1) * P], w2_pair,
                                                 start=True, stop=True, skip_group_check=True)
                            last.then_inc(reflected, 1)
                    run_turns(pe, NCH, body)

                @block.scalar
                def _(act):
                    def copy(i, b, g, first):
                        q, n = (b * G + g) % 2, len(groups[g]) * P
                        act.wait_ge(turned, i * G + g + 1)
                        if not (first and b == 0 and g < 2):
                            act.wait_ge(hidden, i * G + g - 1)
                        act.copy(cat_t[q][:, 0:n], cat_ps[q][0:2 * D, 0:n]).then_inc(copied, 1)

                    def body(i, b, turn, first):
                        copy(i, b, 0, first)
                        for g, ts in enumerate(groups):
                            if g + 1 < G:
                                copy(i, b, g + 1, first)
                            q, n = (b * G + g) % 2, len(ts) * P
                            act.wait_ge(hidden, i * G + g + 1)
                            if not (first and b == 0 and g < 2):
                                act.wait_ge(reflected, i * G + g - 1)
                            act.activation(hid[q][:, 0:n], hid_ps[q][:, 0:n], ACT.Relu, bias=b1_pair).then_inc(rectified, 1)

                    def store(i, b, turn, first):
                        act.wait_ge(summed, i + 1)
                        act.dma_start(out_v[:, bass.ds(i * CW, CW), :], dacc[b][:, :, :]).then_inc(stored[b], 16)
                    run_turns_late(act, NCH, body, store)
                    act.wait_ge(stored[0], 16 * ((NCH + 1) // 2))
                    act.wait_ge(stored[1], 16 * (NCH // 2))

        def selu_of(bias, minus_bias, scaled_bias):
            def function(act, ch, parts, z):
                ch.add(act.activation(parts[0][:, :], z, ACT.Relu, bias=scaled_bias, scale=SELU_SCALE))
                ch.link(act.activation(parts[1][:, :], z, ACT.Relu, bias=minus_bias, scale=-1.0))
                ch.link(act.activation(parts[1][:, :], parts[1][:, :], ACT.Exp, scale=-1.0))
                return act.activation(parts[1][:, :], parts[1][:, :], ACT.Copy, scale=SELU_SCALE * SELU_ALPHA,
                                      bias=-SELU_SCALE * SELU_ALPHA)
            return function

        def layer_norm(name, y, result):
            with ExitStack() as ctx:
                sq = sb(f"{name}_sq", [NP, NK, D], F32, ctx)
                mean, var = sb(f"{name}_mean", [NP, NK], F32, ctx), sb(f"{name}_var", [NP, NK], F32, ctx)
                steps, asked, said = sem(f"{name}_steps"), sem(f"{name}_asked"), sem(f"{name}_said")
                block = ctx.enter_context(nc.Block())
                wide = lambda t: t[:, :].unsqueeze(2).to_broadcast([NP, NK, D])

                @block.vector
                def _(dve):
                    ch = Chain(dve, steps)
                    ch.link(dve.tensor_reduce(mean[:, :], y[:, :, :], AX_X, ALU.add))
                    ch.link(dve.tensor_scalar(mean[:, :], mean[:, :], 1.0 / D, None, ALU.mult))
                    ch.link(dve.tensor_tensor(y[:, :, :], y[:, :, :], wide(mean), ALU.subtract))
                    ch.link(dve.tensor_tensor(sq[:, :, :], y[:, :, :], y[:, :, :], ALU.mult))
                    ch.link(dve.tensor_reduce(var[:, :], sq[:, :, :], AX_X, ALU.add))
                    dve.tensor_scalar(var[:, :], var[:, :], 1.0 / D, 1e-5, ALU.mult, ALU.add).then_inc(asked, 1)
                    dve.wait_ge(said, 1)
                    ch.link(dve.reciprocal(var[:, :], var[:, :]))
                    dve.tensor_tensor(result[:, :, :], y[:, :, :], wide(var), ALU.mult)

                @block.scalar
                def _(act):
                    act.wait_ge(asked, 1)
                    act.activation(var[:, :], var[:, :], ACT.Sqrt).then_inc(said, 1)

        def finish_attention(name, heads, feats, rows, a_src, a_dst, values, result):
            w = heads * feats
            with ExitStack() as ctx:
                e, top, seg_top = (sb(f"{name}_{n}", [NP, NK, heads], F32, ctx) for n in ("e", "top", "seg_top"))
                z = sb(f"{name}_z", [NP, NK, heads], F32, ctx)
                ee = sb(f"{name}_ee", [NP, 2, NK, heads], F32, ctx)
                steps, asked, said = sem(f"{name}_steps"), sem(f"{name}_asked"), sem(f"{name}_said")
                block = ctx.enter_context(nc.Block())
                has = order["d"]["has"]

                @block.vector
                def _(dve):
                    ch = Chain(dve, steps)
                    has_w = has[:, :].unsqueeze(2).to_broadcast([NP, NK, heads])
                    ch.add(dve.tensor_tensor(e[:, :, :], a_src, a_dst, ALU.add))
                    ch.add(dve.tensor_scalar(z[:, :, :], has_w, BIG, -BIG, ALU.mult, ALU.add))
                    ch.link(dve.tensor_tensor(seg_top[:, :, :], rows[:, :, w + heads:w + 2 * heads], has_w, ALU.mult))
                    ch.add(dve.scalar_tensor_tensor(out=e[:, :, :], in0=e[:, :, :], scalar=SLOPE, in1=e[:, :, :],
                                                    op0=ALU.mult, op1=ALU.max))
                    ch.link(dve.tensor_tensor(seg_top[:, :, :], seg_top[:, :, :], z[:, :, :], ALU.add))
                    ch.link(dve.tensor_tensor(top[:, :, :], seg_top[:, :, :], e[:, :, :], ALU.max))
                    ch.add(dve.tensor_tensor(ee[:, 0, :, :], seg_top[:, :, :], top[:, :, :], ALU.subtract))
                    dve.tensor_tensor(ee[:, 1, :, :], e[:, :, :], top[:, :, :], ALU.subtract).then_inc(asked, 1)
                    dve.wait_ge(said, 1)
                    ch.link(dve.tensor_tensor(z[:, :, :], rows[:, :, w:w + heads], ee[:, 0, :, :], ALU.mult))
                    ch.link(dve.tensor_tensor(z[:, :, :], z[:, :, :], ee[:, 1, :, :], ALU.add))
                    ch.link(dve.tensor_scalar(z[:, :, :], z[:, :, :], 1e-16, None, ALU.add))
                    ch.link(dve.reciprocal(z[:, :, :], z[:, :, :]))
                    for n in range(2):
                        ch.add(dve.tensor_tensor(ee[:, n, :, :], ee[:, n, :, :], z[:, :, :], ALU.mult))
                    ch.sync()
                    for h in range(heads):
                        part = result[:, :, h * feats:(h + 1) * feats]
                        ch.link(dve.tensor_tensor(part, values, ee[:, 1, :, h:h + 1].to_broadcast([NP, NK, feats]), ALU.mult))
                        ch.link(dve.tensor_tensor(rows[:, :, h * feats:(h + 1) * feats], rows[:, :, h * feats:(h + 1) * feats],
                                                  ee[:, 0, :, h:h + 1].to_broadcast([NP, NK, feats]), ALU.mult))
                        ch.link(dve.tensor_tensor(part, part, rows[:, :, h * feats:(h + 1) * feats], ALU.add))

                @block.scalar
                def _(act):
                    act.wait_ge(asked, 1)
                    act.activation(ee[:, :, :, :], ee[:, :, :, :], ACT.Exp).then_inc(said, 1)

        def silu_block(name, z, scale, work):
            steps, asked, said = sem(f"{name}_steps"), sem(f"{name}_asked"), sem(f"{name}_said")
            with nc.Block() as block:
                @block.scalar
                def _(act):
                    act.activation(work, z, ACT.Exp, scale=-scale).then_inc(said, 1)

                @block.vector
                def _(dve):
                    ch = Chain(dve, steps)
                    dve.wait_ge(said, 1)
                    ch.link(dve.tensor_scalar(work, work, 1.0, None, ALU.add))
                    ch.link(dve.reciprocal(work, work))
                    dve.scalar_tensor_tensor(out=z, in0=z, scalar=scale, in1=work, op0=ALU.mult, op1=ALU.mult)

        setup()
        count_destinations()
        find_segments("d")

        with ExitStack() as ctx:
            last1 = sb("last1", [P, W1R], F32, ctx)
            att1 = sb("att1", [NP, NK, 2 * H1], F32, ctx)
            w1_blocks = sb("w1_blocks", [H1 * D, HC1], F32, ctx)
            b1c = sb("b1c", [HC1, 3], F32, ctx)
            w2_ext = sb("w2_ext", [HC1, C2 + 2], F32, ctx)
            t2 = sb("t2", [NP, NK, 36], F32, ctx)
            with ExitStack() as c2:
                w1_sb, a1 = sb("w1_sb", [D, HC1], F32, c2), sb("a1", [D, 2, HC1], F32, c2)
                a2 = sb("a2", [HC1, 2, C2], F32, c2)
                att_w, prod1, prod2 = sb("att_w", [D, 2, H1], F32, c2), sb("prod1", [D, 2, HC1], F32, c2), sb(
                    "prod2", [HC1, 2, C2], F32, c2)
                on_vector("clear_w1", lambda dve, ch: ch.add(dve.memset(w1_blocks[:, :], 0.0)))
                load_all("weights1", [(w1_sb[:, :], L0_gnn_W1), (w2_ext[:, 0:C2], L0_gnn_W2),
                                      (a1[:, 0, :], spread(L0_gnn_a_src1.rearrange("h c -> (h c)"), D, HC1)),
                                      (a1[:, 1, :], spread(L0_gnn_a_dst1.rearrange("h c -> (h c)"), D, HC1)),
                                      (a2[:, 0, :], spread(L0_gnn_a_src2.rearrange("h c -> (h c)"), HC1, C2)),
                                      (a2[:, 1, :], spread(L0_gnn_a_dst2.rearrange("h c -> (h c)"), HC1, C2)),
                                      (b1c[:, 0:1], L0_gnn_b1.unsqueeze(1))]
                         + [(w1_blocks[h * D:(h + 1) * D, h * C1:(h + 1) * C1], L0_gnn_W1[:, h * C1:(h + 1) * C1])
                            for h in range(H1)], c2)

                def weights(dve, ch):
                    ch.add(dve.tensor_tensor(prod1[:, :, :], a1[:, :, :], w1_sb[:, :].unsqueeze(1).to_broadcast([D, 2, HC1]),
                                             ALU.mult))
                    ch.add(dve.tensor_tensor(prod2[:, :, :], a2[:, :, :],
                                             w2_ext[:, 0:C2].unsqueeze(1).to_broadcast([HC1, 2, C2]), ALU.mult))
                    ch.add(dve.tensor_scalar(b1c[:, 1:2], b1c[:, 0:1], -1.0, None, ALU.mult))
                    ch.link(dve.tensor_scalar(b1c[:, 2:3], b1c[:, 0:1], SELU_SCALE, None, ALU.mult))
                    ch.add(dve.tensor_reduce(att_w[:, :, :], prod1[:, :, :].rearrange("p s (h c) -> p s h c", h=H1), AX_X, ALU.add))
                    ch.link(dve.tensor_reduce(w2_ext[:, C2:C2 + 2], prod2[:, :, :], AX_X, ALU.add))
                on_vector("weights1_made", weights)
                node_product("att1", [D], whole_groups(x_cur), [att_w[:, :, :].rearrange("p s h -> p (s h)")], 2 * H1, into(att1))
            with ExitStack() as c2:
                t1r, e1r = sb("t1r", [NP, NK, 20], F32, c2), sb("e1r", [NP, NK, 4], F32, c2)

                def rows1(dve, ch):
                    ch.link(dve.memset(t1r[:, :, D + H1:20], 0.0))
                    ch.link(dve.memset(e1r[:, :, H1:4], 0.0))
                    ch.add(dve.tensor_copy(t1r[:, :, 0:D], x_cur[:, :, :]))
                    ch.add(dve.tensor_copy(t1r[:, :, D:D + H1], att1[:, :, 0:H1]))
                    ch.link(dve.tensor_copy(e1r[:, :, 0:H1], att1[:, :, H1:2 * H1]))
                on_vector("rows1", rows1)
                put_rows("put1", table1, t1r, e1r, ex4, 4)
            renew_semaphores()
            attention("gat1", H1, D, table1, 20, gat1_sums, last1, CountSources())
            renew_semaphores()
            find_segments("s")
            join_softmax("join1", H1, D, gat1_sums, last1)
            with ExitStack() as c2:
                seg1, o1 = sb("seg1", [NP, NK, W1R], F32, c2), sb("o1", [NP, NK, H1 * D], F32, c2)
                take_rows("take1", "d", gat1_sums, seg1, W1R)
                finish_attention("fin1", H1, D, seg1, att1[:, :, 0:H1], att1[:, :, H1:2 * H1], x_cur[:, :, :], o1)
                fill2 = into(t2)

                def use2(dve, ch, i, prod):
                    return dve.tensor_scalar(t2[:, bass.ds(i * GK, GK), 0:C2 + 2], prod, 1.0, None, ALU.mult)
                node_product("hidden1", [H1 * D], whole_groups(o1), [w2_ext[:, :]] * 2, C2 + 2, use2,
                             middle=(w1_blocks[:, :], HC1, selu_of(b1c[:, 0:1], b1c[:, 1:2], b1c[:, 2:3])))

            last2 = sb("last2", [P, W2R], F32, ctx)
            wf, b2c = sb("wf", [C2, D], F32, ctx), sb("b2c", [C2, 3], F32, ctx)
            bf_w = sb("bf_w", [NP, D], F32, ctx)
            load_all("weights2", [(wf[:, :], L0_gnn_Wf), (b2c[:, 0:1], L0_gnn_b2.unsqueeze(1)),
                                  (bf_w[:, :], spread(L0_gnn_bf, NP, D))], ctx)
            with ExitStack() as c2:
                e2r = sb("e2r", [NP, NK, 4], F32, c2)

                def rows2(dve, ch):
                    ch.link(dve.memset(t2[:, :, C2 + 2:36], 0.0))
                    ch.link(dve.memset(e2r[:, :, :], 0.0))
                    ch.add(dve.tensor_scalar(b2c[:, 1:2], b2c[:, 0:1], -1.0, None, ALU.mult))
                    ch.add(dve.tensor_scalar(b2c[:, 2:3], b2c[:, 0:1], SELU_SCALE, None, ALU.mult))
                    ch.link(dve.tensor_copy(e2r[:, :, 0:1], t2[:, :, C2 + 1:C2 + 2]))
                on_vector("rows2", rows2)
                put_rows("put2", table2, t2, e2r, ex4, 4)
            renew_semaphores()
            attention("gat2", H2, C2, table2, 36, gat2_sums, last2, PlaceBySource())
            renew_semaphores()
            join_softmax("join2", H2, C2, gat2_sums, last2)
            with ExitStack() as c2:
                seg2, o2 = sb("seg2", [NP, NK, W2R], F32, c2), sb("o2", [NP, NK, C2], F32, c2)
                y0 = sb("y0", [NP, NK, D], F32, c2)
                take_rows("take2", "d", gat2_sums, seg2, W2R)
                finish_attention("fin2", H2, C2, seg2, t2[:, :, C2:C2 + 1], t2[:, :, C2 + 1:C2 + 2], t2[:, :, 0:C2], o2)
                node_product("hidden2", [C2], whole_groups(o2), [wf[:, :]] * 2, D, into(y0),
                             middle=(ident[0:C2, 0:C2], C2, selu_of(b2c[:, 0:1], b2c[:, 1:2], b2c[:, 2:3])))

                def residual0(dve, ch):
                    ch.link(dve.tensor_tensor(y0[:, :, :], y0[:, :, :], bf_w[:, :].unsqueeze(1).to_broadcast([NP, NK, D]), ALU.add))
                    ch.link(dve.tensor_tensor(y0[:, :, :], y0[:, :, :], x_cur[:, :, :], ALU.add))
                on_vector("residual0", residual0)
                layer_norm("norm0", y0, x_cur)

        renew_semaphores()
        norm_msg, norm_upd, norm_lin = (D * DE) ** -0.5, (D * D) ** -0.5, D ** -0.5
        last_s = sb("last_s", [P, D])
        last_d = sb("last_d", [P, D])
        e32 = sb("e32", [NP, NK, EXW])
        with ExitStack() as ctx:
            w_msg = sb("w_msg", [D * DE, D], F32, ctx)
            lin, lin2 = sb("lin", [D, D], F32, ctx), sb("lin2", [D, D], F32, ctx)
            w_upd = [sb(f"w_upd{n}", [P, D], F32, ctx) for n in range(2)]
            upd_v = L1_gnn_W_upd_tp.rearrange("i h k -> (i h) k")
            load_all("weights3", [(w_msg[:, :], L1_gnn_W_msg_tp.rearrange("i j h -> (i j) h")), (lin[:, :], L1_gnn_W_msg_lin),
                                  (lin2[:, :], L1_gnn_W_upd_lin)]
                     + [(w_upd[n][:, :], upd_v[n * P:(n + 1) * P, :]) for n in range(2)], ctx)

            def rows3(dve, ch):
                ch.link(dve.memset(e32[:, :, :], 0.0))
                ch.link(dve.tensor_copy(e32[:, :, 0:D], x_cur[:, :, :]))
            on_vector("rows3", rows3)
            put_rows("put3", None, None, e32, ex32, EXW)

            def outer_nodes_edges(att, mine):
                return mine, att

            def finish1(dve, ch, i, msg, prod, work, own, said):
                dve.wait_ge(said, i + 1)
                ch.link(dve.tensor_scalar(work[:, :, :], msg[:, :, :], 1.0, None, ALU.add))
                ch.link(dve.reciprocal(work[:, :, :], work[:, :, :]))
                return dve.scalar_tensor_tensor(out=msg[:, :, :].rearrange("p t f -> p (t f)"),
                                                in0=prod.rearrange("p t f -> p (t f)"), scalar=norm_msg,
                                                in1=work[:, :, :].rearrange("p t f -> p (t f)"), op0=ALU.mult, op1=ALU.mult)
            messages("msg1", edge_attr_8, D, outer_nodes_edges, [w_msg[:, :]], finish1, exp_scale=-norm_msg)
            renew_semaphores()
            sum_by_source("tail1", last_s)
            join_sums("join3", "s", src_sums, D, last_s)
            with ExitStack() as c2:
                seg3 = sb("seg3", [NP, NK, D], F32, c2)
                agg, up = sb("agg", [NP, NK, D], F32, c2), sb("up", [NP, NK, D], F32, c2)
                work3 = sb("work3", [NP, NK, D], F32, c2)
                take_rows("take3", "s", src_sums, seg3, D)
                on_vector("mask3", lambda dve, ch: ch.link(dve.tensor_tensor(
                    seg3[:, :, :], seg3[:, :, :], order["s"]["has"][:, :].unsqueeze(2).to_broadcast([NP, NK, D]), ALU.mult)))
                node_product("agg1", [D], whole_groups(seg3), [lin[:, :]], D, into(agg, norm_lin))

                def fill_outer(dve, ch, i, stage):
                    for k in range(GK):
                        xs = x_cur[:, bass.ds(i * GK + k, 1), :].rearrange("p k f -> p (k f)")
                        gs = agg[:, bass.ds(i * GK + k, 1), :].rearrange("p k f -> p (k f)")
                        last = dve.tensor_tensor(stage[:, k, :].rearrange("p (a b) -> p a b", b=D),
                                                 xs.unsqueeze(2).to_broadcast([NP, D, D]),
                                                 gs.unsqueeze(1).to_broadcast([NP, D, D]), ALU.mult)
                    return last
                node_product("upd1", [P, P], fill_outer, [w[:, :] for w in w_upd], D, into(up))
                silu_block("silu1", up[:, :, :], norm_upd, work3[:, :, :])
                node_product("lin1", [D], whole_groups(up), [lin2[:, :]], D, into(agg, norm_lin))
                on_vector("residual1", lambda dve, ch: ch.link(dve.scalar_tensor_tensor(
                    out=up[:, :, :], in0=x_cur[:, :, :], scalar=2.0, in1=agg[:, :, :], op0=ALU.mult, op1=ALU.add)))
                layer_norm("norm1", up, x_cur)

        renew_semaphores()
        with ExitStack() as ctx:
            w1_pair, w2_pair = sb("w1_pair", [2 * D, 2 * HID], F32, ctx), sb("w2_pair", [2 * HID, 2 * D], F32, ctx)
            b1_pair, b2_pair = sb("b1_pair", [2 * HID, 1], F32, ctx), sb("b2_pair", [P, 2 * D], F32, ctx)
            dinv = sb("dinv", [NP, NK], F32, ctx)
            on_vector("clear_w2", lambda dve, ch: ch.add(dve.memset(w2_pair[:, :], 0.0)))
            w1t, w2t = L2_gnn_W1.rearrange("h f -> f h"), L2_gnn_W2.rearrange("f h -> h f")
            load_all("weights4", [(w1_pair[:, 0:HID], w1t), (w1_pair[0:D, HID:2 * HID], w1t[D:2 * D, :]),
                                  (w1_pair[D:2 * D, HID:2 * HID], w1t[0:D, :]),
                                  (w2_pair[0:HID, 0:D], w2t), (w2_pair[HID:2 * HID, D:2 * D], w2t),
                                  (b1_pair[0:HID, :], L2_gnn_b1.unsqueeze(1)), (b1_pair[HID:2 * HID, :], L2_gnn_b1.unsqueeze(1)),
                                  (b2_pair[:, 0:D], spread(L2_gnn_b2, P, D)), (b2_pair[:, D:2 * D], spread(L2_gnn_b2, P, D))], ctx)
            root_steps, root_asked, root_said = sem("root_steps"), sem("root_asked"), sem("root_said")
            with ExitStack() as c2:
                t3 = sb("t3", [NP, NK, 20], F32, c2)
                with nc.Block() as block:
                    @block.vector
                    def _(dve):
                        ch = Chain(dve, root_steps)
                        dve.tensor_scalar(dinv[:, :], deg[:, :], 1e-5, None, ALU.max).then_inc(root_asked, 1)
                        ch.link(dve.memset(t3[:, :, D + 1:20], 0.0))
                        dve.wait_ge(root_said, 1)
                        ch.link(dve.reciprocal(dinv[:, :], dinv[:, :]))
                        for t in (t3, e32):
                            ch.add(dve.tensor_copy(t[:, :, 0:D], x_cur[:, :, :]))
                            ch.add(dve.tensor_copy(t[:, :, D], dinv[:, :]))

                    @block.scalar
                    def _(act):
                        act.wait_ge(root_asked, 1)
                        act.activation(dinv[:, :], dinv[:, :], ACT.Sqrt).then_inc(root_said, 1)
                put_rows("put4", table3, t3, e32, ex32, EXW)
            renew_semaphores()
            sheaf(w1_pair[:, :], b1_pair[:, :], w2_pair[:, :], b2_pair[:, :], last_d)
            renew_semaphores()
            join_sums("join4", "d", dst_sums, D, last_d)
            sum_by_source("tail2", last_s)
            join_sums("join5", "s", src_sums, D, last_s)
            with ExitStack() as c2:
                seg_s, seg_d = sb("seg_of_s", [NP, NK, D], F32, c2), sb("seg_of_d", [NP, NK, D], F32, c2)
                take_rows("take4", "s", src_sums, seg_s, D)
                take_rows("take5", "d", dst_sums, seg_d, D)

                def residual2(dve, ch):
                    for s_, o in ((seg_s, "s"), (seg_d, "d")):
                        ch.add(dve.tensor_tensor(s_[:, :, :], s_[:, :, :],
                                                 order[o]["has"][:, :].unsqueeze(2).to_broadcast([NP, NK, D]), ALU.mult))
                    ch.sync()
                    ch.link(dve.tensor_tensor(seg_s[:, :, :], seg_s[:, :, :], seg_d[:, :, :], ALU.add))
                    ch.link(dve.tensor_tensor(seg_s[:, :, :], seg_s[:, :, :], dinv[:, :].unsqueeze(2).to_broadcast([NP, NK, D]),
                                              ALU.mult))
                    ch.link(dve.tensor_tensor(seg_s[:, :, :], seg_s[:, :, :], x_cur[:, :, :], ALU.add))
                    ch.link(dve.tensor_scalar(seg_s[:, :, :], seg_s[:, :, :], 0.0, None, ALU.max))
                    ch.link(dve.tensor_tensor(seg_s[:, :, :], seg_s[:, :, :], x_cur[:, :, :], ALU.add))
                on_vector("residual2", residual2)
                layer_norm("norm2", seg_s, x_cur)

        renew_semaphores()
        with ExitStack() as ctx:
            w_edge = [sb(f"w_edge{n}", [P, D], F32, ctx) for n in range(2)]
            bias_m = sb("bias_m", [D, D], F32, ctx)
            kern = L3_gnn_kernel.rearrange("k (i j) -> k j i", i=D)
            half = P // D
            load_all("weights5", [(w_edge[k // half][(k % half) * D:(k % half + 1) * D, :], kern[k]) for k in range(D)]
                     + [(bias_m[:, :], L3_gnn_bias.rearrange("(i j) -> j i", i=D))], ctx)
            node_product("bias", [D], whole_groups(x_cur), [bias_m[:, :]], D, into(x_new))

            def rows5(dve, ch):
                ch.add(dve.tensor_copy(e32[:, :, 0:D], x_cur[:, :, :]))
                ch.link(dve.tensor_copy(e32[:, :, D:2 * D], x_new[:, :, :]))
            on_vector("rows5", rows5)
            put_rows("put5", None, None, e32, ex32, EXW)

            def outer_edges_nodes(att, mine):
                return att, mine

            def finish3(dve, ch, i, msg, prod, work, own, said):
                return dve.tensor_tensor(msg[:, :, :], prod, own[:, D:2 * D, :].rearrange("p f t -> p t f"), ALU.add)
            messages("msg3", edge_attr_16, 2 * D, outer_edges_nodes, [w[:, :] for w in w_edge], finish3)
            renew_semaphores()
            sum_by_source("tail3", last_s)
            join_sums("join6", "s", src_sums, D, last_s)
            with ExitStack() as c2:
                seg6 = sb("seg6", [NP, NK, D], F32, c2)
                take_rows("take6", "s", src_sums, seg6, D)

                def residual3(dve, ch):
                    ch.link(dve.tensor_tensor(seg6[:, :, :], seg6[:, :, :],
                                              order["s"]["has"][:, :].unsqueeze(2).to_broadcast([NP, NK, D]), ALU.mult))
                    ch.link(dve.tensor_tensor(seg6[:, :, :], seg6[:, :, :], x_cur[:, :, :], ALU.add))
                on_vector("residual3", residual3)
                layer_norm("norm3", seg6, x_new)

        written = sem("written")
        with nc.Block() as block:
            @block.sync
            def _(sp):
                sp.dma_start(out[0:FULL * P, :].rearrange("(p k) d -> p k d", k=NK), x_new[0:FULL, :, :]).then_inc(written, 16)
                if REST:
                    sp.dma_start(out[FULL * P:N, :].rearrange("(p k) d -> p k d", k=REST), x_new[FULL:NP, 0:REST, :]
                                 ).then_inc(written, 16)
                sp.wait_ge(written, 32 if REST else 16)


_INS = ['x', 'src', 'dst', 'edge_attr_16', 'edge_attr_8', 'node_vec1',
        'L0_gnn_W1', 'L0_gnn_a_src1', 'L0_gnn_a_dst1', 'L0_gnn_b1', 'L0_gnn_W2', 'L0_gnn_a_src2',
        'L0_gnn_a_dst2', 'L0_gnn_b2', 'L0_gnn_Wf', 'L0_gnn_bf',
        'L1_gnn_W_msg_tp', 'L1_gnn_W_msg_lin', 'L1_gnn_W_upd_tp', 'L1_gnn_W_upd_lin',
        'L2_gnn_W1', 'L2_gnn_b1', 'L2_gnn_W2', 'L2_gnn_b2', 'L3_gnn_kernel', 'L3_gnn_bias']


def kernel(**inputs):
    import numpy as _np
    import concourse.bacc as _bacc
    from concourse import mybir as _mybir
    from concourse.bass_utils import run_bass_kernel_spmd as _run

    nc = _bacc.Bacc("TRN2", target_bir_lowering=False, num_devices=1)
    arrays, args = {}, []
    for name in _INS:
        a = _np.ascontiguousarray(inputs[name])
        arrays[f"in_{name}_dram"] = a
        args.append(nc.dram_tensor(f"in_{name}_dram", a.shape, _mybir.dt.from_np(a.dtype), kind="ExternalInput").ap())
    shape = inputs["x"].shape
    args.append(nc.dram_tensor("out_0_dram", shape, _mybir.dt.float32, kind="ExternalOutput").ap())
    gnn_kernel(nc, *args)
    r = _run(nc, [arrays], core_ids=[0])
    return r.results[0]["out_0_dram"]
```

```python
from contextlib import ExitStack

import concourse.bass as bass
from concourse import mybir

P = 128
CW = 25
CP = 20
CP_1, CP_2, CP_3 = 19, 13, 20
LANES = 4
ALU = mybir.AluOpType
ACT = mybir.ActivationFunctionType
F32 = mybir.dt.float32
BF16 = mybir.dt.bfloat16
I32 = mybir.dt.int32
AX_X = mybir.AxisListType.X
BIG = 1.0e30
FAR = 4194304.0
TOP_EXP = 85.0
SLOPE = 0.2
SELU_SCALE = 1.0507009873554805
SELU_ALPHA = 1.6732632423543772


class Chain:

    def __init__(self, eng, sem):
        self.eng, self.sem, self.base, self.n, self.per = eng, sem, 0, 0, None

    def begin(self, i):
        if self.per is None and self.n:
            self.per = self.n
        assert self.per is None or self.n == self.per
        self.base = 0 if self.per is None else i * self.per
        self.n = 0

    def add(self, ins):
        ins.then_inc(self.sem, 1)
        self.n += 1

    def sync(self):
        self.eng.wait_ge(self.sem, self.base + self.n)

    def link(self, ins):
        self.add(ins)
        self.sync()


def run_turns(eng, total, body):
    body(0, 0, 0, True)
    body(1, 1, 0, True)
    with eng.Fori(1, total // 2) as h:
        body(2 * h, 0, h, False)
        body(2 * h + 1, 1, h, False)
    if total % 2:
        body(total - 1, 0, total // 2, False)


def run_turns_late(eng, total, pre, post):
    pre(0, 0, 0, True)
    pre(1, 1, 0, True)
    post(0, 0, 0, True)
    pre(2, 0, 1, False)
    post(1, 1, 0, True)
    with eng.Fori(1, (total - 1) // 2) as h:
        pre(2 * h + 1, 1, h, False)
        post(2 * h, 0, h, False)
        pre(2 * h + 2, 0, h + 1, False)
        post(2 * h + 1, 1, h, False)
    if total % 2 == 0:
        pre(total - 1, 1, total // 2 - 1, False)
        post(total - 2, 0, total // 2 - 1, False)
    post(total - 1, (total - 1) % 2, (total - 1) // 2, False)


def run_turns_woven(eng, total, weave):
    weave((0, 0, 0, True), None)
    weave((1, 1, 0, True), (0, 0, 0, True))
    weave((2, 0, 1, False), (1, 1, 0, True))
    with eng.Fori(1, (total - 1) // 2) as h:
        weave((2 * h + 1, 1, h, False), (2 * h, 0, h, False))
        weave((2 * h + 2, 0, h + 1, False), (2 * h + 1, 1, h, False))
    assert total % 2
    weave(None, (total - 1, 0, total // 2, False))


def run_turns_ahead(eng, total, pre, post):
    pre(0, 0, 0, True)
    pre(1, 1, 0, True)
    pre(2, 0, 1, False)
    post(0, 0, 0, True)
    pre(3, 1, 1, False)
    post(1, 1, 0, True)
    with eng.Fori(2, total // 2) as h:
        pre(2 * h, 0, h, False)
        post(2 * h - 2, 0, h - 1, False)
        pre(2 * h + 1, 1, h, False)
        post(2 * h - 1, 1, h - 1, False)
    if total % 2:
        pre(total - 1, 0, total // 2, False)
    for i in range(total - 2 - total % 2, total):
        post(i, i % 2, i // 2, False)


def gnn_kernel(nc, x, src, dst, edge_attr_16, edge_attr_8, node_vec1,
               L0_gnn_W1, L0_gnn_a_src1, L0_gnn_a_dst1, L0_gnn_b1, L0_gnn_W2, L0_gnn_a_src2,
               L0_gnn_a_dst2, L0_gnn_b2, L0_gnn_Wf, L0_gnn_bf,
               L1_gnn_W_msg_tp, L1_gnn_W_msg_lin, L1_gnn_W_upd_tp, L1_gnn_W_upd_lin,
               L2_gnn_W1, L2_gnn_b1, L2_gnn_W2, L2_gnn_b2, L3_gnn_kernel, L3_gnn_bias, out):
    N, D = x.shape
    E = src.shape[0]
    C = E // P
    NCH = C // CW
    NCT = NCH // 5
    cols_of = {"d": C, "s": NCH * CP}
    C_S = cols_of["s"]
    CT = C_S // NCT
    NP = (N + P - 1) // P
    NK = P
    FULL = N // P
    REST = N - FULL * P
    NR = NP * NK
    GK = 4
    assert E == P * C and C % CW == 0 and NCH % 5 == 0 and D == 16 and NP <= P
    H1, C1 = L0_gnn_a_src1.shape
    H2, C2 = L0_gnn_a_src2.shape
    HC1 = H1 * C1
    HID = L2_gnn_W1.shape[0]
    DE = edge_attr_8.shape[1]
    EXW = 32

    root = ExitStack()
    in_use = []

    def sem(name):
        in_use.append(nc.alloc_semaphore(name=name))
        return in_use[-1]

    def renew_semaphores():
        nc.all_engine_barrier()
        nc.clear_and_free_semaphores(list(in_use))
        in_use.clear()
        nc.all_engine_barrier()

    def sb(name, shape, dt=F32, ctx=root):
        return ctx.enter_context(nc.sbuf_tensor(name, shape, dt))

    def dram(name, shape, dt=F32):
        return nc.dram_tensor(name, shape, dt, kind="Internal").ap()

    def edges(t):
        return t.rearrange("(p c) w -> p c w", p=P)

    def node_rows(t):
        return t.rearrange("(p k) w -> p k w", k=NK)

    ex4 = dram("ex4", [E, 4])
    ex32 = dram("ex32", [E, EXW])
    marks = {o: dram(f"marks_{o}", [P * cols_of[o], 2]) for o in ("d", "s")}
    W1R = H1 * D + 2 * H1
    W2R = C2 + 2
    gat1_sums = dram("gat1_sums", [E, W1R])
    gat2_sums = dram("gat2_sums", [E, W2R])
    table1 = dram("table1", [NR, 20])
    table2 = dram("table2", [NR, 36])
    table3 = dram("table3", [NR, 20])
    pos_rows = dram("pos_rows", [P, C_S], I32)
    msgs = dram("msgs", [P * C_S, D])
    msgs_2 = dram("msgs_2", [P * C_S, D])
    src_sums = dram("src_sums", [P * C_S, D])
    dst_sums = dram("dst_sums", [E, D])

    src_v = src.rearrange("(p c) -> p c", p=P)
    dst_v = dst.rearrange("(p c) -> p c", p=P)

    with root:
        ident = sb("ident", [P, P])
        ident_b = sb("ident_b", [P, P], BF16)
        earlier = sb("earlier", [P, P])
        iota_b = sb("iota_b", [P, P], BF16)
        x_cur = sb("x_cur", [NP, NK, D])
        first_edge = {o: sb(f"first_edge_{o}", [P, 1]) for o in ("d", "s")}
        last_edge = {o: sb(f"last_edge_{o}", [P, 1]) for o in ("d", "s")}
        keep = {o: sb(f"keep_{o}", [P, cols_of[o]]) for o in ("d", "s")}

        def order_arrays(o):
            return dict(
                has=sb(f"has_{o}", [NP, NK]), start=sb(f"start_{o}", [NP, NK]),
                put=sb(f"put_{o}", [NP, NK], I32), take=sb(f"take_{o}", [NP, NK], I32),
                begins=sb(f"begins_{o}", [P, 1], I32), whole=sb(f"whole_{o}", [P, 1]),
                fix_get=sb(f"fix_get_{o}", [P, 1], I32), fix_put=sb(f"fix_put_{o}", [P, 1], I32))

        order = {o: order_arrays(o) for o in ("d", "s")}
        cnt = sb("cnt", [NP, NK])
        deg = sb("deg", [NP, NK])
        free_place = sb("free_place", [NP, LANES, NK])
        iota_q = sb("iota_q", [P, NR // 8], mybir.dt.int16)
        iota_8 = sb("iota_8", [P, 8], BF16)
        direct_t = sb("direct_t", [P, NR // 8])
        direct = sb("direct", [NP, NK, D])

        def setup(zeros):
            with ExitStack() as ctx:
                it = sb("it", [P, P], I32, ctx)
                ones = sb("ones", [P, P], F32, ctx)
                fe = sb("fe", [P, 4], I32, ctx)
                made, loaded, cleared = sem("made"), sem("loaded"), sem("cleared")
                block = ctx.enter_context(nc.Block())

                @block.gpsimd
                def _(pool):
                    chain = Chain(pool, made)
                    chain.add(pool.memset(ones[:, :], 1.0))
                    chain.add(pool.memset(ident[:, :], 0.0))
                    chain.add(pool.iota(it[:, :], [[1, P]], base=0, channel_multiplier=0))
                    chain.add(pool.iota(iota_q[:, :], [[1, NR // 8]], base=0, channel_multiplier=0,
                                        allow_small_or_imprecise_dtypes=True))
                    for n, o in enumerate(("d", "s")):
                        chain.link(pool.iota(fe[:, 2 * n:2 * n + 1], [[1, 1]], base=0, channel_multiplier=cols_of[o]))
                        chain.link(pool.iota(fe[:, 2 * n + 1:2 * n + 2], [[1, 1]], base=cols_of[o],
                                             channel_multiplier=cols_of[o]))
                    chain.add(pool.affine_select(out=ident[:, :], in_=ident[:, :], compare_op=ALU.not_equal,
                                                 fill=1.0, base=0, pattern=[[-1, P]], channel_multiplier=1))
                    chain.add(pool.affine_select(out=earlier[:, :], in_=ones[:, :], compare_op=ALU.is_gt,
                                                 fill=0.0, base=0, pattern=[[1, P]], channel_multiplier=-1))

                @block.vector
                def _(dve):
                    dve.memset(zeros[:, :], 0.0)
                    dve.memset(x_cur[:, :, :], 0.0).then_inc(cleared, 1)
                    dve.wait_ge(made, 10)
                    dve.tensor_copy(ident_b[:, :], ident[:, :])
                    dve.tensor_copy(iota_b[:, :], it[:, :])
                    dve.tensor_copy(iota_8[:, :], it[:, 0:8])
                    for n, o in enumerate(("d", "s")):
                        dve.tensor_copy(first_edge[o][:, :], fe[:, 2 * n:2 * n + 1])
                        dve.tensor_copy(last_edge[o][:, :], fe[:, 2 * n + 1:2 * n + 2])

                @block.sync
                def _(sp):
                    sp.wait_ge(cleared, 1)
                    sp.dma_start(x_cur[0:FULL, :, :], x[0:FULL * P, :].rearrange("(p k) d -> p k d", k=NK)
                                 ).then_inc(loaded, 16)
                    if REST:
                        sp.dma_start(x_cur[FULL:NP, 0:REST, :],
                                     x[FULL * P:N, :].rearrange("(p k) d -> p k d", k=REST)).then_inc(loaded, 16)
                    sp.wait_ge(loaded, 32 if REST else 16)

        class OneHots:

            def __init__(self, name, cols, ctx):
                self.cols = cols
                self.key = [sb(f"{name}_key{b}", [P, cols], I32, ctx) for b in range(2)]
                self.part = sb(f"{name}_part", [P, 2, cols], I32, ctx)
                self.part_b = sb(f"{name}_part_b", [P, 2, cols], BF16, ctx)
                self.hot_a = [sb(f"{name}_hot_a{b}", [P, cols, NP], BF16, ctx) for b in range(2)]
                self.hot_k = [sb(f"{name}_hot_k{b}", [P, cols, NK], BF16, ctx) for b in range(2)]

            def make(self, chain, dve, b, ready):
                chain.add(dve.tensor_scalar(self.part[:, 0, :], self.key[b][:, :], 7, None,
                                            ALU.logical_shift_right))
                chain.link(dve.tensor_scalar(self.part[:, 1, :], self.key[b][:, :], NK - 1, None,
                                             ALU.bitwise_and))
                chain.link(dve.tensor_copy(self.part_b[:, :, :], self.part[:, :, :]))
                pa, pk = (self.part_b[:, n, :].unsqueeze(2) for n in range(2))
                chain.add(dve.tensor_tensor(self.hot_a[b][:, :, :], iota_b[:, 0:NP].unsqueeze(1).to_broadcast([P, self.cols, NP]),
                                            pa.to_broadcast([P, self.cols, NP]), ALU.is_equal))
                dve.tensor_tensor(self.hot_k[b][:, :, :], iota_b[:, :].unsqueeze(1).to_broadcast([P, self.cols, NK]),
                                  pk.to_broadcast([P, self.cols, NK]), ALU.is_equal).then_inc(ready, 1)

        class Histogram:

            def __init__(self, name, keys, lanes, ctx):
                self.keys = keys
                self.counts = ctx.enter_context(nc.psum_tensor(f"{name}_counts", [P, 2, 512], F32))
                self.lanes = lanes
                self.hots = OneHots(name, CW, ctx)
                self.zero = sb(f"{name}_zero", [P, 512], BF16, ctx)
                self.loaded = [sem(f"{name}_loaded{b}") for b in range(2)]
                self.steps, self.ready, self.counted, self.zero_set, self.end_steps = (
                    sem(f"{name}_{n}") for n in ("steps", "ready", "counted", "zero_set", "end_steps"))

            def load(self, sp, i, b, first):
                if not first:
                    sp.wait_ge(self.ready, i - 1)
                sp.dma_start(self.hots.key[b][:, :], self.keys[:, bass.ds(i * CW, CW)]).then_inc(self.loaded[b], 16)

            def dve_start(self, dve):
                dve.memset(self.zero[:, :], 0.0).then_inc(self.zero_set, 1)
                self.chain = Chain(dve, self.steps)

            def dve(self, dve, i, b, turn, first):
                self.chain.begin(i)
                dve.wait_ge(self.loaded[b], 16 * turn + 16)
                if not first:
                    dve.wait_ge(self.counted, i - 1)
                self.hots.make(self.chain, dve, b, self.ready)

            def pe_start(self, pe):
                pe.wait_ge(self.zero_set, 1)
                for n in range(2):
                    pe.matmul(self.counts[0:NP, n, :], self.zero[:, 0:NP], self.zero[:, :], start=True, stop=False,
                              skip_group_check=True)

            def lane(self, n):
                return self.counts[0:NP, n // LANES, n % LANES * NK:(n % LANES + 1) * NK]

            def pe(self, pe, i, b, turn, first):
                pe.wait_ge(self.ready, i + 1)
                for t in range(CW):
                    lane = 0 if not self.lanes else t % LANES if t < CP else LANES
                    last = pe.matmul(self.lane(lane), self.hots.hot_a[b][:, t, :], self.hots.hot_k[b][:, t, :],
                                     start=False, stop=False, skip_group_check=True)
                last.then_inc(self.counted, 1)

            def finish(self, dve):
                dve.wait_ge(self.counted, NCH)
                ch = Chain(dve, self.end_steps)
                ch.link(dve.tensor_copy(cnt[:, :], self.lane(0)))
                if not self.lanes:
                    ch.link(dve.tensor_copy(deg[:, :], cnt[:, :]))
                    return
                ch.link(dve.memset(free_place[:, 0, :], 0.0))
                for n in range(1, LANES):
                    ch.link(dve.tensor_copy(free_place[:, n, :], cnt[:, :]))
                    ch.link(dve.tensor_tensor(cnt[:, :], cnt[:, :], self.lane(n), ALU.add))
                ch.link(dve.tensor_tensor(deg[:, :], deg[:, :], cnt[:, :], ALU.add))
                ch.link(dve.tensor_tensor(deg[:, :], deg[:, :], self.lane(LANES), ALU.add))

        def count_destinations(zeros):
            with ExitStack() as ctx:
                hist = Histogram("hist_d", dst_v, False, ctx)
                tables, let_in = sem("tables"), sem("let_in")
                block = ctx.enter_context(nc.Block())

                @block.scalar
                def _(act):
                    parts = ((ex32, EXW, C), (ex4, 4, C), (marks["d"], 2, C), (marks["s"], 2, C_S), (msgs, D, C_S),
                             (msgs_2, D, C_S))
                    with act.Fori(0, NCT) as i:
                        act.wait_ge(hist.counted, i * 5 + 1)
                        act.sem_inc(let_in, 1)
                        for t, w, n_cols in parts:
                            flat_t = t.rearrange("(p c) w -> p (c w)", p=P)
                            step = n_cols // NCT * w
                            act.dma_start(flat_t[:, bass.ds(i * step, step)], zeros[:, 0:step]).then_inc(tables, 16)
                    act.wait_ge(tables, 16 * len(parts) * NCT)

                @block.sync
                def _(sp):
                    run_turns(sp, NCH, lambda i, b, turn, first: hist.load(sp, i, b, first))

                @block.vector
                def _(dve):
                    hist.dve_start(dve)
                    run_turns(dve, NCH, lambda i, b, turn, first: hist.dve(dve, i, b, turn, first))
                    hist.finish(dve)

                @block.tensor
                def _(pe):
                    hist.pe_start(pe)
                    run_turns(pe, NCH, lambda i, b, turn, first: hist.pe(pe, i, b, turn, first))

        def find_segments(o):
            g, cols = order[o], cols_of[o]
            with ExitStack() as ctx:
                incl, end = sb(f"incl_{o}", [NP, NK], F32, ctx), sb(f"end_{o}", [NP, NK], F32, ctx)
                tmp, zero = sb(f"tmp_{o}", [NP, NK], F32, ctx), sb(f"zero_{o}", [NP, NK], F32, ctx)
                mark = sb(f"mark_{o}", [NP, NK, 2], F32, ctx)
                mk = sb(f"mk_{o}", [P, cols, 2], F32, ctx)
                top, row, row2 = (sb(f"top_{o}", [P, 2], F32, ctx), sb(f"row_{o}", [2, P], F32, ctx),
                                  sb(f"row2_{o}", [2, P + 1], F32, ctx))
                seg = sb(f"seg_{o}", [P, 2], F32, ctx)
                v = sb(f"v_{o}", [P, 8], F32, ctx)
                zrow = sb(f"zrow_{o}", [2, P], F32, ctx)
                ps = ctx.enter_context(nc.psum_tensor(f"ps_{o}", [P, 512], F32))
                steps, totals, offs, marked, put_done, got, t1, t2 = (
                    sem(f"seg_{n}_{o}") for n in ("steps", "totals", "offs", "marked", "put", "got", "t1", "t2"))
                rowed, backed, shifted, topped = (sem(f"seg_{n}_{o}") for n in ("rowed", "backed", "shifted", "topped"))
                block = ctx.enter_context(nc.Block())

                @block.vector
                def _(dve):
                    ch = Chain(dve, steps)
                    ch.link(dve.memset(zero[:, :], 0.0))
                    dve.tensor_tensor_scan(incl[:, :], cnt[:, :], zero[:, :], 0.0, ALU.add, ALU.add).then_inc(totals, 1)
                    dve.wait_ge(offs, 1)
                    ch.add(dve.tensor_scalar(g["has"][:, :], cnt[:, :], 0.0, None, ALU.is_gt))
                    ch.link(dve.tensor_copy(v[0:NP, 0:1], ps[0:NP, 0:1]))
                    ch.link(dve.tensor_scalar(end[:, :], incl[:, :], v[0:NP, 0:1], None, ALU.add))
                    ch.link(dve.tensor_tensor(g["start"][:, :], end[:, :], cnt[:, :], ALU.subtract))
                    if o == "s":
                        ch.add(dve.tensor_tensor(free_place[:, :, :], free_place[:, :, :],
                                                 g["start"][:, :].unsqueeze(1).to_broadcast([NP, LANES, NK]), ALU.add))
                    ch.add(dve.tensor_scalar(mark[:, :, 0], g["start"][:, :], 1.0, None, ALU.add))
                    ch.add(dve.tensor_copy(mark[:, :, 1], end[:, :]))
                    ch.link(dve.tensor_scalar(tmp[:, :], g["has"][:, :], -FAR, FAR, ALU.mult, ALU.add))
                    ch.link(dve.tensor_tensor(tmp[:, :], tmp[:, :], g["start"][:, :], ALU.add))
                    ch.link(dve.tensor_copy(g["put"][:, :], tmp[:, :]))
                    ch.link(dve.tensor_scalar(tmp[:, :], end[:, :], -1.0, 0.0, ALU.add, ALU.max))
                    dve.tensor_copy(g["take"][:, :], tmp[:, :]).then_inc(marked, 1)
                    dve.wait_ge(got, 16)
                    if o == "d":
                        ch.add(dve.tensor_scalar(fresh[:, :], mk[:, :, 1], 0.0, -BIG, ALU.is_gt, ALU.mult))
                    ch.add(dve.tensor_scalar(keep[o][:, :], mk[:, :, 1], 0.0, None, ALU.is_equal))
                    ch.add(dve.memset(zrow[:, :], 0.0))
                    ch.add(dve.memset(row2[:, 0:1], 0.0))
                    dve.tensor_reduce(top[:, :], mk[:, :, :].rearrange("p c w -> p w c"), AX_X, ALU.max).then_inc(topped, 1)
                    dve.wait_ge(rowed, 1)
                    ch.link(dve.tensor_copy(row[:, :], ps[0:2, 128:256]))
                    dve.tensor_tensor_scan(row2[:, 1:P + 1], zrow[:, :], row[:, :], 0.0, ALU.add, ALU.max
                                           ).then_inc(shifted, 1)
                    dve.wait_ge(backed, 1)
                    ch.link(dve.tensor_tensor(seg[:, :], ps[:, 256:258], mk[:, 0, :], ALU.max))
                    a1, b = seg[:, 0:1], seg[:, 1:2]
                    ch.add(dve.tensor_tensor(v[:, 0:1], a1, first_edge[o][:, :], ALU.is_le))
                    ch.add(dve.tensor_tensor(v[:, 1:2], b, last_edge[o][:, :], ALU.is_le))
                    ch.add(dve.tensor_tensor(v[:, 2:3], b, last_edge[o][:, :], ALU.is_ge))
                    ch.add(dve.tensor_scalar(v[:, 3:4], b, -1.0, None, ALU.add))
                    ch.link(dve.tensor_scalar(v[:, 4:5], a1, -1.0, None, ALU.add))
                    ch.add(dve.tensor_tensor(g["whole"][:, :], v[:, 0:1], v[:, 2:3], ALU.mult))
                    ch.add(dve.tensor_copy(g["fix_get"][:, :], v[:, 3:4]))
                    ch.add(dve.tensor_copy(g["begins"][:, :], v[:, 4:5]))
                    ch.link(dve.tensor_tensor(v[:, 5:6], v[:, 0:1], v[:, 1:2], ALU.mult))
                    ch.link(dve.tensor_scalar(v[:, 6:7], v[:, 5:6], -FAR, FAR, ALU.mult, ALU.add))
                    ch.link(dve.tensor_tensor(v[:, 7:8], v[:, 6:7], v[:, 3:4], ALU.add))
                    ch.link(dve.tensor_copy(g["fix_put"][:, :], v[:, 7:8]))

                @block.tensor
                def _(pe):
                    pe.wait_ge(totals, 1)
                    pe.matmul(ps[0:NP, 0:1], earlier[0:NP, 0:NP], incl[:, NK - 1:NK], start=True, stop=True
                              ).then_inc(offs, 1)
                    pe.wait_ge(topped, 1)
                    pe.transpose(ps[0:2, 128:256], top[:, :], ident[:, :]).then_inc(rowed, 1)
                    pe.wait_ge(shifted, 1)
                    pe.transpose(ps[:, 256:258], row2[:, 0:P], ident[0:2, 0:2]).then_inc(backed, 1)

                @block.gpsimd
                def _(pool):
                    pool.wait_ge(marked, 1)
                    for k in range(NK):
                        pool.indirect_dma_start(marks[o], bass.IndirectOffsetOnAxis(g["put"][:, k:k + 1], 0),
                                                mark[:, k, :], None, bounds_check=P * cols - 1, oob_is_err=False
                                                ).then_inc(put_done, 16)

                @block.sync
                def _(sp):
                    sp.wait_ge(put_done, 16 * NK)
                    sp.dma_start(mk[:, :, :], edges(marks[o])).then_inc(got, 16)

        def node_product(name, widths, fill, weights, cols, use, middle=None, taken=None, put=None, store=None):
            groups = NK // GK
            L = GK * NP
            total = sum(widths)
            starts = [sum(widths[:n]) for n in range(len(widths))]
            with ExitStack() as ctx:
                stage = [sb(f"{name}_stage{b}", [NP, GK, total], F32, ctx) for b in range(2)]
                flipped = [[sb(f"{name}_flip{b}_{n}", [w, L], F32, ctx) for n, w in enumerate(widths)] for b in range(2)]
                flip_ps = [[ctx.enter_context(nc.psum_tensor(f"{name}_fps{b}_{n}", [P, 512], F32))
                            for n in range(len(widths))] for b in range(2)]
                prod_ps = [ctx.enter_context(nc.psum_tensor(f"{name}_pps{b}", [P, 512], F32)) for b in range(2)]
                s = {n: sem(f"{name}_{n}") for n in
                     ("fill_steps", "staged", "turned", "flipped", "multiplied", "use_steps", "used", "mid_multiplied",
                      "mid_steps", "mid_done", "admitted")}
                if middle:
                    mid_w, M, mid_function = middle
                    mid_ps = [ctx.enter_context(nc.psum_tensor(f"{name}_mps{b}", [P, 512], F32)) for b in range(2)]
                    mid = [[sb(f"{name}_mid{b}{n}", [M, L], F32, ctx) for n in range(2)] for b in range(2)]
                took = [sem(f"{name}_took{b}") for b in range(2)]
                was_put, stored = sem(f"{name}_was_put"), sem(f"{name}_stored")
                block = ctx.enter_context(nc.Block())

                if taken or put:
                    @block.gpsimd
                    def _(pool):
                        for k in range(NK):
                            i = k // GK
                            if taken:
                                o, table, tile = taken
                                if k % GK == 0 and i > 1:
                                    pool.wait_ge(s["staged"], i - 1)
                                pool.indirect_dma_start(tile[:, k, :], None, table,
                                                        bass.IndirectOffsetOnAxis(order[o]["take"][:, k:k + 1], 0)
                                                        ).then_inc(took[i % 2], 16)
                            if put:
                                tile, table = put
                                if k % GK == 0:
                                    pool.wait_ge(s["used"], i + 1)
                                pool.indirect_dma_start(table, bass.IndirectOffsetOnAxis(order["d"]["put"][:, k:k + 1], 0),
                                                        tile[:, k, :], None, bounds_check=E - 1, oob_is_err=False
                                                        ).then_inc(was_put, 16)
                        if put:
                            pool.wait_ge(was_put, 16 * NK)

                if store:
                    @block.sync
                    def _(sp):
                        sp.wait_ge(s["used"], groups)
                        sp.dma_start(node_rows(store[1]), store[0][:, :, :]).then_inc(stored, 16)
                        sp.wait_ge(stored, 16)

                @block.vector
                def _(dve):
                    filling, using = Chain(dve, s["fill_steps"]), Chain(dve, s["use_steps"])

                    def take(i, b, turn, first):
                        using.begin(i)
                        dve.wait_ge(s["multiplied"], i + 1)
                        use(dve, using, i, prod_ps[b][0:NP, 0:GK * cols].rearrange("p (k w) -> p k w", w=cols)
                            ).then_inc(s["used"], 1)

                    def put(i, b, turn, first):
                        filling.begin(i)
                        if not first:
                            dve.wait_ge(s["turned"], i - 1)
                        if taken:
                            dve.wait_ge(took[b], 16 * GK * (turn + 1))
                        fill(dve, filling, i, stage[b]).then_inc(s["staged"], 1)

                    (run_turns_ahead if middle else run_turns_late)(dve, groups, put, take)

                @block.tensor
                def _(pe):
                    def middle_product(i, b):
                        pe.wait_ge(s["flipped"], i + 1)
                        pe.sem_inc(s["admitted"], 1)
                        pe.matmul(mid_ps[b][0:M, 0:L], mid_w, flipped[b][0][:, :], start=True, stop=True
                                  ).then_inc(s["mid_multiplied"], 1)

                    def turn_over(i, b, turn, first):
                        pe.wait_ge(s["staged"], i + 1)
                        if not first:
                            pe.wait_ge(s["flipped"], i - 1)
                        pe.sem_inc(s["admitted"], 1)
                        for n, w in enumerate(widths):
                            for k in range(GK):
                                last = pe.transpose(flip_ps[b][n][0:w, k * NP:(k + 1) * NP],
                                                    stage[b][:, k, starts[n]:starts[n] + w], ident[0:NP, 0:NP])
                        last.then_inc(s["turned"], 1)
                        if middle and not (first and b == 0):
                            middle_product(i - 1, 1 - b)

                    def product(i, b, turn, first):
                        if middle and isinstance(i, int) and i == groups - 1:
                            middle_product(i, b)
                        pe.wait_ge(s["mid_done" if middle else "flipped"], i + 1)
                        if not first:
                            pe.wait_ge(s["used"], i - 1)
                        pe.sem_inc(s["admitted"], 1)
                        left = mid[b] if middle else flipped[b]
                        for k in range(GK):
                            for n in range(len(left)):
                                last = pe.matmul(prod_ps[b][0:NP, k * cols:(k + 1) * cols],
                                                 left[n][:, k * NP:(k + 1) * NP], weights[n],
                                                 start=(n == 0), stop=(n == len(left) - 1))
                        last.then_inc(s["multiplied"], 1)

                    (run_turns_ahead if middle else run_turns_late)(pe, groups, turn_over, product)

                @block.scalar
                def _(act):
                    mid_chain = Chain(act, s["mid_steps"])

                    def flip(i, b, turn, first):
                        act.wait_ge(s["turned"], i + 1)
                        if not first:
                            act.wait_ge(s["mid_multiplied" if middle else "multiplied"], i - 1)
                        for n, w in enumerate(widths):
                            last = act.copy(flipped[b][n][:, :], flip_ps[b][n][0:w, 0:L])
                        last.then_inc(s["flipped"], 1)

                    def in_between(i, b, turn, first):
                        mid_chain.begin(i)
                        act.wait_ge(s["mid_multiplied"], i + 1)
                        if not first:
                            act.wait_ge(s["multiplied"], i - 1)
                        mid_function(act, mid_chain, mid[b], mid_ps[b][0:M, 0:L]).then_inc(s["mid_done"], 1)

                    if middle:
                        run_turns_late(act, groups, flip, in_between)
                    else:
                        run_turns(act, groups, flip)

        def whole_groups(src_tile, scale=1.0):
            def fill(dve, ch, i, stage):
                return dve.tensor_scalar(stage[:, :, :], src_tile[:, bass.ds(i * GK, GK), :], scale, None, ALU.mult)
            return fill

        def into(dst_tile, scale=1.0):
            def use(dve, ch, i, prod):
                return dve.tensor_scalar(dst_tile[:, bass.ds(i * GK, GK), :], prod, scale, None, ALU.mult)
            return use

        def load_all(name, pairs, ctx):
            done = sem(f"{name}_in")
            with nc.Block() as block:
                @block.sync
                def _(sp):
                    with nc.allow_non_contiguous_dma(reason="small weights"):
                        for d, s_ in pairs:
                            sp.dma_start(d, s_).then_inc(done, 16)
                    sp.wait_ge(done, 16 * len(pairs))

        def on_vector(name, body):
            steps = sem(f"{name}_steps")
            with nc.Block() as block:
                @block.vector
                def _(dve):
                    body(dve, Chain(dve, steps))

        def spread(row, parts, w):
            return row.unsqueeze(0).to_broadcast([parts, w])

        def put_rows(name, table_rows, table_tile, starts_tile, starts_table, width):
            stored, put = sem(f"{name}_stored"), sem(f"{name}_put")
            with nc.Block() as block:
                if table_rows is not None:
                    @block.sync
                    def _(sp):
                        sp.dma_start(node_rows(table_rows), table_tile[:, :, :]).then_inc(stored, 16)
                        sp.wait_ge(stored, 16)

                @block.gpsimd
                def _(pool):
                    for k in range(NK):
                        pool.indirect_dma_start(starts_table, bass.IndirectOffsetOnAxis(order["d"]["put"][:, k:k + 1], 0),
                                                starts_tile[:, k, :], None, bounds_check=E - 1, oob_is_err=False
                                                ).then_inc(put, 16)
                    pool.wait_ge(put, 16 * NK)

        def take(pool, took, o, table, tile):
            for k in range(NK):
                pool.indirect_dma_start(tile[:, k, :], None, table,
                                        bass.IndirectOffsetOnAxis(order[o]["take"][:, k:k + 1], 0)).then_inc(took, 16)
            pool.wait_ge(took, 16 * NK)

        def take_rows(name, o, table, tile):
            took = sem(f"{name}_took")
            with nc.Block() as block:
                @block.gpsimd
                def _(pool):
                    take(pool, took, o, table, tile)

        def join_sums(name, o, table, w, last_rows):
            with ExitStack() as ctx:
                wide, rows = sb(f"{name}_wide", [P, w], F32, ctx), sb(f"{name}_rows", [w, 3, P + 1], F32, ctx)
                at = sb(f"{name}_at", [P, w], F32, ctx)
                ps = ctx.enter_context(nc.psum_tensor(f"{name}_ps", [P, 512], F32))
                steps, ready, turned, summed, back, got, fixed, put = (
                    sem(f"{name}_{n}") for n in ("steps", "ready", "turned", "summed", "back", "got", "fixed", "put"))
                block = ctx.enter_context(nc.Block())

                @block.vector
                def _(dve):
                    ch = Chain(dve, steps)
                    dve.tensor_copy(wide[:, :], order[o]["whole"][:, :].to_broadcast([P, w])).then_inc(ready, 1)
                    dve.wait_ge(turned, 1)
                    ch.add(dve.tensor_copy(rows[:, 0, 0:P], ps[0:w, 0:P]))
                    ch.add(dve.memset(rows[:, 2, 0:1], 0.0))
                    ch.link(dve.tensor_copy(rows[:, 1, 0:P], ps[0:w, P:2 * P]))
                    dve.tensor_tensor_scan(rows[:, 2, 1:P + 1], rows[:, 1, 0:P], rows[:, 0, 0:P], 0.0, ALU.mult, ALU.add
                                           ).then_inc(summed, 1)
                    dve.wait_ge(back, 1)
                    dve.wait_ge(got, 16)
                    dve.tensor_tensor(at[:, :], at[:, :], ps[:, 2 * P:2 * P + w], ALU.add).then_inc(fixed, 1)

                @block.tensor
                def _(pe):
                    pe.wait_ge(ready, 1)
                    pe.transpose(ps[0:w, 0:P], last_rows[:, :], ident[:, :])
                    pe.transpose(ps[0:w, P:2 * P], wide[:, :], ident[:, :]).then_inc(turned, 1)
                    pe.wait_ge(summed, 1)
                    pe.transpose(ps[:, 2 * P:2 * P + w], rows[:, 2, 0:P], ident[0:w, 0:w]).then_inc(back, 1)

                @block.gpsimd
                def _(pool):
                    pool.indirect_dma_start(at[:, :], None, table, bass.IndirectOffsetOnAxis(order[o]["fix_get"][:, 0:1], 0)
                                            ).then_inc(got, 16)
                    pool.wait_ge(fixed, 1)
                    pool.indirect_dma_start(table, bass.IndirectOffsetOnAxis(order[o]["fix_put"][:, 0:1], 0), at[:, :], None,
                                            bounds_check=P * cols_of[o] - 1, oob_is_err=False).then_inc(put, 16)
                    pool.wait_ge(put, 16)

        def join_softmax(name, heads, feats, table, last_rows):
            w = heads * (feats + 1)
            full = w + heads
            with ExitStack() as ctx:
                tops, wide = sb(f"{name}_tops", [P, w], F32, ctx), sb(f"{name}_wide", [P, w], F32, ctx)
                rows = sb(f"{name}_rows", [w, 7, P + 1], F32, ctx)
                at, at_top = sb(f"{name}_at", [P, full], F32, ctx), sb(f"{name}_at_top", [P, w], F32, ctx)
                cin = sb(f"{name}_cin", [P, 2, w], F32, ctx)
                new_top, e1, e2 = (sb(f"{name}_{n}", [P, w], F32, ctx) for n in ("new_top", "e1", "e2"))
                done = sb(f"{name}_done", [P, full], F32, ctx)
                ps = ctx.enter_context(nc.psum_tensor(f"{name}_ps", [P, 512], F32))
                ps2 = ctx.enter_context(nc.psum_tensor(f"{name}_ps2", [P, 512], F32))
                steps, ready, turned, summed, back, got, fixed, put, ask, said = (
                    sem(f"{name}_{n}") for n in
                    ("steps", "ready", "turned", "summed", "back", "got", "fixed", "put", "ask", "said"))
                block = ctx.enter_context(nc.Block())

                def by_head(t, rows_ap, first, last):
                    for h in range(heads):
                        yield (t[:, h * feats:(h + 1) * feats], rows_ap[:, w + h:w + h + 1].to_broadcast([P, feats]))
                        yield (t[:, heads * feats + h:heads * feats + h + 1], rows_ap[:, w + h:w + h + 1])

                @block.vector
                def _(dve):
                    ch = Chain(dve, steps)
                    for o_, i_ in by_head(tops, last_rows, 0, 0):
                        ch.add(dve.tensor_copy(o_, i_))
                    ch.sync()
                    dve.tensor_scalar(wide[:, :], order["d"]["whole"][:, :].to_broadcast([P, w]), BIG, -BIG, ALU.mult, ALU.add
                                      ).then_inc(ready, 1)
                    dve.wait_ge(turned, 1)
                    A, B, T, M, DD, S, X = (rows[:, n, :] for n in range(7))
                    ch.add(dve.tensor_copy(A[:, 0:P], ps[0:w, 0:P]))
                    ch.add(dve.tensor_copy(B[:, 0:P], ps[0:w, P:2 * P]))
                    ch.add(dve.tensor_copy(T[:, 0:P], ps[0:w, 2 * P:3 * P]))
                    ch.add(dve.memset(M[:, 0:1], -BIG))
                    ch.link(dve.memset(S[:, 0:1], 0.0))
                    ch.link(dve.tensor_tensor_scan(M[:, 1:P + 1], B[:, 0:P], T[:, 0:P], -BIG, ALU.add, ALU.max))
                    ch.add(dve.tensor_tensor(T[:, 0:P], T[:, 0:P], M[:, 1:P + 1], ALU.subtract))
                    ch.link(dve.tensor_tensor(DD[:, 0:P], M[:, 0:P], B[:, 0:P], ALU.add))
                    dve.tensor_tensor(DD[:, 0:P], DD[:, 0:P], M[:, 1:P + 1], ALU.subtract).then_inc(ask, 1)
                    dve.wait_ge(said, 1)
                    ch.link(dve.tensor_tensor(X[:, 0:P], A[:, 0:P], T[:, 0:P], ALU.mult))
                    dve.tensor_tensor_scan(S[:, 1:P + 1], DD[:, 0:P], X[:, 0:P], 0.0, ALU.mult, ALU.add).then_inc(summed, 1)
                    dve.wait_ge(got, 16)
                    for o_, i_ in by_head(at_top, at, 0, 0):
                        ch.add(dve.tensor_copy(o_, i_))
                    dve.wait_ge(back, 1)
                    ch.add(dve.tensor_copy(cin[:, 0, :], ps2[:, 0:w]))
                    ch.link(dve.tensor_copy(cin[:, 1, :], ps2[:, w:2 * w]))
                    ch.link(dve.tensor_tensor(new_top[:, :], at_top[:, :], cin[:, 1, :], ALU.max))
                    ch.add(dve.tensor_tensor(e1[:, :], at_top[:, :], new_top[:, :], ALU.subtract))
                    dve.tensor_tensor(e2[:, :], cin[:, 1, :], new_top[:, :], ALU.subtract).then_inc(ask, 1)
                    dve.wait_ge(said, 2)
                    ch.add(dve.tensor_tensor(e1[:, :], e1[:, :], at[:, 0:w], ALU.mult))
                    ch.add(dve.tensor_tensor(e2[:, :], e2[:, :], cin[:, 0, :], ALU.mult))
                    for h in range(heads):
                        ch.add(dve.tensor_copy(done[:, w + h:w + h + 1], new_top[:, heads * feats + h:heads * feats + h + 1]))
                    ch.sync()
                    dve.tensor_tensor(done[:, 0:w], e1[:, :], e2[:, :], ALU.add).then_inc(fixed, 1)

                @block.scalar
                def _(act):
                    act.wait_ge(ask, 1)
                    act.activation(rows[:, 2, 0:P], rows[:, 2, 0:P], ACT.Exp)
                    act.activation(rows[:, 4, 0:P], rows[:, 4, 0:P], ACT.Exp).then_inc(said, 1)
                    act.wait_ge(ask, 2)
                    act.activation(e1[:, :], e1[:, :], ACT.Exp)
                    act.activation(e2[:, :], e2[:, :], ACT.Exp).then_inc(said, 1)

                @block.tensor
                def _(pe):
                    pe.wait_ge(ready, 1)
                    pe.transpose(ps[0:w, 0:P], last_rows[:, 0:w], ident[:, :])
                    pe.transpose(ps[0:w, P:2 * P], wide[:, :], ident[:, :])
                    pe.transpose(ps[0:w, 2 * P:3 * P], tops[:, :], ident[:, :]).then_inc(turned, 1)
                    pe.wait_ge(summed, 1)
                    pe.transpose(ps2[:, 0:w], rows[:, 5, 0:P], ident[0:w, 0:w])
                    pe.transpose(ps2[:, w:2 * w], rows[:, 3, 0:P], ident[0:w, 0:w]).then_inc(back, 1)

                @block.gpsimd
                def _(pool):
                    pool.indirect_dma_start(at[:, :], None, table,
                                            bass.IndirectOffsetOnAxis(order["d"]["fix_get"][:, 0:1], 0)).then_inc(got, 16)
                    pool.wait_ge(fixed, 1)
                    pool.indirect_dma_start(table, bass.IndirectOffsetOnAxis(order["d"]["fix_put"][:, 0:1], 0),
                                            done[:, :], None, bounds_check=E - 1, oob_is_err=False).then_inc(put, 16)
                    pool.wait_ge(put, 16)

        def attention(name, heads, feats, table, tw, sums, last_rows, extra):
            w = heads * (feats + 1)
            full = w + heads
            sums_v = edges(sums)
            ex_v = edges(ex4)
            with ExitStack() as ctx:
                idx = [sb(f"{name}_idx{b}", [P, CW], I32, ctx) for b in range(2)]
                got = [sb(f"{name}_got{b}", [P, CW, tw], F32, ctx) for b in range(2)]
                ex = [sb(f"{name}_ex{b}", [P, CW, 4], F32, ctx) for b in range(2)]
                ad = [sb(f"{name}_ad{b}", [P, heads, CW], F32, ctx) for b in range(2)]
                sc = sb(f"{name}_sc", [P, heads, CW], F32, ctx)
                top = [sb(f"{name}_top{b}", [P, heads, CW + 1], F32, ctx) for b in range(2)]
                ex_in = sb(f"{name}_ex_in", [P, 2, heads, CW], F32, ctx)
                ex_out = sb(f"{name}_ex_out", [P, 2, heads, CW], F32, ctx)
                px = sb(f"{name}_px", [P, heads, feats, CW], F32, ctx)
                acc = [sb(f"{name}_acc{b}", [P, CW, full], F32, ctx) for b in range(2)]
                first_row = sb(f"{name}_first", [P, 4], F32, ctx)
                idx_in, ex_in_s, gathered, stored = ([sem(f"{name}_{n}{b}") for b in range(2)]
                                                     for n in ("idx_in", "ex_in", "gathered", "stored"))
                steps, spread_, asked, said, done, admitted, let_in, first_got, start_steps = (
                    sem(f"{name}_{n}") for n in
                    ("steps", "spread", "asked", "said", "done", "admitted", "let_in", "first_got", "start_steps"))
                extra.allocate(ctx)
                block = ctx.enter_context(nc.Block())

                @block.sync
                def _(sp):
                    def body(i, b, turn, first):
                        if not first:
                            sp.wait_ge(gathered[b], 16 * CW * turn)
                        sp.dma_start(idx[b][:, :], src_v[:, bass.ds(i * CW, CW)]).then_inc(idx_in[b], 16)
                        if not first:
                            sp.wait_ge(spread_, i - 1)
                            sp.sem_inc(let_in, 1)
                        sp.dma_start(ex[b][:, :, :], ex_v[:, bass.ds(i * CW, CW), :]).then_inc(ex_in_s[b], 16)
                        extra.sync(sp, i, b, turn, first)
                    run_turns(sp, NCH, body)
                    extra.sync_end(sp)

                @block.gpsimd
                def _(pool):
                    pool.indirect_dma_start(first_row[:, :], None, ex4,
                                            bass.IndirectOffsetOnAxis(order["d"]["begins"][:, 0:1], 0)).then_inc(first_got, 16)

                    def body(i, b, turn, first):
                        pool.wait_ge(idx_in[b], 16 * turn + 16)
                        if not first:
                            pool.wait_ge(done, i - 1)
                        pool.sem_inc(admitted, 1)
                        for j in range(CW):
                            pool.indirect_dma_start(got[b][:, j, :], None, table,
                                                    bass.IndirectOffsetOnAxis(idx[b][:, j:j + 1], 0)
                                                    ).then_inc(gathered[b], 16)
                    run_turns(pool, NCH, body)

                @block.vector
                def _(dve):
                    start = Chain(dve, start_steps)
                    dve.wait_ge(first_got, 16)
                    for h in range(heads):
                        start.add(dve.tensor_copy(ad[1][:, h, CW - 1:CW], first_row[:, h:h + 1]))
                    start.add(dve.memset(top[1][:, :, CW:CW + 1], -BIG))
                    start.add(dve.memset(acc[1][:, CW - 1, :], 0.0))
                    start.sync()
                    extra.vector_start(dve)
                    ch = Chain(dve, steps)

                    def ask(i, b, turn, first):
                        ch.begin(i)
                        kp, fr = keep["d"][:, bass.ds(i * CW, CW)], fresh[:, bass.ds(i * CW, CW)]
                        dve.wait_ge(ex_in_s[b], 16 * turn + 16)
                        for h in range(heads):
                            last = dve.tensor_tensor_scan(ad[b][:, h, :], kp, ex[b][:, :, h], ad[1 - b][:, h, CW - 1:CW],
                                                          ALU.mult, ALU.add)
                        last.then_inc(spread_, 1)
                        dve.wait_ge(spread_, i + 1)
                        dve.wait_ge(gathered[b], 16 * CW * (turn + 1))
                        g_a = got[b][:, :, feats:feats + heads].rearrange("p t f -> p f t")
                        ch.add(dve.tensor_copy(top[b][:, :, 0:1], top[1 - b][:, :, CW:CW + 1]))
                        ch.link(dve.tensor_tensor(sc[:, :, :], ad[b][:, :, :], g_a, ALU.add))
                        ch.link(dve.scalar_tensor_tensor(out=sc[:, :, :], in0=sc[:, :, :], scalar=SLOPE, in1=sc[:, :, :],
                                                         op0=ALU.mult, op1=ALU.max))
                        for h in range(heads):
                            ch.add(dve.tensor_tensor_scan(top[b][:, h, 1:CW + 1], fr, sc[:, h, :],
                                                          top[1 - b][:, h, CW:CW + 1], ALU.add, ALU.max))
                        ch.sync()
                        ch.add(dve.tensor_tensor(ex_in[:, 1, :, :], sc[:, :, :], top[b][:, :, 1:CW + 1], ALU.subtract))
                        ch.link(dve.tensor_tensor(ex_in[:, 0, :, :], top[b][:, :, 0:CW],
                                                  fr.unsqueeze(1).to_broadcast([P, heads, CW]), ALU.add))
                        dve.tensor_tensor(ex_in[:, 0, :, :], ex_in[:, 0, :, :], top[b][:, :, 1:CW + 1], ALU.subtract
                                          ).then_inc(asked, 1)

                    def weigh(i, b, turn, first):
                        g_x = got[b][:, :, 0:feats].rearrange("p t f -> p f t")
                        dve.wait_ge(said, i + 1)
                        p = ex_out[:, 1, :, :]
                        ch.link(dve.tensor_tensor(px[:, :, :, :], g_x.unsqueeze(1).to_broadcast([P, heads, feats, CW]),
                                                  p.unsqueeze(2).to_broadcast([P, heads, feats, CW]), ALU.mult))
                        if not first:
                            dve.wait_ge(stored[b], 16 * turn)
                        for h in range(heads):
                            for f in range(feats):
                                c = h * feats + f
                                dve.tensor_tensor_scan(acc[b][:, :, c], ex_out[:, 0, h, :], px[:, h, f, :],
                                                       acc[1 - b][:, CW - 1, c:c + 1], ALU.mult, ALU.add)
                            c = heads * feats + h
                            dve.tensor_tensor_scan(acc[b][:, :, c], ex_out[:, 0, h, :], p[:, h, :],
                                                   acc[1 - b][:, CW - 1, c:c + 1], ALU.mult, ALU.add)
                        dve.tensor_copy(acc[b][:, :, w:full], top[b][:, :, 1:CW + 1].rearrange("p h t -> p t h")
                                        ).then_inc(done, 1)
                        dve.wait_ge(done, i + 1)

                    run_turns_woven(dve, NCH, lambda now, before: extra.vector(dve, now, before, ask, weigh))
                    dve.tensor_copy(last_rows[:, :], acc[0][:, CW - 1, :])
                    extra.vector_end(dve)

                @block.scalar
                def _(act):
                    def exponential(i, b, turn, first):
                        act.wait_ge(asked, i + 1)
                        act.activation(ex_out[:, :, :, :], ex_in[:, :, :, :], ACT.Exp).then_inc(said, 1)

                    def store(i, b, turn, first):
                        act.wait_ge(done, i + 1)
                        act.dma_start(sums_v[:, bass.ds(i * CW, CW), :], acc[b][:, :, :]).then_inc(stored[b], 16)
                    run_turns_woven(act, NCH, lambda now, before: extra.scalar(act, now, before, exponential, store))
                    act.wait_ge(stored[0], 16 * ((NCH + 1) // 2))
                    act.wait_ge(stored[1], 16 * (NCH // 2))
                    extra.scalar_end(act)

                @block.tensor
                def _(pe):
                    extra.tensor_start(pe)
                    run_turns(pe, NCH, lambda i, b, turn, first: extra.tensor(pe, i, b, turn, first))

        class CountSources:

            def allocate(self, ctx):
                self.hist = Histogram("hist_s", src_v, True, ctx)

            def sync(self, sp, i, b, turn, first):
                self.hist.load(sp, i, b, first)

            def sync_end(self, sp):
                pass

            def vector_start(self, dve):
                self.hist.dve_start(dve)

            def vector(self, dve, now, before, ask, weigh):
                if now:
                    self.hist.dve(dve, *now)
                    ask(*now)
                    weigh(*now)

            def vector_end(self, dve):
                self.hist.finish(dve)

            def scalar(self, act, now, before, exponential, store):
                if now:
                    exponential(*now)
                    store(*now)

            def scalar_end(self, act):
                pass

            def tensor_start(self, pe):
                self.hist.pe_start(pe)

            def tensor(self, pe, i, b, turn, first):
                self.hist.pe(pe, i, b, turn, first)

        class PlaceBySource:

            def allocate(self, ctx):
                self.groups = [list(range(t, min(t + LANES, CP))) for t in range(0, CP, LANES)]
                self.G = len(self.groups)
                ps = lambda n: ctx.enter_context(nc.psum_tensor(n, [P, 512], F32))
                self.hots = OneHots("place", CP, ctx)
                self.loaded = [sem(f"place_loaded{b}") for b in range(2)]
                self.next_ps = ps("place_next_ps")
                self.turn_ps = [ctx.enter_context(nc.psum_tensor(f"place_turn_ps{q}", [P, 1024], BF16)) for q in range(2)]
                self.same_ps = [ps(f"place_same_ps{q}") for q in range(2)]
                self.look_ps = [ps(f"place_look_ps{q}") for q in range(2)]
                self.hot_at = [sb(f"place_hot_at{q}", [NP, LANES, P], F32, ctx) for q in range(self.G)]
                self.hot_at_b = [sb(f"place_hot_at_b{q}", [NP, LANES, P], BF16, ctx) for q in range(self.G)]
                self.nexts = [sb(f"place_nexts{q}", [NP, LANES, NK], F32, ctx) for q in range(2)]
                self.same = [sb(f"place_same{q}", [P, LANES, P], BF16, ctx) for q in range(2)]
                self.tmp = sb("place_tmp", [P, LANES, NK], F32, ctx)
                self.place = [sb(f"place_place{b}", [P, CP], F32, ctx) for b in range(2)]
                self.place_i = [sb(f"place_place_i{b}", [P, CP], I32, ctx) for b in range(2)]
                self.stored = [sem(f"place_stored{b}") for b in range(2)]
                (self.steps, self.late_steps, self.ready, self.turned, self.flat, self.matched, self.masked, self.looked,
                 self.summed, self.counted, self.copied, self.placed) = (
                    sem(f"place_{n}") for n in
                    ("steps", "late_steps", "ready", "turned", "flat", "matched", "masked", "looked", "summed", "counted",
                     "copied", "placed"))

            def sync(self, sp, i, b, turn, first):
                if not first:
                    sp.wait_ge(self.ready, i - 1)
                sp.dma_start(self.hots.key[b][:, :], src_v[:, bass.ds(i * CW, CP)]).then_inc(self.loaded[b], 16)

            def sync_end(self, sp):
                pass

            def vector_start(self, dve):
                self.chain, self.late_chain = Chain(dve, self.steps), Chain(dve, self.late_steps)

            def make_hots(self, dve, i, b, turn, first):
                self.chain.begin(i)
                dve.wait_ge(self.loaded[b], 16 * turn + 16)
                if not first:
                    dve.wait_ge(self.counted, self.G * (i - 1) + 1)
                    dve.wait_ge(self.placed, i - 1)
                self.hots.make(self.chain, dve, b, self.ready)

            def vector(self, dve, now, before, ask, weigh):
                if before is None:
                    self.make_hots(dve, *now)
                    ask(*now)
                    weigh(*now)
                    return
                (i, b, turn, first), ch = before, self.late_chain
                ch.begin(i)
                dve.wait_ge(self.ready, i + 1)
                if not first:
                    dve.wait_ge(self.stored[b], 16 * turn)
                self.mask(dve, i, b, 0)
                for g in range(self.G):
                    if g + 1 < self.G:
                        self.mask(dve, i, b, g + 1)
                    if now and g == 0:
                        ask(*now)
                    if now and g == 1:
                        weigh(*now)
                    if now and g == 2:
                        self.make_hots(dve, *now)
                    self.take(dve, ch, i, b, g)
                dve.tensor_copy(self.place_i[b][:, :], self.place[b][:, :]).then_inc(self.placed, 1)

            def mask(self, dve, i, b, g):
                q, n = (b * self.G + g) % 2, len(self.groups[g])
                dve.wait_ge(self.matched, i * self.G + g + 1)
                dve.tensor_tensor(self.same[q][:, 0:n, :], self.same_ps[q][:, 0:n * P].rearrange("p (t e) -> p t e", e=P),
                                  earlier[:, :].unsqueeze(1).to_broadcast([P, n, P]), ALU.mult).then_inc(self.masked, 1)

            def take(self, dve, ch, i, b, g):
                G, ts = len(self.groups), self.groups[g]
                q, n = (b * G + g) % 2, len(ts)
                dve.wait_ge(self.looked, i * G + g + 1)
                ch.link(dve.tensor_tensor(self.tmp[:, 0:n, :], self.look_ps[q][:, 0:n * NK].rearrange("p (t k) -> p t k", k=NK),
                                          self.hots.hot_k[b][:, ts[0]:ts[0] + n, :], ALU.mult))
                dve.tensor_reduce(self.place[b][:, ts[0]:ts[0] + n], self.tmp[:, 0:n, :], AX_X, ALU.add).then_inc(self.summed, 1)
                dve.wait_ge(self.summed, i * G + g + 1)

            def vector_end(self, dve):
                pass

            def flatten(self, act, i, b, g, first):
                G, n = self.G, len(self.groups[g])
                act.wait_ge(self.turned, i * G + g + 1)
                if not (first and b == 0):
                    act.wait_ge(self.looked, i * G + g + 1 - G)
                turned = self.turn_ps[(b * G + g) % 2][0:NP, 0:n * P].rearrange("a (t e) -> a t e", e=P)
                act.copy(self.hot_at_b[g][:, 0:n, :], turned)
                act.copy(self.hot_at[g][:, 0:n, :], turned).then_inc(self.flat, 1)

            def scalar(self, act, now, before, exponential, store):
                G = self.G
                if before is None:
                    exponential(*now)
                else:
                    i, b, turn, first = before
                    for g in range(G):
                        act.wait_ge(self.counted, i * G + g + 1)
                        act.copy(self.nexts[(b * G + g) % 2][:, :, :].rearrange("a t k -> a (t k)"), self.next_ps[0:NP, :]
                                 ).then_inc(self.copied, 1)
                        if g + 2 < G:
                            self.flatten(act, i, b, g + 2, first)
                        if now and g == 0:
                            exponential(*now)
                if now:
                    for g in range(2):
                        self.flatten(act, now[0], now[1], g, now[3])
                    store(*now)
                if before is not None:
                    act.wait_ge(self.placed, i + 1)
                    act.dma_start(pos_rows[:, bass.ds(i * CP, CP)], self.place_i[b][:, :]).then_inc(self.stored[b], 16)

            def scalar_end(self, act):
                act.wait_ge(self.stored[0], 16 * ((NCH + 1) // 2))
                act.wait_ge(self.stored[1], 16 * (NCH // 2))

            def tensor_start(self, pe):
                pe.matmul(self.next_ps[0:NP, :], ident[0:NP, 0:NP], free_place[:, :, :].rearrange("a t k -> a (t k)"),
                          start=True, stop=False, skip_group_check=True).then_inc(self.counted, 1)

            def tensor(self, pe, i, b, turn, first):
                G = len(self.groups)
                hot_a, hot_k = self.hots.hot_a[b], self.hots.hot_k[b]

                def turn_(g):
                    q, ts = (b * G + g) % 2, self.groups[g]
                    for n, t in enumerate(ts):
                        last = pe.transpose(self.turn_ps[q][0:NP, n * P:(n + 1) * P], hot_a[:, t, :], ident_b[:, :])
                    last.then_inc(self.turned, 1)

                def match(g):
                    q, ts = (b * G + g) % 2, self.groups[g]
                    pe.wait_ge(self.flat, i * G + g + 1)
                    if not (first and b == 0 and g < 2):
                        pe.wait_ge(self.masked, i * G + g - 1)
                    for n, t in enumerate(ts):
                        last = pe.matmul(self.same_ps[q][:, n * P:(n + 1) * P], self.hot_at_b[g][:, n, :],
                                         self.hot_at_b[g][:, n, :], start=True, stop=True)
                    last.then_inc(self.matched, 1)

                pe.wait_ge(self.ready, i + 1)
                turn_(0)
                turn_(1)
                match(0)
                for g, ts in enumerate(self.groups):
                    if g + 2 < G:
                        turn_(g + 2)
                    if g + 1 < G:
                        match(g + 1)
                    q = (b * G + g) % 2
                    pe.wait_ge(self.masked, i * G + g + 1)
                    if not (first and b == 0 and g < 2):
                        pe.wait_ge(self.summed, i * G + g - 1)
                    pe.wait_ge(self.copied, i * G + g + 1)
                    for n, t in enumerate(ts):
                        pe.matmul(self.look_ps[q][:, n * NK:(n + 1) * NK], self.hot_at[g][:, n, :],
                                  self.nexts[q][:, n, :], start=True, stop=False, skip_group_check=True)
                        last = pe.matmul(self.look_ps[q][:, n * NK:(n + 1) * NK], self.same[q][:, n, :], hot_k[:, t, :],
                                         start=False, stop=True, skip_group_check=True)
                    last.then_inc(self.looked, 1)
                    for n, t in enumerate(ts):
                        last = pe.matmul(self.next_ps[0:NP, n * NK:(n + 1) * NK], hot_a[:, t, :], hot_k[:, t, :],
                                         start=False, stop=False, skip_group_check=True)
                    last.then_inc(self.counted, 1)

        class DirectSums:

            def __init__(self, name, cp, ctx):
                self.cp, self.cd, depth = cp, CW - cp, 2
                CD = self.cd
                self.depth = depth
                self.Q = NR // 8
                self.BQ = self.Q // 4
                self.acc = ctx.enter_context(nc.psum_tensor(f"{name}_dps", [P, 4, 512], F32))
                self.key = [sb(f"{name}_dkey{b}", [P, CD], I32, ctx) for b in range(2)]
                self.part = sb(f"{name}_dpart", [P, 2, CD], I32, ctx)
                self.q = sb(f"{name}_dq", [P, CD], F32, ctx)
                self.k8 = sb(f"{name}_dk8", [P, CD], BF16, ctx)
                self.hot8 = sb(f"{name}_dhot8", [P, CD, 8], BF16, ctx)
                self.rest = sb(f"{name}_drest", [P, CD, D], F32, ctx)
                self.pieces = sb(f"{name}_dpieces", [P, 3, CD, D], BF16, ctx)
                self.left = [sb(f"{name}_dleft{r}", [P, 3, CD, 8 * D], BF16, ctx) for r in range(depth)]
                self.hot_q = [sb(f"{name}_dhotq{r}", [P, CD, self.Q], BF16, ctx) for r in range(depth)]
                self.zero = sb(f"{name}_dzero", [P, 512], BF16, ctx)
                self.key_in = [sem(f"{name}_dkey_in{b}") for b in range(2)]
                self.steps, self.keyed, self.hot, self.used, self.zero_set, self.let_in = (
                    sem(f"{name}_d{n}") for n in ("steps", "keyed", "hot", "used", "zero_set", "let_in"))

            def load(self, sp, i, b, first):
                if not first:
                    sp.wait_ge(self.keyed, i - 1)
                    sp.sem_inc(self.let_in, 1)
                sp.dma_start(self.key[b][:, :], src_v[:, bass.ds(i * CW + self.cp, self.cd)]).then_inc(self.key_in[b], 16)

            def vector_start(self, dve):
                dve.memset(self.zero[:, :], 0.0).then_inc(self.zero_set, 1)
                self.chain = Chain(dve, self.steps)

            def vector(self, dve, i, b, turn, first, msg):
                ch = self.chain
                ch.begin(i)
                if not (first and b < self.depth):
                    dve.wait_ge(self.used, self.cd * (i + 1 - self.depth))
                left, hot_q = self.left[b % self.depth], self.hot_q[b % self.depth]
                dve.wait_ge(self.key_in[b], 16 * turn + 16)
                ch.add(dve.tensor_scalar(self.part[:, 0, :], self.key[b][:, :], 3, None, ALU.logical_shift_right))
                dve.tensor_scalar(self.part[:, 1, :], self.key[b][:, :], 7, None, ALU.bitwise_and).then_inc(self.keyed, 1)
                dve.wait_ge(self.keyed, i + 1)
                ch.add(dve.tensor_copy(self.q[:, :], self.part[:, 0, :]))
                ch.add(dve.tensor_copy(self.pieces[:, 0, :, :], msg[:, self.cp:CW, :]))
                ch.link(dve.tensor_copy(self.k8[:, :], self.part[:, 1, :]))
                ch.add(dve.tensor_tensor(self.hot8[:, :, :], iota_8[:, :].unsqueeze(1).to_broadcast([P, self.cd, 8]),
                                         self.k8[:, :].unsqueeze(2).to_broadcast([P, self.cd, 8]), ALU.is_equal))
                ch.link(dve.tensor_tensor(self.rest[:, :, :], msg[:, self.cp:CW, :], self.pieces[:, 0, :, :], ALU.subtract))
                ch.link(dve.tensor_copy(self.pieces[:, 1, :, :], self.rest[:, :, :]))
                ch.link(dve.tensor_tensor(self.pieces[:, 2, :, :], self.rest[:, :, :], self.pieces[:, 1, :, :], ALU.subtract))
                for s_ in range(3):
                    last = dve.tensor_tensor(left[:, s_, :, :].rearrange("p t (k f) -> p t k f", f=D),
                                             self.pieces[:, s_, :, :].unsqueeze(2).to_broadcast([P, self.cd, 8, D]),
                                             self.hot8[:, :, :].unsqueeze(3).to_broadcast([P, self.cd, 8, D]), ALU.mult)
                    ch.add(last)
                for t in range(self.cd):
                    dve.tensor_scalar(hot_q[:, t, :], iota_q[:, :], self.q[:, t:t + 1], None, ALU.is_equal
                                      ).then_inc(self.hot, 1)

            def tensor_start(self, pe):
                pe.wait_ge(self.zero_set, 1)
                for n in range(4):
                    pe.matmul(self.acc[:, n, :], self.zero[:, 0:P], self.zero[:, :], start=True, stop=False,
                              skip_group_check=True)

            def tensor(self, pe, i, b, t):
                left, hot_q = self.left[b % self.depth], self.hot_q[b % self.depth]
                pe.wait_ge(self.hot, i * self.cd + t + 1)
                for s_ in range(3):
                    for n in range(4):
                        last = pe.matmul(self.acc[:, n, 0:self.BQ], left[:, s_, t, :],
                                         hot_q[:, t, n * self.BQ:(n + 1) * self.BQ],
                                         start=False, stop=False, skip_group_check=True)
                last.then_inc(self.used, 1)

            def finish(self, dve):
                dve.wait_ge(self.used, self.cd * NCH)
                dve.tensor_copy(direct_t[:, :].rearrange("p (n q) -> p n q", n=4), self.acc[:, :, 0:self.BQ])

        def settle_direct(name):
            with ExitStack() as ctx:
                ps = [ctx.enter_context(nc.psum_tensor(f"{name}_sps{n}", [P, 512], F32)) for n in range(4)]
                turned = sem(f"{name}_turned")
                block = ctx.enter_context(nc.Block())
                cols = direct_t[:, :].rearrange("m (a k) -> m k a", k=NK // 8)

                @block.tensor
                def _(pe):
                    for k in range(NK // 8):
                        pe.transpose(ps[k // 4][0:NP, k % 4 * P:(k % 4 + 1) * P], cols[:, k, :], ident[:, :]).then_inc(turned, 1)

                @block.vector
                def _(dve):
                    for n in range(4):
                        dve.wait_ge(turned, 4 * n + 4)
                        dve.tensor_copy(direct[:, 32 * n:32 * n + 32, :].rearrange("p k f -> p (k f)"), ps[n][0:NP, :])

        def both_sums(dve, ch, seg):
            ch.link(dve.tensor_tensor(seg[:, :, :], seg[:, :, :],
                                      order["s"]["has"][:, :].unsqueeze(2).to_broadcast([NP, NK, D]), ALU.mult))
            ch.link(dve.tensor_tensor(seg[:, :, :], seg[:, :, :], direct[:, :, :], ALU.add))

        def messages(name, attr, fills, outer_of, weights, finish, cp, exponential=False):
            de = attr.shape[1]
            lots = len(weights)
            attr_v, ex_v = edges(attr), edges(ex32)
            groups = [list(range(t, min(t + 4, CW))) for t in range(0, CW, 4)]
            G = len(groups)
            U = G * lots
            with ExitStack() as ctx:
                att = [sb(f"{name}_att{b}", [P, CW, de], F32, ctx) for b in range(2)]
                ex = [sb(f"{name}_ex{b}", [P, CW, EXW], F32, ctx) for b in range(2)]
                pos = [sb(f"{name}_pos{b}", [P, cp], I32, ctx) for b in range(2)]
                own = [sb(f"{name}_own{b}", [P, fills, CW], F32, ctx) for b in range(2)]
                outer = [sb(f"{name}_outer{b}", [P, CW, lots * P], F32, ctx) for b in range(2)]
                flip = [[sb(f"{name}_flip{q}{n}", [P, 4 * P], F32, ctx) for n in range(lots)] for q in range(2)]
                msg = [sb(f"{name}_msg{b}", [P, CW, D], F32, ctx) for b in range(2)]
                work = sb(f"{name}_work", [P, CW, D], F32, ctx)
                first_row = sb(f"{name}_first", [P, EXW], F32, ctx)
                sums = DirectSums(name, cp, ctx)
                flip_ps = [ctx.enter_context(nc.psum_tensor(f"{name}_fps{r}", [P, 512], F32)) for r in range(2)]
                msg_ps = [ctx.enter_context(nc.psum_tensor(f"{name}_mps{b}", [P, 512], F32)) for b in range(2)]
                att_in, ex_in, pos_in, scattered = ([sem(f"{name}_{n}{b}") for b in range(2)]
                                                    for n in ("att_in", "ex_in", "pos_in", "scattered"))
                spread_, outered, turned, copied, multiplied, done, asked, said, admitted, let_in, first_got, steps, start_steps = (
                    sem(f"{name}_{n}") for n in
                    ("spread", "outered", "turned", "copied", "multiplied", "done", "asked", "said", "admitted", "let_in",
                     "first_got", "steps", "start_steps"))
                block = ctx.enter_context(nc.Block())

                @block.sync
                def _(sp):
                    def body(i, b, turn, first):
                        if not first:
                            sp.wait_ge(outered, i - 1)
                        sp.dma_start(att[b][:, :, :], attr_v[:, bass.ds(i * CW, CW), :]).then_inc(att_in[b], 16)
                        sp.dma_start(ex[b][:, :, :], ex_v[:, bass.ds(i * CW, CW), :]).then_inc(ex_in[b], 16)
                        if not first:
                            sp.wait_ge(scattered[b], 16 * cp * turn)
                            sp.sem_inc(let_in, 1)
                        sp.dma_start(pos[b][:, :], pos_rows[:, bass.ds(i * CP, cp)]).then_inc(pos_in[b], 16)
                        sums.load(sp, i, b, first)
                    run_turns(sp, NCH, body)

                @block.gpsimd
                def _(pool):
                    pool.indirect_dma_start(first_row[:, :], None, ex32,
                                            bass.IndirectOffsetOnAxis(order["d"]["begins"][:, 0:1], 0)).then_inc(first_got, 16)

                    def body(i, b, turn, first):
                        pool.wait_ge(pos_in[b], 16 * turn + 16)
                        pool.wait_ge(done, i + 1)
                        pool.sem_inc(admitted, 1)
                        for j in range(cp):
                            pool.indirect_dma_start(msgs, bass.IndirectOffsetOnAxis(pos[b][:, j:j + 1], 0),
                                                    msg[b][:, j, :], None).then_inc(scattered[b], 16)
                    run_turns(pool, NCH, body)
                    pool.wait_ge(scattered[0], 16 * cp * ((NCH + 1) // 2))
                    pool.wait_ge(scattered[1], 16 * cp * (NCH // 2))

                @block.vector
                def _(dve):
                    start, ch = Chain(dve, start_steps), Chain(dve, steps)
                    dve.wait_ge(first_got, 16)
                    start.link(dve.tensor_copy(own[1][:, :, CW - 1], first_row[:, 0:fills]))
                    sums.vector_start(dve)

                    def post(i, b, turn, first):
                        ch.begin(i)
                        dve.wait_ge(multiplied, G * (i + 1))
                        if not first:
                            dve.wait_ge(scattered[b], 16 * cp * turn)
                        finish(dve, ch, i, msg[b], msg_ps[b][:, 0:CW * D].rearrange("p (t f) -> p t f", f=D), work,
                               own[b], asked, said).then_inc(done, 1)
                        dve.wait_ge(done, i + 1)
                        sums.vector(dve, i, b, turn, first, msg[b])

                    def body(i, b, turn, first):
                        dve.wait_ge(att_in[b], 16 * turn + 16)
                        dve.wait_ge(ex_in[b], 16 * turn + 16)
                        kp = keep["d"][:, bass.ds(i * CW, CW)]
                        for f in range(fills):
                            last = dve.tensor_tensor_scan(own[b][:, f, :], kp, ex[b][:, :, f], own[1 - b][:, f, CW - 1:CW],
                                                          ALU.mult, ALU.add)
                        last.then_inc(spread_, 1)
                        dve.wait_ge(spread_, i + 1)
                        if not first:
                            dve.wait_ge(turned, U * (i - 1))
                        mine = own[b][:, 0:D, :].rearrange("p f t -> p t f")
                        left, right = outer_of(att[b][:, :, :], mine)
                        la, ra = left.shape[2], right.shape[2]
                        dve.tensor_tensor(outer[b][:, :, :].rearrange("p t (l r) -> p t l r", r=ra),
                                          left.unsqueeze(3).to_broadcast([P, CW, la, ra]),
                                          right.unsqueeze(2).to_broadcast([P, CW, la, ra]), ALU.mult).then_inc(outered, 1)
                    run_turns_late(dve, NCH, body, post)
                    sums.finish(dve)

                @block.tensor
                def _(pe):
                    def turn_group(i, b, g, first):
                        for n in range(lots):
                            u = g * lots + n
                            if not (first and b == 0 and u < 2):
                                pe.wait_ge(copied, i * U + u - 1)
                            for k, t in enumerate(groups[g]):
                                last = pe.transpose(flip_ps[(b * U + u) % 2][:, k * P:(k + 1) * P],
                                                    outer[b][:, t, n * P:(n + 1) * P], ident[:, :])
                            last.then_inc(turned, 1)

                    def body(i, b, turn, first):
                        pe.wait_ge(outered, i + 1)
                        if not first:
                            pe.wait_ge(done, i - 1)
                        turn_group(i, b, 0, first)
                        for g, ts in enumerate(groups):
                            if g + 1 < G:
                                turn_group(i, b, g + 1, first)
                            pe.wait_ge(copied, i * U + (g + 1) * lots)
                            q = (b * G + g) % 2
                            for k, t in enumerate(ts):
                                for n in range(lots):
                                    last = pe.matmul(msg_ps[b][:, t * D:(t + 1) * D], flip[q][n][:, k * P:(k + 1) * P],
                                                     weights[n], start=(n == 0), stop=(n == lots - 1),
                                                     skip_group_check=True)
                            last.then_inc(multiplied, 1)
                            if not first and g0 <= g < g0 + sums.cd:
                                sums.tensor(pe, i - 2, b, g - g0)
                    g0 = 0 if lots > 1 else G - sums.cd
                    assert 0 <= g0 and sums.cd <= G
                    sums.tensor_start(pe)
                    run_turns(pe, NCH, body)
                    for i in (NCH - 2, NCH - 1):
                        for t in range(sums.cd):
                            sums.tensor(pe, i, i % 2, t)

                @block.scalar
                def _(act):
                    def body(i, b, turn, first):
                        for g, ts in enumerate(groups):
                            q = (b * G + g) % 2
                            for n in range(lots):
                                u = g * lots + n
                                act.wait_ge(turned, i * U + u + 1)
                                if n == 0 and not (first and b == 0 and g < 2):
                                    act.wait_ge(multiplied, i * G + g - 1)
                                act.copy(flip[q][n][:, 0:len(ts) * P], flip_ps[(b * U + u) % 2][:, 0:len(ts) * P]
                                         ).then_inc(copied, 1)
                        if exponential:
                            act.wait_ge(asked, i + 1)
                            act.activation(work[:, :, :], work[:, :, :], ACT.Exp).then_inc(said, 1)
                    run_turns(act, NCH, body)

        def sum_by_source(name, table, last_rows, beside=None):
            msg_v, out_v = edges(table), edges(src_sums)
            with ExitStack() as ctx:
                m = [sb(f"{name}_m{b}", [P, CT, D], F32, ctx) for b in range(2)]
                acc = [sb(f"{name}_acc{b}", [P, CT, D], F32, ctx) for b in range(2)]
                loaded, stored = ([sem(f"{name}_{n}{b}") for b in range(2)] for n in ("loaded", "stored"))
                summed, cleared = sem(f"{name}_summed"), sem(f"{name}_cleared")
                block = ctx.enter_context(nc.Block())

                @block.sync
                def _(sp):
                    def body(i, b, turn, first):
                        if not first:
                            sp.wait_ge(summed, i - 1)
                        sp.dma_start(m[b][:, :, :], msg_v[:, bass.ds(i * CT, CT), :]).then_inc(loaded[b], 16)
                    run_turns(sp, NCT, body)

                @block.vector
                def _(dve):
                    dve.memset(acc[1][:, CT - 1, :], 0.0).then_inc(cleared, 1)
                    dve.wait_ge(cleared, 1)

                    def body(i, b, turn, first):
                        dve.wait_ge(loaded[b], 16 * turn + 16)
                        if not first:
                            dve.wait_ge(stored[b], 16 * turn)
                        for f in range(D):
                            last = dve.tensor_tensor_scan(acc[b][:, :, f], keep["s"][:, bass.ds(i * CT, CT)], m[b][:, :, f],
                                                          acc[1 - b][:, CT - 1, f:f + 1], ALU.mult, ALU.add)
                        last.then_inc(summed, 1)
                        dve.wait_ge(summed, i + 1)
                    run_turns(dve, NCT, body)
                    dve.tensor_copy(last_rows[:, :], acc[(NCT - 1) % 2][:, CT - 1, :])

                @block.scalar
                def _(act):
                    def body(i, b, turn, first):
                        act.wait_ge(summed, i + 1)
                        act.dma_start(out_v[:, bass.ds(i * CT, CT), :], acc[b][:, :, :]).then_inc(stored[b], 16)
                    run_turns(act, NCT, body)
                    act.wait_ge(stored[0], 16 * ((NCT + 1) // 2))
                    act.wait_ge(stored[1], 16 * (NCT // 2))

                if beside:
                    @block.gpsimd
                    def _(pool):
                        beside(pool)

        def sheaf(w1_pair, b1_pair, w2_pair, b2_pair, last_rows, cp):
            name = "sheaf"
            groups = [list(range(t, min(t + 4, CW))) for t in range(0, CW, 4)]
            G = len(groups)
            tw = 20
            ex_v, out_v = edges(ex32), edges(dst_sums)
            with ExitStack() as ctx:
                two = lambda n, shape, dt=F32: [sb(f"{name}_{n}{b}", shape, dt, ctx) for b in range(2)]
                idx, pos = two("idx", [P, CW], I32), two("pos", [P, cp], I32)
                got, ex = two("got", [P, CW, tw]), two("ex", [P, CW, EXW])
                cat = two("cat", [P, CW, 2, D])
                own = two("own", [P, CW])
                his = two("his", [P, CW])
                cat_t, hid = two("cat_t", [2 * D, 4 * P]), two("hid", [P, 4 * P])
                msg, dmsg, dacc = two("msg", [P, CW, D]), sb(f"{name}_dmsg", [P, CW, D], F32, ctx), two("dacc", [P, CW, D])
                v, y, t1 = (sb(f"{name}_{n}", [P, CW, 2, D], F32, ctx) for n in ("v", "y", "t1"))
                q2, dot = (sb(f"{name}_{n}", [P, CW, 2], F32, ctx) for n in ("q2", "dot"))
                first_row = sb(f"{name}_first", [P, EXW], F32, ctx)
                ps = lambda n, w: ctx.enter_context(nc.psum_tensor(f"{name}_{n}", [P, w], F32))
                sums = DirectSums(name, cp, ctx)
                cat_ps, hid_ps, v_ps = ps("cps", 512), ps("hps", 512), ps("vps", 1024)
                idx_in, pos_in, ex_in, gathered, scattered, stored = ([sem(f"{name}_{n}{b}") for b in range(2)] for n in
                    ("idx_in", "pos_in", "ex_in", "gathered", "scattered", "stored"))
                (spread_, paired, turned, copied, hidden, rectified, reflected, sent, summed, admitted, let_in, first_got,
                 steps, start_steps, taken) = (
                    sem(f"{name}_{n}") for n in
                    ("spread", "paired", "turned", "copied", "hidden", "rectified", "reflected", "sent", "summed",
                     "admitted", "let_in", "first_got", "steps", "start_steps", "taken"))
                block = ctx.enter_context(nc.Block())

                @block.sync
                def _(sp):
                    def rows(i, b, turn, first):
                        if not first:
                            sp.wait_ge(paired, i - 1)
                            sp.sem_inc(let_in, 1)
                        sp.dma_start(idx[b][:, :], src_v[:, bass.ds(i * CW, CW)]).then_inc(idx_in[b], 16)
                        sp.dma_start(ex[b][:, :, :], ex_v[:, bass.ds(i * CW, CW), :]).then_inc(ex_in[b], 16)

                    def places(i, b, turn, first):
                        if not first:
                            sp.wait_ge(scattered[b], 16 * cp * turn)
                            sp.sem_inc(let_in, 1)
                        sp.dma_start(pos[b][:, :], pos_rows[:, bass.ds(i * CP, cp)]).then_inc(pos_in[b], 16)
                        sums.load(sp, i, b, first)
                    run_turns_late(sp, NCH, rows, places)

                @block.gpsimd
                def _(pool):
                    pool.indirect_dma_start(first_row[:, :], None, ex32,
                                            bass.IndirectOffsetOnAxis(order["d"]["begins"][:, 0:1], 0)).then_inc(first_got, 16)

                    def gather(i, b, turn, first):
                        pool.wait_ge(idx_in[b], 16 * turn + 16)
                        if not first:
                            pool.wait_ge(paired, i - 1)
                        pool.sem_inc(admitted, 1)
                        for j in range(CW):
                            pool.indirect_dma_start(got[b][:, j, :], None, table3,
                                                    bass.IndirectOffsetOnAxis(idx[b][:, j:j + 1], 0)).then_inc(gathered[b], 16)

                    def scatter(i, b, turn, first):
                        pool.wait_ge(pos_in[b], 16 * turn + 16)
                        pool.wait_ge(sent, i + 1)
                        pool.sem_inc(admitted, 1)
                        for j in range(cp):
                            pool.indirect_dma_start(msgs_2, bass.IndirectOffsetOnAxis(pos[b][:, j:j + 1], 0),
                                                    msg[b][:, j, :], None).then_inc(scattered[b], 16)
                    run_turns_ahead(pool, NCH, gather, scatter)
                    pool.wait_ge(scattered[0], 16 * cp * ((NCH + 1) // 2))
                    pool.wait_ge(scattered[1], 16 * cp * (NCH // 2))

                @block.vector
                def _(dve):
                    start, ch = Chain(dve, start_steps), Chain(dve, steps)
                    dve.wait_ge(first_got, 16)
                    start.add(dve.tensor_copy(cat[1][:, CW - 1, 1, :], first_row[:, 0:D]))
                    start.add(dve.memset(dacc[1][:, CW - 1, :], 0.0))
                    start.link(dve.tensor_copy(own[1][:, CW - 1:CW], first_row[:, D:D + 1]))
                    sums.vector_start(dve)

                    def pre(i, b, turn, first):
                        kp = keep["d"][:, bass.ds(i * CW, CW)]
                        dve.wait_ge(ex_in[b], 16 * turn + 16)
                        if not first:
                            dve.wait_ge(turned, G * (i - 1))
                        for f in range(D):
                            dve.tensor_tensor_scan(cat[b][:, :, 1, f], kp, ex[b][:, :, f], cat[1 - b][:, CW - 1, 1, f:f + 1],
                                                   ALU.mult, ALU.add)
                        dve.tensor_tensor_scan(own[b][:, :], kp, ex[b][:, :, D], own[1 - b][:, CW - 1:CW],
                                               ALU.mult, ALU.add).then_inc(spread_, 1)
                        dve.wait_ge(gathered[b], 16 * CW * (turn + 1))
                        dve.tensor_copy(his[b][:, :], got[b][:, :, D])
                        dve.tensor_copy(cat[b][:, :, 0, :], got[b][:, :, 0:D]).then_inc(paired, 1)
                        dve.wait_ge(spread_, i + 1)
                        dve.wait_ge(paired, i + 1)

                    def apply(i, source, target, swapped):
                        ch.link(dve.tensor_tensor(t1[:, :, :, :], v[:, :, :, :], source[:, :, :, :], ALU.mult))
                        ch.link(dve.tensor_reduce(dot[:, :, :], t1[:, :, :, :], AX_X, ALU.add))
                        ch.link(dve.tensor_tensor(dot[:, :, :], dot[:, :, :], q2[:, :, :], ALU.mult))
                        ch.link(dve.tensor_tensor(t1[:, :, :, :], v[:, :, :, :], dot[:, :, :].unsqueeze(3).to_broadcast([P, CW, 2, D]),
                                                  ALU.mult))
                        if swapped:
                            for h in range(2):
                                ch.add(dve.tensor_tensor(target[:, :, 1 - h, :], source[:, :, h, :], t1[:, :, h, :], ALU.add))
                            ch.sync()

                    def post(i, b, turn, first):
                        ch.begin(i)
                        dve.wait_ge(reflected, G * (i + 1))
                        vp = v_ps[:, 0:CW * 2 * D].rearrange("p (t s f) -> p t (s f)", s=2, f=D)
                        dve.tensor_tensor(v[:, :, :, :].rearrange("p t s f -> p t (s f)"), vp,
                                          b2_pair.unsqueeze(1).to_broadcast([P, CW, 2 * D]), ALU.add).then_inc(taken, 1)
                        dve.wait_ge(taken, i + 1)
                        ch.link(dve.tensor_tensor(t1[:, :, :, :], v[:, :, :, :], v[:, :, :, :], ALU.mult))
                        ch.link(dve.tensor_reduce(q2[:, :, :], t1[:, :, :, :], AX_X, ALU.add))
                        ch.link(dve.tensor_scalar(q2[:, :, :], q2[:, :, :], 1.0e-24, None, ALU.max))
                        ch.link(dve.reciprocal(q2[:, :, :], q2[:, :, :]))
                        ch.link(dve.tensor_scalar(q2[:, :, :], q2[:, :, :], -2.0, None, ALU.mult))
                        apply(i, cat[b], y, True)
                        apply(i, y, None, False)
                        ch.link(dve.tensor_tensor(y[:, :, :, :], y[:, :, :, :], t1[:, :, :, :], ALU.add))
                        ch.link(dve.tensor_tensor(dmsg[:, :, :], y[:, :, 1, :],
                                                  his[b][:, :].unsqueeze(2).to_broadcast([P, CW, D]), ALU.mult))
                        if not first:
                            dve.wait_ge(scattered[b], 16 * cp * turn)
                            dve.wait_ge(stored[b], 16 * turn)
                        dve.tensor_tensor(msg[b][:, :, :], y[:, :, 0, :], own[b][:, :].unsqueeze(2).to_broadcast([P, CW, D]),
                                          ALU.mult).then_inc(sent, 1)
                        for f in range(D):
                            last = dve.tensor_tensor_scan(dacc[b][:, :, f], keep["d"][:, bass.ds(i * CW, CW)], dmsg[:, :, f],
                                                          dacc[1 - b][:, CW - 1, f:f + 1], ALU.mult, ALU.add)
                        last.then_inc(summed, 1)
                        dve.wait_ge(summed, i + 1)
                        dve.wait_ge(sent, i + 1)
                        sums.vector(dve, i, b, turn, first, msg[b])

                    run_turns_late(dve, NCH, pre, post)
                    dve.tensor_copy(last_rows[:, :], dacc[(NCH - 1) % 2][:, CW - 1, :])
                    sums.finish(dve)

                @block.tensor
                def _(pe):
                    def turn_group(i, b, g, first):
                        if not (first and b == 0 and g < 1):
                            pe.wait_ge(copied, i * G + g)
                        for k, t in enumerate(groups[g]):
                            last = pe.transpose(cat_ps[0:2 * D, k * P:(k + 1) * P],
                                                cat[b][:, t, :, :].rearrange("p s f -> p (s f)"), ident[:, :])
                        last.then_inc(turned, 1)

                    def body(i, b, turn, first):
                        pe.wait_ge(paired, i + 1)
                        pe.wait_ge(spread_, i + 1)
                        turn_group(i, b, 0, first)
                        for g, ts in enumerate(groups):
                            q, n = (b * G + g) % 2, len(ts) * P
                            pe.wait_ge(copied, i * G + g + 1)
                            if not (first and b == 0 and g < 1):
                                pe.wait_ge(rectified, i * G + g)
                            pe.matmul(hid_ps[:, 0:n], w1_pair, cat_t[q][:, 0:n], start=True, stop=True).then_inc(hidden, 1)
                            if g + 1 < G:
                                turn_group(i, b, g + 1, first)
                            if not first:
                                for t in range(g * sums.cd // G, (g + 1) * sums.cd // G):
                                    sums.tensor(pe, i - 2, b, t)
                            pe.wait_ge(rectified, i * G + g + 1)
                            if g == 0 and not (first and b == 0):
                                pe.wait_ge(taken, i)
                            for k, t in enumerate(ts):
                                last = pe.matmul(v_ps[:, t * 2 * D:(t + 1) * 2 * D], hid[q][:, k * P:(k + 1) * P], w2_pair,
                                                 start=True, stop=True, skip_group_check=True)
                            last.then_inc(reflected, 1)
                    sums.tensor_start(pe)
                    run_turns(pe, NCH, body)
                    for i in (NCH - 2, NCH - 1):
                        for t in range(sums.cd):
                            sums.tensor(pe, i, i % 2, t)

                @block.scalar
                def _(act):
                    def copy(i, b, g, first):
                        q, n = (b * G + g) % 2, len(groups[g]) * P
                        act.wait_ge(turned, i * G + g + 1)
                        if not (first and b == 0 and g < 2):
                            act.wait_ge(hidden, i * G + g - 1)
                        act.copy(cat_t[q][:, 0:n], cat_ps[0:2 * D, 0:n]).then_inc(copied, 1)

                    def body(i, b, turn, first):
                        copy(i, b, 0, first)
                        for g, ts in enumerate(groups):
                            if g + 1 < G:
                                copy(i, b, g + 1, first)
                            q, n = (b * G + g) % 2, len(ts) * P
                            act.wait_ge(hidden, i * G + g + 1)
                            if not (first and b == 0 and g < 2):
                                act.wait_ge(reflected, i * G + g - 1)
                            act.activation(hid[q][:, 0:n], hid_ps[:, 0:n], ACT.Relu, bias=b1_pair).then_inc(rectified, 1)

                    def store(i, b, turn, first):
                        act.wait_ge(summed, i + 1)
                        act.dma_start(out_v[:, bass.ds(i * CW, CW), :], dacc[b][:, :, :]).then_inc(stored[b], 16)
                    run_turns_late(act, NCH, body, store)
                    act.wait_ge(stored[0], 16 * ((NCH + 1) // 2))
                    act.wait_ge(stored[1], 16 * (NCH // 2))

        def selu_of(bias, minus_bias, scaled_bias):
            def function(act, ch, parts, z):
                ch.add(act.activation(parts[0][:, :], z, ACT.Relu, bias=scaled_bias, scale=SELU_SCALE))
                ch.link(act.activation(parts[1][:, :], z, ACT.Relu, bias=minus_bias, scale=-1.0))
                ch.link(act.activation(parts[1][:, :], parts[1][:, :], ACT.Exp, scale=-1.0))
                return act.activation(parts[1][:, :], parts[1][:, :], ACT.Copy, scale=SELU_SCALE * SELU_ALPHA,
                                      bias=-SELU_SCALE * SELU_ALPHA)
            return function

        def layer_norm(name, y, result):
            with ExitStack() as ctx:
                sq = sb(f"{name}_sq", [NP, NK, D], F32, ctx)
                mean, var = sb(f"{name}_mean", [NP, NK], F32, ctx), sb(f"{name}_var", [NP, NK], F32, ctx)
                steps, asked, said = sem(f"{name}_steps"), sem(f"{name}_asked"), sem(f"{name}_said")
                block = ctx.enter_context(nc.Block())
                wide = lambda t: t[:, :].unsqueeze(2).to_broadcast([NP, NK, D])

                @block.vector
                def _(dve):
                    ch = Chain(dve, steps)
                    ch.link(dve.tensor_reduce(mean[:, :], y[:, :, :], AX_X, ALU.add))
                    ch.link(dve.tensor_scalar(mean[:, :], mean[:, :], 1.0 / D, None, ALU.mult))
                    ch.link(dve.tensor_tensor(y[:, :, :], y[:, :, :], wide(mean), ALU.subtract))
                    ch.link(dve.tensor_tensor(sq[:, :, :], y[:, :, :], y[:, :, :], ALU.mult))
                    ch.link(dve.tensor_reduce(var[:, :], sq[:, :, :], AX_X, ALU.add))
                    dve.tensor_scalar(var[:, :], var[:, :], 1.0 / D, 1e-5, ALU.mult, ALU.add).then_inc(asked, 1)
                    dve.wait_ge(said, 1)
                    ch.link(dve.reciprocal(var[:, :], var[:, :]))
                    dve.tensor_tensor(result[:, :, :], y[:, :, :], wide(var), ALU.mult)

                @block.scalar
                def _(act):
                    act.wait_ge(asked, 1)
                    act.activation(var[:, :], var[:, :], ACT.Sqrt).then_inc(said, 1)

        def finish_attention(name, heads, feats, rows, a_src, a_dst, values, result):
            w = heads * feats
            with ExitStack() as ctx:
                e, top, seg_top = (sb(f"{name}_{n}", [NP, NK, heads], F32, ctx) for n in ("e", "top", "seg_top"))
                z = sb(f"{name}_z", [NP, NK, heads], F32, ctx)
                ee = sb(f"{name}_ee", [NP, 2, NK, heads], F32, ctx)
                steps, asked, said = sem(f"{name}_steps"), sem(f"{name}_asked"), sem(f"{name}_said")
                block = ctx.enter_context(nc.Block())
                has = order["d"]["has"]

                @block.vector
                def _(dve):
                    ch = Chain(dve, steps)
                    has_w = has[:, :].unsqueeze(2).to_broadcast([NP, NK, heads])
                    ch.add(dve.tensor_tensor(e[:, :, :], a_src, a_dst, ALU.add))
                    ch.add(dve.tensor_scalar(z[:, :, :], has_w, BIG, -BIG, ALU.mult, ALU.add))
                    ch.link(dve.tensor_tensor(seg_top[:, :, :], rows[:, :, w + heads:w + 2 * heads], has_w, ALU.mult))
                    ch.add(dve.scalar_tensor_tensor(out=e[:, :, :], in0=e[:, :, :], scalar=SLOPE, in1=e[:, :, :],
                                                    op0=ALU.mult, op1=ALU.max))
                    ch.link(dve.tensor_tensor(seg_top[:, :, :], seg_top[:, :, :], z[:, :, :], ALU.add))
                    ch.link(dve.tensor_tensor(top[:, :, :], seg_top[:, :, :], e[:, :, :], ALU.max))
                    ch.add(dve.tensor_tensor(ee[:, 0, :, :], seg_top[:, :, :], top[:, :, :], ALU.subtract))
                    dve.tensor_tensor(ee[:, 1, :, :], e[:, :, :], top[:, :, :], ALU.subtract).then_inc(asked, 1)
                    dve.wait_ge(said, 1)
                    ch.link(dve.tensor_tensor(z[:, :, :], rows[:, :, w:w + heads], ee[:, 0, :, :], ALU.mult))
                    ch.link(dve.tensor_tensor(z[:, :, :], z[:, :, :], ee[:, 1, :, :], ALU.add))
                    ch.link(dve.tensor_scalar(z[:, :, :], z[:, :, :], 1e-16, None, ALU.add))
                    ch.link(dve.reciprocal(z[:, :, :], z[:, :, :]))
                    for n in range(2):
                        ch.add(dve.tensor_tensor(ee[:, n, :, :], ee[:, n, :, :], z[:, :, :], ALU.mult))
                    ch.sync()
                    for h in range(heads):
                        part = result[:, :, h * feats:(h + 1) * feats]
                        ch.link(dve.tensor_tensor(part, values, ee[:, 1, :, h:h + 1].to_broadcast([NP, NK, feats]), ALU.mult))
                        ch.link(dve.tensor_tensor(rows[:, :, h * feats:(h + 1) * feats], rows[:, :, h * feats:(h + 1) * feats],
                                                  ee[:, 0, :, h:h + 1].to_broadcast([NP, NK, feats]), ALU.mult))
                        ch.link(dve.tensor_tensor(part, part, rows[:, :, h * feats:(h + 1) * feats], ALU.add))

                @block.scalar
                def _(act):
                    act.wait_ge(asked, 1)
                    act.activation(ee[:, :, :, :], ee[:, :, :, :], ACT.Exp).then_inc(said, 1)

        def silu_block(name, z, scale, work):
            steps, asked, said = sem(f"{name}_steps"), sem(f"{name}_asked"), sem(f"{name}_said")
            with nc.Block() as block:
                @block.scalar
                def _(act):
                    act.wait_ge(asked, 1)
                    act.activation(work, work, ACT.Exp).then_inc(said, 1)

                @block.vector
                def _(dve):
                    ch = Chain(dve, steps)
                    dve.tensor_scalar(work, z, -scale, TOP_EXP, ALU.mult, ALU.min).then_inc(asked, 1)
                    dve.wait_ge(said, 1)
                    ch.link(dve.tensor_scalar(work, work, 1.0, None, ALU.add))
                    ch.link(dve.reciprocal(work, work))
                    dve.scalar_tensor_tensor(out=z, in0=z, scalar=scale, in1=work, op0=ALU.mult, op1=ALU.mult)

        with ExitStack() as ctx:
            zeros = sb("zeros", [P, CW * EXW * 5], F32, ctx)
            setup(zeros)
            count_destinations(zeros)
        with ExitStack() as ctx:
            fresh = sb("fresh", [P, C], F32, ctx)
            find_segments("d")
            last1 = sb("last1", [P, W1R], F32, ctx)
            att1 = sb("att1", [NP, NK, 2 * H1], F32, ctx)
            w1_blocks = sb("w1_blocks", [H1 * D, HC1], F32, ctx)
            b1c = sb("b1c", [HC1, 3], F32, ctx)
            w2_ext = sb("w2_ext", [HC1, C2 + 2], F32, ctx)
            t2 = sb("t2", [NP, NK, 36], F32, ctx)
            with ExitStack() as c2:
                w1_sb, a1 = sb("w1_sb", [D, HC1], F32, c2), sb("a1", [D, 2, HC1], F32, c2)
                a2 = sb("a2", [HC1, 2, C2], F32, c2)
                att_w, prod1, prod2 = sb("att_w", [D, 2, H1], F32, c2), sb("prod1", [D, 2, HC1], F32, c2), sb(
                    "prod2", [HC1, 2, C2], F32, c2)
                on_vector("clear_w1", lambda dve, ch: ch.add(dve.memset(w1_blocks[:, :], 0.0)))
                load_all("weights1", [(w1_sb[:, :], L0_gnn_W1), (w2_ext[:, 0:C2], L0_gnn_W2),
                                      (a1[:, 0, :], spread(L0_gnn_a_src1.rearrange("h c -> (h c)"), D, HC1)),
                                      (a1[:, 1, :], spread(L0_gnn_a_dst1.rearrange("h c -> (h c)"), D, HC1)),
                                      (a2[:, 0, :], spread(L0_gnn_a_src2.rearrange("h c -> (h c)"), HC1, C2)),
                                      (a2[:, 1, :], spread(L0_gnn_a_dst2.rearrange("h c -> (h c)"), HC1, C2)),
                                      (b1c[:, 0:1], L0_gnn_b1.unsqueeze(1))]
                         + [(w1_blocks[h * D:(h + 1) * D, h * C1:(h + 1) * C1], L0_gnn_W1[:, h * C1:(h + 1) * C1])
                            for h in range(H1)], c2)

                def weights(dve, ch):
                    ch.add(dve.tensor_tensor(prod1[:, :, :], a1[:, :, :], w1_sb[:, :].unsqueeze(1).to_broadcast([D, 2, HC1]),
                                             ALU.mult))
                    ch.add(dve.tensor_tensor(prod2[:, :, :], a2[:, :, :],
                                             w2_ext[:, 0:C2].unsqueeze(1).to_broadcast([HC1, 2, C2]), ALU.mult))
                    ch.add(dve.tensor_scalar(b1c[:, 1:2], b1c[:, 0:1], -1.0, None, ALU.mult))
                    ch.link(dve.tensor_scalar(b1c[:, 2:3], b1c[:, 0:1], SELU_SCALE, None, ALU.mult))
                    ch.add(dve.tensor_reduce(att_w[:, :, :], prod1[:, :, :].rearrange("p s (h c) -> p s h c", h=H1), AX_X, ALU.add))
                    ch.link(dve.tensor_reduce(w2_ext[:, C2:C2 + 2], prod2[:, :, :], AX_X, ALU.add))
                on_vector("weights1_made", weights)
                t1r, e1r = sb("t1r", [NP, NK, 20], F32, c2), sb("e1r", [NP, NK, 4], F32, c2)

                def rows1(dve, ch):
                    ch.link(dve.memset(t1r[:, :, D + H1:20], 0.0))
                    ch.link(dve.memset(e1r[:, :, H1:4], 0.0))
                    ch.link(dve.tensor_copy(t1r[:, :, 0:D], x_cur[:, :, :]))
                on_vector("rows1", rows1)

                def use1(dve, ch, i, prod):
                    group = bass.ds(i * GK, GK)
                    ch.add(dve.tensor_scalar(att1[:, group, :], prod, 1.0, None, ALU.mult))
                    ch.add(dve.tensor_scalar(t1r[:, group, D:D + H1], prod[:, :, 0:H1], 1.0, None, ALU.mult))
                    return dve.tensor_scalar(e1r[:, group, 0:H1], prod[:, :, H1:2 * H1], 1.0, None, ALU.mult)
                node_product("att1", [D], whole_groups(x_cur), [att_w[:, :, :].rearrange("p s h -> p (s h)")], 2 * H1, use1,
                             put=(e1r, ex4), store=(t1r, table1))
            renew_semaphores()
            attention("gat1", H1, D, table1, 20, gat1_sums, last1, CountSources())
            renew_semaphores()
            find_segments("s")
            join_softmax("join1", H1, D, gat1_sums, last1)
            with ExitStack() as c2:
                seg1, o1 = sb("seg1", [NP, NK, W1R], F32, c2), sb("o1", [NP, NK, H1 * D], F32, c2)
                take_rows("take1", "d", gat1_sums, seg1)
                finish_attention("fin1", H1, D, seg1, att1[:, :, 0:H1], att1[:, :, H1:2 * H1], x_cur[:, :, :], o1)
                e2r = sb("e2r", [NP, NK, 4], F32, c2)

                def rows2(dve, ch):
                    ch.link(dve.memset(t2[:, :, C2 + 2:36], 0.0))
                    ch.link(dve.memset(e2r[:, :, :], 0.0))
                on_vector("rows2", rows2)

                def use2(dve, ch, i, prod):
                    group = bass.ds(i * GK, GK)
                    ch.add(dve.tensor_scalar(t2[:, group, 0:C2 + 2], prod, 1.0, None, ALU.mult))
                    return dve.tensor_scalar(e2r[:, group, 0:1], prod[:, :, C2 + 1:C2 + 2], 1.0, None, ALU.mult)
                node_product("hidden1", [H1 * D], whole_groups(o1), [w2_ext[:, :]] * 2, C2 + 2, use2,
                             middle=(w1_blocks[:, :], HC1, selu_of(b1c[:, 0:1], b1c[:, 1:2], b1c[:, 2:3])),
                             put=(e2r, ex4), store=(t2, table2))

            last2 = sb("last2", [P, W2R], F32, ctx)
            wf, b2c = sb("wf", [C2, D], F32, ctx), sb("b2c", [C2, 3], F32, ctx)
            bf_w = sb("bf_w", [NP, D], F32, ctx)
            load_all("weights2", [(wf[:, :], L0_gnn_Wf), (b2c[:, 0:1], L0_gnn_b2.unsqueeze(1)),
                                  (bf_w[:, :], spread(L0_gnn_bf, NP, D))], ctx)

            def biases2(dve, ch):
                ch.add(dve.tensor_scalar(b2c[:, 1:2], b2c[:, 0:1], -1.0, None, ALU.mult))
                ch.add(dve.tensor_scalar(b2c[:, 2:3], b2c[:, 0:1], SELU_SCALE, None, ALU.mult))
            on_vector("biases2", biases2)
            renew_semaphores()
            attention("gat2", H2, C2, table2, 36, gat2_sums, last2, PlaceBySource())
            renew_semaphores()
            join_softmax("join2", H2, C2, gat2_sums, last2)
            with ExitStack() as c2:
                seg2, o2 = sb("seg2", [NP, NK, W2R], F32, c2), sb("o2", [NP, NK, C2], F32, c2)
                y0 = sb("y0", [NP, NK, D], F32, c2)
                take_rows("take2", "d", gat2_sums, seg2)
                finish_attention("fin2", H2, C2, seg2, t2[:, :, C2:C2 + 1], t2[:, :, C2 + 1:C2 + 2], t2[:, :, 0:C2], o2)
                node_product("hidden2", [C2], whole_groups(o2), [wf[:, :]] * 2, D, into(y0),
                             middle=(ident[0:C2, 0:C2], C2, selu_of(b2c[:, 0:1], b2c[:, 1:2], b2c[:, 2:3])))

                def residual0(dve, ch):
                    ch.link(dve.tensor_tensor(y0[:, :, :], y0[:, :, :], bf_w[:, :].unsqueeze(1).to_broadcast([NP, NK, D]), ALU.add))
                    ch.link(dve.tensor_tensor(y0[:, :, :], y0[:, :, :], x_cur[:, :, :], ALU.add))
                on_vector("residual0", residual0)
                layer_norm("norm0", y0, x_cur)

        renew_semaphores()
        norm_msg, norm_upd, norm_lin = (D * DE) ** -0.5, (D * D) ** -0.5, D ** -0.5
        last_s = sb("last_s", [P, D])
        last_d = sb("last_d", [P, D])
        with ExitStack() as ctx:
            w_msg = sb("w_msg", [D * DE, D], F32, ctx)
            lin, lin2 = sb("lin", [D, D], F32, ctx), sb("lin2", [D, D], F32, ctx)
            w_upd = [sb(f"w_upd{n}", [P, D], F32, ctx) for n in range(2)]
            upd_v = L1_gnn_W_upd_tp.rearrange("i h k -> (i h) k")
            load_all("weights3", [(w_msg[:, :], L1_gnn_W_msg_tp.rearrange("i j h -> (i j) h")), (lin[:, :], L1_gnn_W_msg_lin),
                                  (lin2[:, :], L1_gnn_W_upd_lin)]
                     + [(w_upd[n][:, :], upd_v[n * P:(n + 1) * P, :]) for n in range(2)], ctx)

            with ExitStack() as c2:
                e32 = sb("e32_3", [NP, NK, EXW], F32, c2)

                def rows3(dve, ch):
                    ch.link(dve.memset(e32[:, :, :], 0.0))
                    ch.link(dve.tensor_copy(e32[:, :, 0:D], x_cur[:, :, :]))
                on_vector("rows3", rows3)
                put_rows("put3", None, None, e32, ex32, EXW)

            def outer_nodes_edges(att, mine):
                return mine, att

            def finish1(dve, ch, i, msg, prod, work, own, asked, said):
                dve.tensor_scalar(work[:, :, :], prod, -norm_msg, TOP_EXP, ALU.mult, ALU.min).then_inc(asked, 1)
                dve.wait_ge(said, i + 1)
                ch.link(dve.tensor_scalar(work[:, :, :], work[:, :, :], 1.0, None, ALU.add))
                ch.link(dve.reciprocal(work[:, :, :], work[:, :, :]))
                return dve.scalar_tensor_tensor(out=msg[:, :, :].rearrange("p t f -> p (t f)"),
                                                in0=prod.rearrange("p t f -> p (t f)"), scalar=norm_msg,
                                                in1=work[:, :, :].rearrange("p t f -> p (t f)"), op0=ALU.mult, op1=ALU.mult)
            messages("msg1", edge_attr_8, D, outer_nodes_edges, [w_msg[:, :]], finish1, CP_1, exponential=True)
            renew_semaphores()
            settle_direct("settle1")
            sum_by_source("tail1", msgs, last_s)
            join_sums("join3", "s", src_sums, D, last_s)
            with ExitStack() as c2:
                seg3 = sb("seg3", [NP, NK, D], F32, c2)
                agg, up = sb("agg", [NP, NK, D], F32, c2), sb("up", [NP, NK, D], F32, c2)
                work3 = sb("work3", [NP, NK, D], F32, c2)

                def fill_sums(dve, ch, i, stage):
                    group = bass.ds(i * GK, GK)
                    ch.link(dve.tensor_tensor(stage[:, :, :], seg3[:, group, :],
                                              order["s"]["has"][:, group].unsqueeze(2).to_broadcast([NP, GK, D]), ALU.mult))
                    return dve.tensor_tensor(stage[:, :, :], stage[:, :, :], direct[:, group, :], ALU.add)
                node_product("agg1", [D], fill_sums, [lin[:, :]], D, into(agg, norm_lin), taken=("s", src_sums, seg3))

                def fill_outer(dve, ch, i, stage):
                    for k in range(GK):
                        xs = x_cur[:, bass.ds(i * GK + k, 1), :].rearrange("p k f -> p (k f)")
                        gs = agg[:, bass.ds(i * GK + k, 1), :].rearrange("p k f -> p (k f)")
                        last = dve.tensor_tensor(stage[:, k, :].rearrange("p (a b) -> p a b", b=D),
                                                 xs.unsqueeze(2).to_broadcast([NP, D, D]),
                                                 gs.unsqueeze(1).to_broadcast([NP, D, D]), ALU.mult)
                    return last
                node_product("upd1", [P, P], fill_outer, [w[:, :] for w in w_upd], D, into(up))
                silu_block("silu1", up[:, :, :], norm_upd, work3[:, :, :])
                node_product("lin1", [D], whole_groups(up), [lin2[:, :]], D, into(agg, norm_lin))
                on_vector("residual1", lambda dve, ch: ch.link(dve.scalar_tensor_tensor(
                    out=up[:, :, :], in0=x_cur[:, :, :], scalar=2.0, in1=agg[:, :, :], op0=ALU.mult, op1=ALU.add)))
                layer_norm("norm1", up, x_cur)

        renew_semaphores()
        with ExitStack() as ctx:
            w1_pair, w2_pair = sb("w1_pair", [2 * D, 2 * HID], F32, ctx), sb("w2_pair", [2 * HID, 2 * D], F32, ctx)
            b1_pair, b2_pair = sb("b1_pair", [2 * HID, 1], F32, ctx), sb("b2_pair", [P, 2 * D], F32, ctx)
            dinv = sb("dinv", [NP, NK], F32, ctx)
            on_vector("clear_w2", lambda dve, ch: ch.add(dve.memset(w2_pair[:, :], 0.0)))
            w1t, w2t = L2_gnn_W1.rearrange("h f -> f h"), L2_gnn_W2.rearrange("f h -> h f")
            load_all("weights4", [(w1_pair[:, 0:HID], w1t), (w1_pair[0:D, HID:2 * HID], w1t[D:2 * D, :]),
                                  (w1_pair[D:2 * D, HID:2 * HID], w1t[0:D, :]),
                                  (w2_pair[0:HID, 0:D], w2t), (w2_pair[HID:2 * HID, D:2 * D], w2t),
                                  (b1_pair[0:HID, :], L2_gnn_b1.unsqueeze(1)), (b1_pair[HID:2 * HID, :], L2_gnn_b1.unsqueeze(1)),
                                  (b2_pair[:, 0:D], spread(L2_gnn_b2, P, D)), (b2_pair[:, D:2 * D], spread(L2_gnn_b2, P, D))], ctx)
            root_steps, root_asked, root_said = sem("root_steps"), sem("root_asked"), sem("root_said")
            with ExitStack() as c2:
                t3, e32 = sb("t3", [NP, NK, 20], F32, c2), sb("e32_4", [NP, NK, EXW], F32, c2)
                with nc.Block() as block:
                    @block.vector
                    def _(dve):
                        ch = Chain(dve, root_steps)
                        dve.tensor_scalar(dinv[:, :], deg[:, :], 1e-5, None, ALU.max).then_inc(root_asked, 1)
                        ch.add(dve.memset(e32[:, :, D + 1:EXW], 0.0))
                        ch.link(dve.memset(t3[:, :, D + 1:20], 0.0))
                        dve.wait_ge(root_said, 1)
                        ch.link(dve.reciprocal(dinv[:, :], dinv[:, :]))
                        for t in (t3, e32):
                            ch.add(dve.tensor_copy(t[:, :, 0:D], x_cur[:, :, :]))
                            ch.add(dve.tensor_copy(t[:, :, D], dinv[:, :]))

                    @block.scalar
                    def _(act):
                        act.wait_ge(root_asked, 1)
                        act.activation(dinv[:, :], dinv[:, :], ACT.Sqrt).then_inc(root_said, 1)
                put_rows("put4", table3, t3, e32, ex32, EXW)
            renew_semaphores()
            sheaf(w1_pair[:, :], b1_pair[:, :], w2_pair[:, :], b2_pair[:, :], last_d, CP_2)
            renew_semaphores()
            join_sums("join4", "d", dst_sums, D, last_d)
            settle_direct("settle2")
            with ExitStack() as c2:
                seg_s, seg_d = sb("seg_of_s", [NP, NK, D], F32, c2), sb("seg_of_d", [NP, NK, D], F32, c2)
                took_d = sem("took_d")
                sum_by_source("tail2", msgs_2, last_s, lambda pool: take(pool, took_d, "d", dst_sums, seg_d))
                join_sums("join5", "s", src_sums, D, last_s)
                take_rows("take4", "s", src_sums, seg_s)

                def residual2(dve, ch):
                    both_sums(dve, ch, seg_s)
                    ch.link(dve.tensor_tensor(seg_d[:, :, :], seg_d[:, :, :],
                                              order["d"]["has"][:, :].unsqueeze(2).to_broadcast([NP, NK, D]), ALU.mult))
                    ch.link(dve.tensor_tensor(seg_s[:, :, :], seg_s[:, :, :], seg_d[:, :, :], ALU.add))
                    ch.link(dve.tensor_tensor(seg_s[:, :, :], seg_s[:, :, :], dinv[:, :].unsqueeze(2).to_broadcast([NP, NK, D]),
                                              ALU.mult))
                    ch.link(dve.tensor_tensor(seg_s[:, :, :], seg_s[:, :, :], x_cur[:, :, :], ALU.add))
                    ch.link(dve.tensor_scalar(seg_s[:, :, :], seg_s[:, :, :], 0.0, None, ALU.max))
                    ch.link(dve.tensor_tensor(seg_s[:, :, :], seg_s[:, :, :], x_cur[:, :, :], ALU.add))
                on_vector("residual2", residual2)
                layer_norm("norm2", seg_s, x_cur)

        renew_semaphores()
        with ExitStack() as ctx:
            x_new = sb("x_new", [NP, NK, D], F32, ctx)
            w_edge = [sb(f"w_edge{n}", [P, D], F32, ctx) for n in range(2)]
            bias_m = sb("bias_m", [D, D], F32, ctx)
            kern = L3_gnn_kernel.rearrange("k (i j) -> k j i", i=D)
            half = P // D
            load_all("weights5", [(w_edge[k // half][(k % half) * D:(k % half + 1) * D, :], kern[k]) for k in range(D)]
                     + [(bias_m[:, :], L3_gnn_bias.rearrange("(i j) -> j i", i=D))], ctx)
            with ExitStack() as c2:
                e32 = sb("e32_5", [NP, NK, EXW], F32, c2)

                on_vector("rows5", lambda dve, ch: ch.link(dve.tensor_copy(e32[:, :, 0:D], x_cur[:, :, :])))

                def use5(dve, ch, i, prod):
                    return dve.tensor_scalar(e32[:, bass.ds(i * GK, GK), D:2 * D], prod, 1.0, None, ALU.mult)
                node_product("bias", [D], whole_groups(x_cur), [bias_m[:, :]], D, use5, put=(e32, ex32))

            def outer_edges_nodes(att, mine):
                return att, mine

            def finish3(dve, ch, i, msg, prod, work, own, asked, said):
                return dve.tensor_tensor(msg[:, :, :], prod, own[:, D:2 * D, :].rearrange("p f t -> p t f"), ALU.add)
            messages("msg3", edge_attr_16, 2 * D, outer_edges_nodes, [w[:, :] for w in w_edge], finish3, CP_3)
            renew_semaphores()
            settle_direct("settle3")
            sum_by_source("tail3", msgs, last_s)
            join_sums("join6", "s", src_sums, D, last_s)
            with ExitStack() as c2:
                seg6 = sb("seg6", [NP, NK, D], F32, c2)
                take_rows("take6", "s", src_sums, seg6)

                def residual3(dve, ch):
                    both_sums(dve, ch, seg6)
                    ch.link(dve.tensor_tensor(seg6[:, :, :], seg6[:, :, :], x_cur[:, :, :], ALU.add))
                on_vector("residual3", residual3)
                layer_norm("norm3", seg6, x_new)

            written = sem("written")
            with nc.Block() as block:
                @block.sync
                def _(sp):
                    sp.dma_start(out[0:FULL * P, :].rearrange("(p k) d -> p k d", k=NK), x_new[0:FULL, :, :]).then_inc(written, 16)
                    if REST:
                        sp.dma_start(out[FULL * P:N, :].rearrange("(p k) d -> p k d", k=REST), x_new[FULL:NP, 0:REST, :]
                                     ).then_inc(written, 16)
                    sp.wait_ge(written, 32 if REST else 16)


_INS = ['x', 'src', 'dst', 'edge_attr_16', 'edge_attr_8', 'node_vec1',
        'L0_gnn_W1', 'L0_gnn_a_src1', 'L0_gnn_a_dst1', 'L0_gnn_b1', 'L0_gnn_W2', 'L0_gnn_a_src2',
        'L0_gnn_a_dst2', 'L0_gnn_b2', 'L0_gnn_Wf', 'L0_gnn_bf',
        'L1_gnn_W_msg_tp', 'L1_gnn_W_msg_lin', 'L1_gnn_W_upd_tp', 'L1_gnn_W_upd_lin',
        'L2_gnn_W1', 'L2_gnn_b1', 'L2_gnn_W2', 'L2_gnn_b2', 'L3_gnn_kernel', 'L3_gnn_bias']


def kernel(**inputs):
    import numpy as _np
    import concourse.bacc as _bacc
    from concourse import mybir as _mybir
    from concourse.bass_utils import run_bass_kernel_spmd as _run

    nc = _bacc.Bacc("TRN2", target_bir_lowering=False, num_devices=1)
    arrays, args = {}, []
    for name in _INS:
        a = _np.ascontiguousarray(inputs[name])
        arrays[f"in_{name}_dram"] = a
        args.append(nc.dram_tensor(f"in_{name}_dram", a.shape, _mybir.dt.from_np(a.dtype), kind="ExternalInput").ap())
    shape = inputs["x"].shape
    args.append(nc.dram_tensor("out_0_dram", shape, _mybir.dt.float32, kind="ExternalOutput").ap())
    gnn_kernel(nc, *args)
    r = _run(nc, [arrays], core_ids=[0])
    return r.results[0]["out_0_dram"]
```
